# Optimizing a Trainium2 kernel written in Bass

```python
import numpy as np
import jax
import jax.numpy as jnp

def _softmax(x, axis=-1):
    return jax.nn.softmax(x, axis=axis)

def _gelu(x):
    return jax.nn.gelu(x, approximate=True)

def _silu(x):
    return jax.nn.silu(x)

def _sigmoid(x):
    return jax.nn.sigmoid(x)

def _layernorm(x, axis=-1, eps=1e-05):
    m = jnp.mean(x, axis=axis, keepdims=True)
    v = jnp.var(x, axis=axis, keepdims=True)
    return (x - m) / jnp.sqrt(v + eps)

def _scatter_add(tgt, idx, src, axis=0):
    return tgt.at[idx].add(src)

def _segment_sum(src, seg, n):
    return jax.ops.segment_sum(src, seg, n)
kernel_name = 'mk_cond_resid_d4_seqx_r2_e8302c'

def setup_inputs(seed: int=0):
    np.random.seed(seed)
    _w = jnp.asarray

    def _rec_inputs():
        import jax
        import jax.numpy as jnp
        _rk = jax.random.key(seed)
        x = -0.000125 + 0.9999 * jax.random.normal(jax.random.fold_in(_rk, 1), (64, 128, 512), jnp.float32)
        _lenS = 128 - jax.random.randint(jax.random.fold_in(_rk, 7), (64,), 0, max(1, 128 // 4) + 1, jnp.int32)
        _lenS2 = 128 - jax.random.randint(jax.random.fold_in(_rk, 8), (64,), 0, max(1, 128 // 4) + 1, jnp.int32)
        fside_Bx2_0 = -2.90419 + 8.51931 * jax.random.normal(jax.random.fold_in(_rk, 11), (64, 2), jnp.float32)
        condB_angle = 0.0111926 + 0.196324 * jax.random.normal(jax.random.fold_in(_rk, 12), (64,), jnp.float32)
        itok_B_0_7 = jax.random.randint(jax.random.fold_in(_rk, 13), (64,), 0, 8, jnp.int32)
        itok_B_0_2 = jax.random.randint(jax.random.fold_in(_rk, 14), (64,), 0, 3, jnp.int32)
        itok_B_0_8 = jax.random.randint(jax.random.fold_in(_rk, 15), (64,), 0, 9, jnp.int32)
        return (x, fside_Bx2_0, condB_angle, itok_B_0_7, itok_B_0_2, itok_B_0_8)
    x, fside_Bx2_0, condB_angle, itok_B_0_7, itok_B_0_2, itok_B_0_8 = _rec_inputs()

    def _L0_cond_setup():
        import jax, jax.numpy as jnp
        import numpy as np
        B, H, W = (32, 512, 512)
        SCALE_DX = 1.0
        SCALE_ANGLE = 1.0

        def _rigid_transform(X, dx, angle):
            b, h, w = X.shape
            gx = jnp.arange(w, dtype=jnp.float32)[None, :] - w / 2.0
            gy = jnp.arange(h, dtype=jnp.float32)[:, None] - h / 2.0
            theta = angle * SCALE_ANGLE
            c = jnp.cos(theta)[:, None, None]
            s = jnp.sin(theta)[:, None, None]
            xp = c * gx - s * gy + dx[:, 0, None, None] * SCALE_DX
            yp = s * gx + c * gy + dx[:, 1, None, None] * SCALE_DX
            gx_n = yp / h * 2.0
            gy_n = xp / w * 2.0
            ix = (gx_n + 1.0) * 0.5 * (w - 1)
            iy = (gy_n + 1.0) * 0.5 * (h - 1)
            ix0 = jnp.floor(ix)
            iy0 = jnp.floor(iy)
            wx1 = ix - ix0
            wy1 = iy - iy0
            wx0 = 1.0 - wx1
            wy0 = 1.0 - wy1
            ix0i = ix0.astype(jnp.int32)
            iy0i = iy0.astype(jnp.int32)
            ix1i = ix0i + 1
            iy1i = iy0i + 1
            bidx = jnp.arange(b, dtype=jnp.int32)[:, None, None]

            def gather(yi, xi):
                valid = (xi >= 0) & (xi <= w - 1) & (yi >= 0) & (yi <= h - 1)
                xc = jnp.clip(xi, 0, w - 1)
                yc = jnp.clip(yi, 0, h - 1)
                return X[bidx, yc, xc] * valid.astype(X.dtype)
            out = gather(iy0i, ix0i) * (wy0 * wx0) + gather(iy0i, ix1i) * (wy0 * wx1) + gather(iy1i, ix0i) * (wy1 * wx0) + gather(iy1i, ix1i) * (wy1 * wx1)
            return out
        key = jax.random.key(seed)
        k1, k2, k3 = jax.random.split(key, 3)
        X = jax.random.normal(k1, (B, H, W), dtype=jnp.float32)
        dx = jax.random.normal(k2, (B, 2), dtype=jnp.float32) * 8.0
        angle = jax.random.normal(k3, (B,), dtype=jnp.float32) * 0.2
        return {'X': X, 'dx': dx, 'angle': angle}
    _L0_cond_all = _L0_cond_setup()
    _L0_cond_in = {k: v for k, v in _L0_cond_all.items() if k in ()}
    del _L0_cond_all

    def _L1_cond_setup():
        import jax, jax.numpy as jnp
        import numpy as np
        B, S, D, F = (32, 256, 512, 2048)
        R_COMMON, R_DOMAIN, E = (16, 16, 8)
        ALPHA = 2.0

        def _expert_lora(x, expert_ids, Wa, Wb):
            Ab = Wa[expert_ids]
            Bb = Wb[expert_ids]
            low = jnp.einsum('bsd,brd->bsr', x, Ab)
            return ALPHA * jnp.einsum('bsr,bor->bso', low, Bb)
        key = jax.random.key(seed)
        ks = jax.random.split(key, 12)
        sd = lambda k, shape: jax.random.normal(k, shape, dtype=jnp.float32) * (1.0 / np.sqrt(shape[-1]))
        return {'hidden_states': jax.random.normal(ks[0], (B, S, D), dtype=jnp.float32), 'expert_ids': jax.random.randint(ks[1], (B,), 0, E, dtype=jnp.int32), 'wi': sd(ks[2], (F, D)), 'wo': sd(ks[3], (D, F)), 'common_wi_a': sd(ks[4], (R_COMMON, D)), 'common_wi_b': sd(ks[5], (F, R_COMMON)), 'common_wo_a': sd(ks[6], (R_COMMON, F)), 'common_wo_b': sd(ks[7], (D, R_COMMON)), 'experts_wi_a': sd(ks[8], (E, R_DOMAIN, D)), 'experts_wi_b': sd(ks[9], (F, R_DOMAIN)) * jnp.ones((E, 1, 1)) * 0.0 + sd(ks[9], (E, F, R_DOMAIN)), 'experts_wo_a': sd(ks[10], (E, R_DOMAIN, F)), 'experts_wo_b': sd(ks[11], (E, D, R_DOMAIN))}
    _L1_cond_all = _L1_cond_setup()
    _L1_cond_in = {k: v for k, v in _L1_cond_all.items() if k in ('wi', 'wo', 'common_wi_a', 'common_wi_b', 'common_wo_a', 'common_wo_b', 'experts_wi_a', 'experts_wi_b', 'experts_wo_a', 'experts_wo_b')}
    del _L1_cond_all

    def _L2_cond_setup():
        import jax, jax.numpy as jnp
        import numpy as np
        NEG_INF = -1e+30
        key = jax.random.key(seed)
        k1, k2, k3, k4, k5 = jax.random.split(key, 5)
        B, S, D, A = (16, 512, 512, 128)
        hidden = jax.random.normal(k1, (B, S, D), dtype=jnp.float32)
        W1 = jax.random.normal(k2, (D, A), dtype=jnp.float32) / np.sqrt(D)
        b1 = jax.random.normal(k3, (A,), dtype=jnp.float32) * 0.01
        v = jax.random.normal(k4, (A,), dtype=jnp.float32) / np.sqrt(A)
        prompt_type_ids = jax.random.randint(k5, (B,), 0, 3, dtype=jnp.int32)
        return {'hidden': hidden, 'W1': W1, 'b1': b1, 'v': v, 'prompt_type_ids': prompt_type_ids}
    _L2_cond_all = _L2_cond_setup()
    _L2_cond_in = {k: v for k, v in _L2_cond_all.items() if k in ('W1', 'b1', 'v')}
    del _L2_cond_all

    def _L3_cond_setup():
        import jax, jax.numpy as jnp
        import numpy as np
        LN_EPS = 1e-05
        key = jax.random.key(seed)
        ks = jax.random.split(key, 8)
        B, S, H, A, L = (32, 1024, 512, 128, 10)
        return {'hidden_states': jax.random.normal(ks[0], (B, S, H), dtype=jnp.float32), 'language_ids': jax.random.randint(ks[1], (B,), 0, L, dtype=jnp.int64), 'W1': jax.random.normal(ks[2], (L, H, A), dtype=jnp.float32) * (1.0 / np.sqrt(H)), 'b1': jnp.zeros((L, A), dtype=jnp.float32), 'W2': jax.random.normal(ks[3], (L, A, H), dtype=jnp.float32) * (1.0 / np.sqrt(A)), 'b2': jnp.zeros((L, H), dtype=jnp.float32), 'gamma': jnp.ones((L, H), dtype=jnp.float32), 'beta': jnp.zeros((L, H), dtype=jnp.float32)}
    _L3_cond_all = _L3_cond_setup()
    _L3_cond_in = {k: v for k, v in _L3_cond_all.items() if k in ('W1', 'b1', 'W2', 'b2', 'gamma', 'beta')}
    del _L3_cond_all
    return {'x': x, 'fside_Bx2_0': fside_Bx2_0, 'condB_angle': condB_angle, 'itok_B_0_7': itok_B_0_7, 'itok_B_0_2': itok_B_0_2, 'itok_B_0_8': itok_B_0_8, 'L1_cond_wi': _L1_cond_in['wi'], 'L1_cond_wo': _L1_cond_in['wo'], 'L1_cond_common_wi_a': _L1_cond_in['common_wi_a'], 'L1_cond_common_wi_b': _L1_cond_in['common_wi_b'], 'L1_cond_common_wo_a': _L1_cond_in['common_wo_a'], 'L1_cond_common_wo_b': _L1_cond_in['common_wo_b'], 'L1_cond_experts_wi_a': _L1_cond_in['experts_wi_a'], 'L1_cond_experts_wi_b': _L1_cond_in['experts_wi_b'], 'L1_cond_experts_wo_a': _L1_cond_in['experts_wo_a'], 'L1_cond_experts_wo_b': _L1_cond_in['experts_wo_b'], 'L2_cond_W1': _L2_cond_in['W1'], 'L2_cond_b1': _L2_cond_in['b1'], 'L2_cond_v': _L2_cond_in['v'], 'L3_cond_W1': _L3_cond_in['W1'], 'L3_cond_b1': _L3_cond_in['b1'], 'L3_cond_W2': _L3_cond_in['W2'], 'L3_cond_b2': _L3_cond_in['b2'], 'L3_cond_gamma': _L3_cond_in['gamma'], 'L3_cond_beta': _L3_cond_in['beta']}

def reference(x, fside_Bx2_0, condB_angle, itok_B_0_7, itok_B_0_2, itok_B_0_8, L1_cond_wi, L1_cond_wo, L1_cond_common_wi_a, L1_cond_common_wi_b, L1_cond_common_wo_a, L1_cond_common_wo_b, L1_cond_experts_wi_a, L1_cond_experts_wi_b, L1_cond_experts_wo_a, L1_cond_experts_wo_b, L2_cond_W1, L2_cond_b1, L2_cond_v, L3_cond_W1, L3_cond_b1, L3_cond_W2, L3_cond_b2, L3_cond_gamma, L3_cond_beta):
    import jax
    import jax.numpy as jnp

    def _L0_cond_ref(X, dx, angle):
        import jax, jax.numpy as jnp
        import numpy as np
        B, H, W = (32, 512, 512)
        SCALE_DX = 1.0
        SCALE_ANGLE = 1.0

        def _rigid_transform(X, dx, angle):
            b, h, w = X.shape
            gx = jnp.arange(w, dtype=jnp.float32)[None, :] - w / 2.0
            gy = jnp.arange(h, dtype=jnp.float32)[:, None] - h / 2.0
            theta = angle * SCALE_ANGLE
            c = jnp.cos(theta)[:, None, None]
            s = jnp.sin(theta)[:, None, None]
            xp = c * gx - s * gy + dx[:, 0, None, None] * SCALE_DX
            yp = s * gx + c * gy + dx[:, 1, None, None] * SCALE_DX
            gx_n = yp / h * 2.0
            gy_n = xp / w * 2.0
            ix = (gx_n + 1.0) * 0.5 * (w - 1)
            iy = (gy_n + 1.0) * 0.5 * (h - 1)
            ix0 = jnp.floor(ix)
            iy0 = jnp.floor(iy)
            wx1 = ix - ix0
            wy1 = iy - iy0
            wx0 = 1.0 - wx1
            wy0 = 1.0 - wy1
            ix0i = ix0.astype(jnp.int32)
            iy0i = iy0.astype(jnp.int32)
            ix1i = ix0i + 1
            iy1i = iy0i + 1
            bidx = jnp.arange(b, dtype=jnp.int32)[:, None, None]

            def gather(yi, xi):
                valid = (xi >= 0) & (xi <= w - 1) & (yi >= 0) & (yi <= h - 1)
                xc = jnp.clip(xi, 0, w - 1)
                yc = jnp.clip(yi, 0, h - 1)
                return X[bidx, yc, xc] * valid.astype(X.dtype)
            out = gather(iy0i, ix0i) * (wy0 * wx0) + gather(iy0i, ix1i) * (wy0 * wx1) + gather(iy1i, ix0i) * (wy1 * wx0) + gather(iy1i, ix1i) * (wy1 * wx1)
            return out
        return _rigid_transform(X, dx, angle)

    def _L1_cond_ref(hidden_states, expert_ids, wi, wo, common_wi_a, common_wi_b, common_wo_a, common_wo_b, experts_wi_a, experts_wi_b, experts_wo_a, experts_wo_b):
        import jax, jax.numpy as jnp
        import numpy as np
        B, S, D, F = (32, 256, 512, 2048)
        R_COMMON, R_DOMAIN, E = (16, 16, 8)
        ALPHA = 2.0

        def _expert_lora(x, expert_ids, Wa, Wb):
            Ab = Wa[expert_ids]
            Bb = Wb[expert_ids]
            low = jnp.einsum('bsd,brd->bsr', x, Ab)
            return ALPHA * jnp.einsum('bsr,bor->bso', low, Bb)
        x = hidden_states
        hidden_i = jnp.einsum('bsd,fd->bsf', x, wi)
        hidden_i += ALPHA * jnp.einsum('bsr,fr->bsf', jnp.einsum('bsd,rd->bsr', x, common_wi_a), common_wi_b)
        hidden_i += _expert_lora(x, expert_ids, experts_wi_a, experts_wi_b)
        hidden_i = jax.nn.relu(hidden_i)
        hidden_o = jnp.einsum('bsf,df->bsd', hidden_i, wo)
        hidden_o += ALPHA * jnp.einsum('bsr,dr->bsd', jnp.einsum('bsf,rf->bsr', hidden_i, common_wo_a), common_wo_b)
        hidden_o += _expert_lora(hidden_i, expert_ids, experts_wo_a, experts_wo_b)
        return hidden_o

    def _L2_cond_ref(hidden, W1, b1, v, prompt_type_ids):
        import jax, jax.numpy as jnp
        import numpy as np
        NEG_INF = -1e+30
        B, S, D = hidden.shape
        attn_in = jnp.tanh(jnp.einsum('bsd,da->bsa', hidden, W1) + b1)
        scores = jnp.einsum('bsa,a->bs', attn_in, v)
        idx = jnp.arange(S)
        j = idx[:, None]
        l = idx[None, :]
        prefix_m = l <= j
        postfix_m = l >= j
        cloze_m = l != j
        pt = prompt_type_ids[:, None, None]
        mask = jnp.where(pt == 0, prefix_m[None], jnp.where(pt == 1, postfix_m[None], cloze_m[None]))
        masked_scores = jnp.where(mask, scores[:, None, :], NEG_INF)
        p = jax.nn.softmax(masked_scores, axis=-1)
        cnt = jnp.sum(mask, axis=-1).astype(hidden.dtype)
        pooled = jnp.einsum('bjl,bld->bjd', p, hidden) / cnt[..., None]
        return pooled

    def _L3_cond_ref(hidden_states, language_ids, W1, b1, W2, b2, gamma, beta):
        import jax, jax.numpy as jnp
        import numpy as np
        LN_EPS = 1e-05
        w1 = W1[language_ids]
        w2 = W2[language_ids]
        h = jnp.einsum('bsh,bha->bsa', hidden_states, w1) + b1[language_ids][:, None, :]
        h = jax.nn.relu(h)
        adapted = jnp.einsum('bsa,bah->bsh', h, w2) + b2[language_ids][:, None, :]
        x = hidden_states + adapted
        mean = jnp.mean(x, axis=-1, keepdims=True)
        var = jnp.mean(jnp.square(x - mean), axis=-1, keepdims=True)
        normed = (x - mean) * jax.lax.rsqrt(var + LN_EPS)
        return normed * gamma[language_ids][:, None, :] + beta[language_ids][:, None, :]
    x = x + _L0_cond_ref(x, fside_Bx2_0, condB_angle)
    x = x + _L1_cond_ref(x, itok_B_0_7, L1_cond_wi, L1_cond_wo, L1_cond_common_wi_a, L1_cond_common_wi_b, L1_cond_common_wo_a, L1_cond_common_wo_b, L1_cond_experts_wi_a, L1_cond_experts_wi_b, L1_cond_experts_wo_a, L1_cond_experts_wo_b)
    x = x + _L2_cond_ref(x, L2_cond_W1, L2_cond_b1, L2_cond_v, itok_B_0_2)
    x = x + _L3_cond_ref(x, itok_B_0_8, L3_cond_W1, L3_cond_b1, L3_cond_W2, L3_cond_b2, L3_cond_gamma, L3_cond_beta)
    return x

_drawn_inputs = setup_inputs


def setup_inputs(seed=0):
    import zlib

    import numpy as np

    out = dict(_drawn_inputs(seed))
    spreads = {'L3_cond_b1': (0.0, 2.0),
     'L3_cond_b2': (0.0, 2.0),
     'L3_cond_gamma': (1.0, 0.6),
     'L3_cond_beta': (0.0, 0.666)}
    factors = {'L2_cond_W1': 4.469, 'L2_cond_b1': 64.0, 'L2_cond_v': 3.937}
    for name, (base, spread) in spreads.items():
        noise = np.random.default_rng([zlib.crc32(name.encode()), seed]).standard_normal(out[name].shape)
        drawn = base * np.exp(spread * noise) if base else spread * noise
        out[name] = jnp.asarray(drawn.astype(out[name].dtype))
    for name, factor in factors.items():
        out[name] = (out[name] * factor).astype(out[name].dtype)
    return out
```

```python
import numpy as np
import concourse.bass as bass
from concourse import mybir
from contextlib import ExitStack

T = 128
D = 512
F = 2048
KT = D // 128
FT = F // 128
E, R = 8, 16
NL = 10
A = 128
ALPHA = 2.0
EPS = 1e-5
BIG = 1e30

RY = (T - 1) / D
RX = (D - 1) / T
GP = 8
NG = 8
Q = GP * GP
HALF = Q // 2
TAPS = 3
SW, SS = 128, 64
NS = D // SS + 2
PADY = 5
ROWS = T + 2 * PADY
SLOT = NS * ROWS * SW
RUN = 4 * SW + 44
OFF_MAX = 2 * SW + 39
XLO, XHI = -float(SS), float(D)
YLO, YHI = -float(PADY), float(T)

ALU = mybir.AluOpType
ACT = mybir.ActivationFunctionType
AX = mybir.AxisListType
fp32, i32 = mybir.dt.float32, mybir.dt.int32


def build(nc, x, fside, angle, tok_expert, tok_prompt, tok_lang, wi, wo, cwi_a, cwi_b, cwo_a, cwo_b,
          ewi_a, ewi_b, ewo_a, ewo_b, aW1, ab1, av, lW1, lb1, lW2, lb2, lgamma, lbeta, out):
    B = x.shape[0]
    NP = B // 2
    ctx = ExitStack()
    with ctx:
        def sb(name, shape, dt=fp32):
            return ctx.enter_context(nc.sbuf_tensor(name, shape, dt))

        def sem(name):
            return ctx.enter_context(nc.semaphore(name))

        def ap(handle, offset, dims):
            return bass.AP(handle.tensor, offset, dims)

        strips = nc.dram_tensor("strips", (2, NS, ROWS, SW), fp32).ap()
        frac_dram = nc.dram_tensor("frac_dram", (B, 2 * Q), fp32).ap()
        offs_dram = nc.dram_tensor("offs_dram", (B, Q), i32).ap()

        wiT = sb("wiT", [128, KT, F])
        woT = sb("woT", [128, FT, D])
        ewiaT = sb("ewiaT", [128, KT, E * R])
        ewibT = sb("ewibT", [E * R, F])
        ewoaT = sb("ewoaT", [128, FT, E * R])
        ewobT = sb("ewobT", [E * R, D])
        aw1 = sb("aw1", [128, KT, A])
        ab1c = sb("ab1c", [A, 1])
        avc = sb("avc", [A, 1])
        vneg = sb("vneg", [A, T])
        ident = sb("ident", [128, 128])
        ones_row = sb("ones_row", [1, 128])
        prompt_mask = sb("prompt_mask", [T, 3, T])
        is_prefix = sb("is_prefix", [128, B])
        is_postfix = sb("is_postfix", [128, B])
        inv_count = sb("inv_count", [128, B])
        expert_gain = sb("expert_gain", [128, B])
        lb1_img = sb("lb1_img", [A, B])
        lang_row = sb("lang_row", [1, B], i32)
        gather_at = sb("gather_at", [128, B, NG], i32)
        gather_now = sb("gather_now", [128, 2, NG], i32)
        frac_group = sb("frac_group", [128, B, 2, NG])
        WORK = NG * RUN + NG * HALF * 9 + 2 * NG * Q * TAPS
        work = sb("work", [128, WORK])
        o1 = NG * RUN
        o2 = o1 + NG * HALF * 9
        win = work[:, 0:o1].rearrange("p (g r) -> p g r", g=NG)
        prod = work[:, o1:o2]
        taps = work[:, o2:WORK]
        warp_sum = sb("warp_sum", [128, D])
        warped = sb("warped", [T, 2, D])
        frac_pix = sb("frac_pix", [128, 2, 2 * Q])
        offs = sb("offs", [1, 2, Q], i32)
        xin = sb("xin", [T, 2, D])
        x1 = sb("x1", [T, 2, D])
        x1T = sb("x1T", [128, KT, 2 * T])
        hidden = sb("hidden", [128, 4, 2 * T])
        low_i = sb("low_i", [E * R, 2 * T])
        low_o = sb("low_o", [E * R, 2 * T])
        x2 = sb("x2", [T, 2, D])
        xT = sb("xT", [128, 2, KT, T])
        att = sb("att", [A, 2, T])
        masked = sb("masked", [T, 2, T])
        mask_now = sb("mask_now", [T, 2, T])
        probs = sb("probs", [T, 2, T])
        probsT = sb("probsT", [T, 2, T])
        hA = sb("hA", [A, 2, T])
        neg_max = sb("neg_max", [T, 2])
        row_sum = sb("row_sum", [T, 2])
        pool_scale = sb("pool_scale", [T, 2])
        stats = sb("stats", [T, 2, 6])
        mv = sb("mv", [T, 2, 2])
        rstd = sb("rstd", [T, 2])
        gain_now = sb("gain_now", [128, 2])
        lb1_now = sb("lb1_now", [A, 2])
        var_eps = sb("var_eps", [T, 2])
        newton = sb("newton", [T, 2])
        guess_i = sb("guess_i", [T, 2], i32)
        y = sb("y", [T, 2, D])
        lw1 = sb("lw1", [128, 2, KT, A])
        lw2 = sb("lw2", [A, 2, D])
        gamma_b = sb("gamma_b", [T, 2, D])
        beta_b = sb("beta_b", [T, 2, D])
        lb2_row = sb("lb2_row", [1, 2, D])
        NA = B + 1
        ang = sb("ang", [128, NA])
        sincos = sb("sincos", [128, 2, NA])
        trig = sb("trig", [128, 2, NA])
        part_i = sb("part_i", [128, 3], i32)
        part = sb("part", [128, 5])
        group_i = sb("group_i", [128, 2, NG], i32)
        group = sb("group", [128, 2, NG])
        pixel_i = sb("pixel_i", [128, 2, Q], i32)
        shift = sb("shift", [128, B, 2])
        ids_i = sb("ids_i", [128, 3, B], i32)
        ids = sb("ids", [128, 3, B])

        banks = [ctx.enter_context(nc.psum_tensor(f"bank{n}", [128, 512], fp32)) for n in range(8)]
        up_ps = [banks[0], banks[1]]
        down_ps = [banks[2], banks[3]]
        low_ps = banks[4]
        tr_ps = banks[5]
        mid_ps = banks[6]
        wide_ps = banks[7]

        in_loaded = sem("in_loaded")
        wi_in = [sem("wi_in0"), sem("wi_in1")]
        wo_in = [sem("wo_in0"), sem("wo_in1")]
        common_in = sem("common_in")
        corr_in = sem("corr_in")
        ewib_in = sem("ewib_in")
        zero_ready = sem("zero_ready")
        strips_zero = sem("strips_zero")
        consts_ready = sem("consts_ready")
        pool_chain = sem("pool_chain")
        set_chain = sem("set_chain")
        set_ready = sem("set_ready")
        sin_ready = sem("sin_ready")
        tables_ready = sem("tables_ready")
        pe_set = sem("pe_set")
        ev_dve = sem("ev_dve")
        ev_act = sem("ev_act")
        pix_out = sem("pix_out")
        strips_in = [sem("strips_in0"), sem("strips_in1")]
        x_in = [sem("x_in0"), sem("x_in1")]
        pix_in = [sem("pix_in0"), sem("pix_in1")]
        lang_in = [sem("lang_in0"), sem("lang_in1")]
        stored = [sem("stored0"), sem("stored1")]
        gathered = [sem("gathered0"), sem("gathered1")]
        taps_ready = sem("taps_ready")
        taps_used = sem("taps_used")
        win_used = sem("win_used")
        warp_chain = sem("warp_chain")
        x1_ready = sem("x1_ready")
        x1T_ps = sem("x1T_ps")
        x1T_ready = sem("x1T_ready")
        low_i_ps = sem("low_i_ps")
        low_i_ready = sem("low_i_ready")
        up_done = sem("up_done")
        hidden_ready = sem("hidden_ready")
        down_done = sem("down_done")
        low_o_ps = sem("low_o_ps")
        low_o_ready = sem("low_o_ready")
        ffn_done = sem("ffn_done")
        x2_ready = sem("x2_ready")
        x2T_ps = sem("x2T_ps")
        xT_ready = sem("xT_ready")
        att_ps = sem("att_ps")
        att_ready = sem("att_ready")
        score_ps = sem("score_ps")
        masked_ready = sem("masked_ready")
        probs_ready = sem("probs_ready")
        probsT_ps = sem("probsT_ps")
        probsT_ready = sem("probsT_ready")
        pooled_ps = sem("pooled_ps")
        x3_ready = sem("x3_ready")
        x3T_ps = sem("x3T_ps")
        h_ps = sem("h_ps")
        h_ready = sem("h_ready")
        adapt_ps = sem("adapt_ps")
        adapt_read = sem("adapt_read")
        y_ready = sem("y_ready")
        tail_chain = sem("tail_chain")
        act_chain = sem("act_chain")

        def ge(eng, s, n):
            if not isinstance(n, int) or n > 0:
                eng.wait_ge(s, n)

        def col(table, n):
            return table[:, bass.ds(n, 1)]


        def ge(eng, s, n):
            if not isinstance(n, int) or n > 0:
                eng.wait_ge(s, n)

        def settle(eng):
            eng.wait_ge(consts_ready, 1)

        def col(table, n):
            return table[:, bass.ds(n, 1)]

        st_w = work[:, 0:4096]
        st_ewib = work[:, 4096:6144].rearrange("p (t e r) -> p t e r", e=E, r=R)
        st_ewoa = work[:, 6144:8192]
        st_ewia = work[:, 8192:8704]
        st_ewob = work[:, 8704:9216].rearrange("p (t e r) -> p t e r", e=E, r=R)
        st_cwib = work[:, 9216:9472].rearrange("p (t r) -> p t r", r=R)
        st_cwob = work[:, 9472:9536].rearrange("p (t r) -> p t r", r=R)
        st_lb1 = y[0:NL, 0, 0:A]
        lang_hot = y[0:NL, 0, A:A + B]
        st_cwia = xin[0:R, 0, :]
        cwobT = xin[0:R, 1, :]
        hidden_flat = hidden[:, :, :].rearrange("p s t -> p (s t)")
        cwibT = [hidden_flat[0:R, 0:512], hidden_flat[0:R, 512:1024], x2[0:R, 0, :], x2[0:R, 1, :]]
        st_cwoa = [gamma_b[0:R, 0, :], gamma_b[0:R, 1, :], beta_b[0:R, 0, :], beta_b[0:R, 1, :]]

        jobs = ([("cwib", t) for t in range(FT // 4)] + [("cwob", 0)] + [("wi", t) for t in range(FT)]
                + [("ewia", 0), ("lb1", 0)] + [("ewoa", t) for t in range(4)] + [("ewob", 0)]
                + [("ewib", t) for t in range(4)]
                + [("wo", (dt, t)) for dt in range(KT) for t in range(4)])
        at_job = {job: n for n, job in enumerate(jobs)}
        halves = [len(jobs[0::2]), len(jobs[1::2])]

        def job_ends(kind, t):
            b = banks[at_job[(kind, t)] % 8]
            tiles = b[:, :].rearrange("p (a b) -> p a b", b=128)
            if kind == "cwib":
                return cwibT[t], b[0:R, :], ALPHA
            if kind == "cwob":
                return cwobT, b[0:R, :], ALPHA
            if kind == "wi":
                return wiT[:, :, t * 128:(t + 1) * 128], tiles, 1.0
            if kind == "ewia":
                return ewiaT[:, :, :], tiles, 1.0
            if kind == "ewib":
                return ewibT[:, t * 512:(t + 1) * 512], b[:, :], 1.0
            if kind == "ewoa":
                return ewoaT[:, 4 * t:4 * t + 4, :], tiles, 1.0
            if kind == "ewob":
                return ewobT[:, :], b[:, :], 1.0
            if kind == "lb1":
                return lb1_img[:, :], b[:, 0:B], 1.0
            dt, t = t
            return woT[:, 4 * t:4 * t + 4, dt * 128:(dt + 1) * 128], tiles, 1.0

        CORR = 2 + KT + 4
        pixel_f = xT[:, :, :, :].rearrange("p k t c -> p (k t c)")[0:B, :]
        pix_frac = pixel_f[:, 6 * Q:8 * Q]
        pix_offs = pixel_f[:, 8 * Q:9 * Q].bitcast(i32)

        block = ctx.enter_context(nc.Block())

        @block.sync
        def _(sp):
            small = 0
            sp.dma_start(ang[:, 0:B], angle.unsqueeze(0).broadcast_to([128, B])).then_inc(in_loaded, 16)
            sp.dma_start(shift[:, :, :].rearrange("p b c -> p (b c)"),
                         fside.rearrange("b c -> (b c)").unsqueeze(0).broadcast_to([128, 2 * B])).then_inc(in_loaded, 16)
            for n, tok in enumerate((tok_expert, tok_prompt, tok_lang)):
                sp.dma_start(ids_i[:, n, :], tok.unsqueeze(0).broadcast_to([128, B])).then_inc(in_loaded, 16)
            sp.dma_start(lang_row[:, :], tok_lang.unsqueeze(0)).then_inc(in_loaded, 16)
            sp.wait_ge(set_ready, 1)
            sp.dma_start(ang[0:B, B:B + 1], angle.unsqueeze(1)).then_inc(in_loaded, 16)
            sp.dma_start(st_cwib, cwi_b.rearrange("(t p) r -> p t r", p=128)).then_inc(common_in, 16)
            sp.dma_start(st_cwia, cwi_a).then_inc(common_in, 16)
            sp.dma_start(st_cwob, cwo_b.rearrange("(t p) r -> p t r", p=128)).then_inc(common_in, 16)
            for t in range(4):
                sp.dma_start(st_cwoa[t], cwo_a[:, t * 512:(t + 1) * 512]).then_inc(common_in, 16)
            sp.dma_start(st_w.rearrange("p (t d) -> p t d", t=8),
                         wi[0:1024, :].rearrange("(t p) d -> p t d", p=128)).then_inc(wi_in[0], 16)
            sp.dma_start(st_ewia, ewi_a.rearrange("e r d -> (e r) d")).then_inc(corr_in, 16)
            sp.dma_start(st_ewoa, ewo_a.rearrange("e r f -> (e r) f")).then_inc(corr_in, 16)
            for t in range(KT):
                sp.dma_start(st_ewob[:, t], ewo_b[:, t * 128:(t + 1) * 128, :].rearrange("e p r -> p e r")).then_inc(corr_in, 16)
            sp.dma_start(aw1[:, :, :], aW1.rearrange("(t p) a -> p t a", p=128)).then_inc(corr_in, 16)
            sp.dma_start(ab1c[:, :], ab1.unsqueeze(1)).then_inc(corr_in, 16)
            sp.dma_start(avc[:, :], av.unsqueeze(1)).then_inc(corr_in, 16)
            sp.dma_start(st_lb1, lb1).then_inc(corr_in, 16)
            sp.wait_ge(zero_ready, 1)
            per = 2 * SLOT // 128
            flat = strips.rearrange("k s r c -> (k s r c)").rearrange("(p n) -> p n", p=128)
            zeros = warped[:, :, :].rearrange("p k d -> p (k d)")
            cuts = list(range(0, per, 1024)) + [per]
            for a, b in zip(cuts[:-1], cuts[1:]):
                sp.dma_start(flat[:, a:b], zeros[:, 0:b - a]).then_inc(strips_zero, 16)
            sp.wait_ge(pe_set, at_job[("wi", 7)] + 1)
            sp.dma_start(st_w.rearrange("p (t d) -> p t d", t=8),
                         wi[1024:2048, :].rearrange("(t p) d -> p t d", p=128)).then_inc(wi_in[1], 16)
            sp.wait_ge(strips_zero, 16 * (len(cuts) - 1))

            def load_strips(a, k):
                ge(sp, gathered[k], 16 * NG * a)
                img = x[bass.ds(a * 2 + k, 1)].squeeze(0)
                src = bass.AP(img.tensor, img.offset, [[SS, NS - 3], [D, T], [1, SW]])
                sp.dma_start(strips[k, 1:NS - 2, PADY:PADY + T, :], src).then_inc(strips_in[k], 16)
                sp.dma_start(strips[k, 0, PADY:PADY + T, SS:SW], img[:, 0:SS]).then_inc(strips_in[k], 16)
                sp.dma_start(strips[k, NS - 2, PADY:PADY + T, 0:SS], img[:, D - SS:D]).then_inc(strips_in[k], 16)

            def load_pix(a, k):
                ge(sp, taps_ready, a * 2 + (k - 1))
                ge(sp, win_used, a * 2 + (k - 1))
                sp.dma_start(frac_pix[:, k, :], frac_dram[bass.ds(a * 2 + k, 1), :].broadcast_to([128, 2 * Q])).then_inc(pix_in[k], 16)
                sp.dma_start(offs[:, k, :], offs_dram[bass.ds(a * 2 + k, 1), :]).then_inc(pix_in[k], 16)

            def load_x(a, k):
                ge(sp, x1_ready, a * 2 + (k - 1))
                sp.dma_start(xin[:, k, :], x[bass.ds(a * 2 + k, 1)].squeeze(0)).then_inc(x_in[k], 16)

            def load_lang(c, k):
                ge(sp, y_ready, c * 2 + (k - 1))
                lang = sp.value_load(lang_row[0:1, bass.ds(c * 2 + k, 1)], min_val=0, max_val=NL - 1)
                pick = bass.ds(lang, 1)
                sp.dma_start(lw1[:, k, :, :], lW1[pick].squeeze(0).rearrange("(t p) a -> p t a", p=128)).then_inc(lang_in[k], 16)
                sp.dma_start(lw2[:, k, :], lW2[pick].squeeze(0)).then_inc(lang_in[k], 16)
                sp.dma_start(lb2_row[:, k, :], lb2[pick, :]).then_inc(lang_in[k], 16)
                sp.dma_start(gamma_b[:, k, :], lgamma[pick, :].broadcast_to([T, D])).then_inc(lang_in[k], 16)
                sp.dma_start(beta_b[:, k, :], lbeta[pick, :].broadcast_to([T, D])).then_inc(lang_in[k], 16)

            def store(c, k):
                sp.wait_ge(y_ready, c * 2 + (k + 1))
                sp.dma_start(out[bass.ds(c * 2 + k, 1)].squeeze(0), y[:, k, :]).then_inc(stored[k], 16)

            for k in range(2):
                load_strips(0, k)
            for r, last in enumerate((("wi", FT - 1), ("wo", (1, 3)))):
                sp.wait_ge(pe_set, at_job[last] + 1)
                sp.dma_start(st_w.rearrange("p (t f) -> p t f", t=2),
                             wo[r * 256:(r + 1) * 256, :].rearrange("(t p) f -> p t f", p=128)).then_inc(wo_in[r], 16)
            sp.wait_ge(set_ready, 3)
            sp.dma_start(frac_dram, pix_frac).then_inc(pix_out, 16)
            sp.dma_start(offs_dram, pix_offs).then_inc(pix_out, 16)
            sp.wait_ge(pix_out, 32)
            sp.wait_ge(pe_set, len(jobs))
            for k in range(2):
                load_pix(0, k)
                load_x(0, k)
            for k in range(2):
                load_strips(1, k)
            for k in range(2):
                load_pix(1, k)
            for k in range(2):
                load_x(1, k)

            def body(i, warp, tail):
                if tail:
                    for k in range(2):
                        load_lang(i - 1, k)
                if warp:
                    for k in range(2):
                        load_strips(i + 2, k)
                    for k in range(2):
                        load_pix(i + 2, k)
                if tail:
                    for k in range(2):
                        store(i - 1, k)
                if warp:
                    for k in range(2):
                        load_x(i + 2, k)

            body(0, True, False)
            body(1, True, True)
            with sp.Fori(2, NP - 2) as i:
                body(i, True, True)
            for i in range(NP - 2, NP + 1):
                body(i, False, True)
            for k in range(2):
                sp.wait_ge(stored[k], 16 * NP)

        @block.gpsimd
        def _(pool):
            g = nc.gpsimd
            g.memset(warped[:, :, :], 0.0).then_inc(zero_ready, 1)
            g.memset(ident[:, :], 0.0).then_inc(pool_chain, 1)
            g.memset(prompt_mask[:, :, :], 0.0).then_inc(pool_chain, 1)
            g.memset(ones_row[:, :], 1.0).then_inc(consts_ready, 1)
            g.iota(part_i[:, 0:1], pattern=[[0, 1]], base=0, channel_multiplier=1).then_inc(consts_ready, 1)
            g.iota(group_i[:, 0, :], pattern=[[32 * GP, 2], [0, 4]], base=-D // 2, channel_multiplier=0).then_inc(consts_ready, 1)
            g.iota(group_i[:, 1, :], pattern=[[0, 2], [GP, 4]], base=-T // 2, channel_multiplier=1).then_inc(consts_ready, 1)
            g.iota(pixel_i[:, 0, :], pattern=[[0, GP], [1, GP]], base=0, channel_multiplier=0).then_inc(consts_ready, 1)
            g.iota(pixel_i[:, 1, :], pattern=[[1, GP], [0, GP]], base=0, channel_multiplier=0).then_inc(consts_ready, 1)
            pool.wait_ge(pool_chain, 2)
            g.affine_select(out=ident[:, :], in_=ident[:, :], compare_op=ALU.not_equal, fill=1.0, base=0,
                            pattern=[[-1, 128]], channel_multiplier=1).then_inc(consts_ready, 1)
            for n, (op, sign) in enumerate(((ALU.is_ge, 1), (ALU.is_ge, -1), (ALU.not_equal, 1))):
                g.affine_select(out=prompt_mask[:, n, :], in_=prompt_mask[:, n, :], compare_op=op, fill=BIG, base=0,
                                pattern=[[-sign, T]], channel_multiplier=sign).then_inc(consts_ready, 1)
            for t in range(FT):
                pool.dma_start(st_ewib[:, t], ewi_b[:, t * 128:(t + 1) * 128, :].rearrange("e p r -> p e r")).then_inc(ewib_in, 16)
            pool.wait_ge(set_ready, 3)
            pool.wait_ge(pe_set, len(jobs))
            flat = bass.AP(strips.tensor, 0, [[1, 2 * SLOT], [1, 1]])
            t5 = taps.rearrange("p (x h g q t) -> p x h g q t", x=2, h=2, g=NG, q=HALF)
            t2 = taps.rearrange("p (m t) -> p m t", t=TAPS)
            def warp(a, k):
                n = a * 2 + k
                pool.sem_clear(pool_chain)
                pool.wait_ge(strips_in[k], a * 48 + 48)
                ge(pool, win_used, n)
                ge(pool, gathered[k], a * (16 * NG))
                g.tensor_copy(gather_now[:, k, :], gather_at[:, bass.ds(n, 1), :].squeeze(1)).then_inc(pool_chain, 1)
                pool.wait_ge(pool_chain, 1)
                for gi in range(NG):
                    at = gather_now[:, k, gi:gi + 1]
                    g.indirect_dma_start(out=win[:, gi, :], out_offset=None, in_=flat,
                                         in_offset=bass.IndirectOffsetOnAxis(at, 0)).then_inc(gathered[k], 16)
                pool.wait_ge(pix_in[k], a * 32 + 32)
                ge(pool, taps_used, n)
                for ax in range(2):
                    fg = frac_group[:, bass.ds(n, 1), ax, :].squeeze(1)
                    fp = frac_pix[:, k, ax * Q:(ax + 1) * Q].rearrange("p (h q) -> p h q", h=2)
                    g.tensor_tensor(t5[:, ax, :, :, :, 1],
                                    fg.unsqueeze(1).unsqueeze(3).broadcast_to([128, 2, NG, HALF]),
                                    fp.unsqueeze(2).broadcast_to([128, 2, NG, HALF]),
                                    ALU.add).then_inc(pool_chain, 1)
                pool.wait_ge(pool_chain, 3)
                g.tensor_scalar(t2[:, :, 0], t2[:, :, 1], 0.0, -1.0, ALU.min, ALU.mult).then_inc(pool_chain, 1)
                g.tensor_scalar(t2[:, :, 2], t2[:, :, 1], 0.0, None, ALU.max).then_inc(pool_chain, 1)
                pool.wait_ge(pool_chain, 5)
                g.tensor_tensor(t2[:, :, 1], t2[:, :, 0], t2[:, :, 2], ALU.add).then_inc(pool_chain, 1)
                pool.wait_ge(pool_chain, 6)
                g.tensor_scalar(t2[:, :, 1], t2[:, :, 1], -1.0, 1.0, ALU.mult, ALU.add).then_inc(taps_ready, 1)

            for k in range(2):
                warp(0, k)
            with pool.Fori(0, NP - 1) as i:
                for k in range(2):
                    warp(i + 1, k)

        @block.vector
        def _(dve):
            v = nc.vector
            chain = [0]

            def link(ins):
                chain[0] += 1
                ins.then_inc(set_chain, 1)
                dve.wait_ge(set_chain, chain[0])

            v.memset(ang[:, B:B + 1], 0.0).then_inc(set_ready, 1)
            dve.wait_ge(in_loaded, 16 * 7)
            dve.wait_ge(consts_ready, 10)
            PI = 3.1415925
            two_pi_hi, two_pi_lo = 6.28125, 2 * np.pi - 6.28125
            turns, r = trig[:, 1, :], trig[:, 0, :]
            turns_i = gather_at[:, :, :].rearrange("p b g -> p (b g)")[:, 0:NA]
            step = sincos[:, 0, :]
            link(v.tensor_scalar(turns_i, ang[:, :], float(1 / (2 * np.pi)), None, ALU.mult))
            link(v.tensor_copy(turns, turns_i))
            link(v.scalar_tensor_tensor(r, turns, -two_pi_hi, ang[:, :], ALU.mult, ALU.add))
            link(v.scalar_tensor_tensor(r, turns, -two_pi_lo, r, ALU.mult, ALU.add))
            link(v.tensor_scalar(step, r, PI, float(-2 * np.pi), ALU.is_gt, ALU.mult))
            link(v.tensor_tensor(r, r, step, ALU.add))
            link(v.tensor_scalar(step, r, -PI, float(2 * np.pi), ALU.is_lt, ALU.mult))
            link(v.tensor_tensor(r, r, step, ALU.add))
            link(v.tensor_scalar(trig[:, 1, :], r, float(np.pi / 2), None, ALU.add))
            link(v.tensor_scalar(step, trig[:, 1, :], PI, float(-2 * np.pi), ALU.is_gt, ALU.mult))
            link(v.tensor_tensor(trig[:, 1, :], trig[:, 1, :], step, ALU.add))
            v.tensor_scalar(trig[:, :, :], trig[:, :, :], PI, -PI, ALU.min, ALU.max).then_inc(set_ready, 1)
            link(v.tensor_scalar(part_i[:, 1:2], part_i[:, 0:1], 31, None, ALU.bitwise_and))
            link(v.tensor_scalar(part_i[:, 2:3], part_i[:, 0:1], 4, None, ALU.arith_shift_right))
            link(v.tensor_copy(part[:, 0:3], part_i[:, :]))
            link(v.tensor_scalar(part[:, 3:4], part[:, 0:1], float(2 - T), None, ALU.add))
            link(v.tensor_scalar(part[:, 4:5], part[:, 0:1], -1.0, 1.0, ALU.mult, ALU.add))
            link(v.tensor_copy(group[:, :, :], group_i[:, :, :]))
            eight = trig_free = stats[:, 0, 0:1]
            link(v.tensor_scalar(eight, part[:, 1:2], float(GP), None, ALU.mult))
            link(v.tensor_scalar(group[:, 0, :], group[:, 0, :], eight, None, ALU.add))
            link(v.tensor_scalar(group[:, 1, :], group[:, 1, :], part[:, 1:2], None, ALU.subtract))
            link(v.tensor_copy(ids[:, :, :], ids_i[:, :, :]))
            link(v.tensor_scalar(expert_gain[:, :], ids[:, 0, :], part[:, 2:3], ALPHA, ALU.is_equal, ALU.mult))
            link(v.tensor_scalar(is_prefix[:, :], ids[:, 1, :], 0.0, None, ALU.is_equal))
            link(v.tensor_scalar(is_postfix[:, :], ids[:, 1, :], 1.0, None, ALU.is_equal))
            link(v.tensor_scalar(lang_hot, ids[0:NL, 2, :], part[0:NL, 0:1], None, ALU.is_equal))
            link(v.tensor_scalar(inv_count[:, :], is_prefix[:, :], part[:, 3:4], float(T - 1), ALU.mult, ALU.add))
            link(v.scalar_tensor_tensor(inv_count[:, :], is_postfix[:, :], part[:, 4:5], inv_count[:, :], ALU.mult, ALU.add))
            link(v.reciprocal(inv_count[:, :], inv_count[:, :]))
            for n in range(2):
                link(v.tensor_tensor(prompt_mask[:, n, :], prompt_mask[:, n, :], prompt_mask[:, 2, :], ALU.subtract))
            dve.wait_ge(sin_ready, 1)
            sin, cos = sincos[:, 0, :], sincos[:, 1, :]
            low = trig
            link(v.tensor_scalar(low[:, 0, :], sin, 0.0, None, ALU.max))
            link(v.tensor_scalar(low[:, 1, :], cos, 0.0, None, ALU.min))
            link(v.tensor_tensor(low[:, 0, :], low[:, 1, :], low[:, 0, :], ALU.subtract))
            link(v.tensor_scalar(ang[:, :], sin, 0.0, None, ALU.min))
            link(v.tensor_tensor(low[:, 1, :], low[:, 1, :], ang[:, :], ALU.add))
            link(v.tensor_scalar(low[:, :, :], low[:, :, :], float(GP - 1), None, ALU.mult))

            def floor(value, whole_i, whole, over):
                link(v.tensor_copy(whole_i, value))
                link(v.tensor_copy(whole, whole_i))
                link(v.tensor_tensor(over, whole, value, ALU.is_gt))
                link(v.tensor_tensor(whole, whole, over, ALU.subtract))

            x1_flat = x1[:, :, :].rearrange("p k d -> p (k d)")
            x1T_flat = x1T[:, :, :].rearrange("p k t -> p (k t)")
            M = B * NG
            shape = lambda t: t.rearrange("p (b g) -> p b g", g=NG)
            pos, other = x1_flat[:, 0:M], x1_flat[:, M:2 * M] if 2 * M <= 2 * D else None
            whole, whole_i = x1T_flat[:, 0:M], x1T_flat[:, M:2 * M].bitcast(i32)
            at_f = y[:, 1, 0:M]
            for ax in range(2):
                on_x, on_y = (cos, sin) if ax == 0 else (sin, cos)
                wide = lambda t: t.unsqueeze(2).broadcast_to([128, B, NG])
                grp = lambda t: t.unsqueeze(1).broadcast_to([128, B, NG])
                link(v.tensor_tensor(shape(pos), wide(on_x[:, 0:B]), grp(group[:, 0, :]), ALU.mult))
                link(v.tensor_tensor(shape(other), wide(on_y[:, 0:B]), grp(group[:, 1, :]), ALU.mult))
                link(v.tensor_tensor(pos, pos, other, ALU.subtract if ax == 0 else ALU.add))
                link(v.tensor_tensor(ang[:, 0:B], shift[:, :, ax], low[:, ax, 0:B], ALU.add))
                link(v.tensor_tensor(shape(pos), shape(pos), wide(ang[:, 0:B]), ALU.add))
                rate, mid, lo, hi = (RY, (T - 1) / 2, YLO, YHI) if ax == 0 else (RX, (D - 1) / 2, XLO, XHI)
                link(v.tensor_scalar(pos, pos, rate, mid, ALU.mult, ALU.add))
                link(v.tensor_scalar(pos, pos, hi, lo, ALU.min, ALU.max))
                floor(pos, whole_i, whole, other)
                link(v.scalar_tensor_tensor(frac_group[:, :, ax, :], shape(pos), -1.0, shape(whole), ALU.add, ALU.subtract))
                if ax == 0:
                    link(v.tensor_scalar(at_f, whole, float(PADY), float(SW), ALU.add, ALU.mult))
                else:
                    strip_i, in_strip_i = pos.bitcast(i32), other.bitcast(i32)
                    link(v.tensor_scalar(whole_i, whole, float(SS), None, ALU.add))
                    link(v.tensor_scalar(strip_i, whole_i, 6, None, ALU.arith_shift_right))
                    link(v.tensor_scalar(in_strip_i, whole_i, SS - 1, None, ALU.bitwise_and))
                    link(v.tensor_copy(whole, strip_i))
                    link(v.scalar_tensor_tensor(at_f, whole, float(ROWS * SW), at_f, ALU.mult, ALU.add))
                    link(v.tensor_copy(whole, in_strip_i))
                    link(v.tensor_tensor(at_f, at_f, whole, ALU.add))
            odd = at_f.rearrange("p (a k g) -> p a k g", k=2, g=NG)[:, :, 1, :]
            link(v.tensor_scalar(odd, odd, float(SLOT), None, ALU.add))
            link(v.tensor_copy(gather_at[:, :, :].rearrange("p b g -> p (b g)"), at_f))

            pix = pixel_f
            own_sin, own_cos = sincos[0:B, 0, B:NA], sincos[0:B, 1, B:NA]
            row, column = pix[:, 0:Q], pix[:, Q:2 * Q]
            a1, a2, a3, a4 = (pix[:, (2 + n) * Q:(3 + n) * Q] for n in range(4))
            link(v.tensor_copy(pix[:, 0:2 * Q], pixel_i[0:B, :, :].rearrange("p a q -> p (a q)")))
            for ax in range(2):
                on_x, on_y = (own_cos, own_sin) if ax == 0 else (own_sin, own_cos)
                link(v.tensor_scalar(a1, column, on_x, None, ALU.mult))
                link(v.tensor_scalar(a2, row, on_y, None, ALU.mult))
                link(v.tensor_tensor(a1, a1, a2, ALU.subtract if ax == 0 else ALU.add))
                link(v.tensor_scalar(a1, a1, low[0:B, ax, B:NA], RY if ax == 0 else RX, ALU.subtract, ALU.mult))
                link(v.tensor_scalar(a1, a1, 0.0, None, ALU.max))
                floor(a1, pix_offs, a2, a3)
                link(v.tensor_tensor(pix_frac[:, ax * Q:(ax + 1) * Q], a1, a2, ALU.subtract))
                if ax == 0:
                    link(v.tensor_scalar(a4, a2, float(SW), None, ALU.mult))
                else:
                    link(v.tensor_tensor(a4, a4, a2, ALU.add))
            v.tensor_copy(pix_offs, a4).then_inc(set_ready, 1)
            dve.wait_ge(corr_in, 16 * CORR)
            v.tensor_scalar(vneg[:, :], ident[:, :], 0.0, avc[:, 0:1], ALU.mult, ALU.subtract).then_inc(tables_ready, 1)

            for n in range(0, len(jobs), 2):
                dst, src, factor = job_ends(*jobs[n])
                dve.wait_ge(pe_set, n + 1)
                v.tensor_scalar(dst, src, factor, None, ALU.mult).then_inc(ev_dve, 1)

            regs = [ctx.enter_context(v.register(f"window_offset{n}")) for n in range(8)]

            def warp(a, k):
                n = a * 2 + k
                count = [0]

                def link(ins):
                    count[0] += 1
                    ins.then_inc(warp_chain, 1)
                    dve.wait_ge(warp_chain, count[0])

                dve.sem_clear(warp_chain)
                dve.wait_ge(taps_ready, n + 1)
                t6 = taps.rearrange("p (x h m t) -> p x h m t", x=2, h=2, t=TAPS)
                p3 = prod.rearrange("p (m a b) -> p m a b", a=3, b=3)
                p2 = prod.rearrange("p (g q t) -> p g q t", g=NG, q=HALF)
                p5 = prod.rearrange("p (w g j i t) -> p w g j i t", w=2, g=4, j=4, t=9)
                s5 = warp_sum[:, :].rearrange("p (w j g i) -> p w g j i", w=2, j=GP, g=4)
                for h in range(2):
                    wy = t6[:, 0, h].unsqueeze(3).broadcast_to([128, NG * HALF, 3, 3])
                    wx = t6[:, 1, h].unsqueeze(2).broadcast_to([128, NG * HALF, 3, 3])
                    if h == 0:
                        dve.wait_ge(gathered[k], a * (16 * NG) + 16 * NG)
                        dve.wait_ge(pix_in[k], a * 32 + 32)
                        link(v.tensor_tensor(p3, wy, wx, ALU.mult))
                        v.load(regs, offs[0:1, k, 0:8])
                    else:
                        v.load(regs, offs[0:1, k, HALF:HALF + 8])
                        v.tensor_tensor(p3, wy, wx, ALU.mult).then_inc(taps_used, 1)
                        dve.wait_ge(taps_used, n + 1)
                    for q in range(HALF):
                        if q and q % 8 == 0:
                            v.load(regs, offs[0:1, k, h * HALF + q:h * HALF + q + 8])
                        at = v.snap(regs[q % 8], min_val=0, max_val=OFF_MAX)
                        first = win[:, :, bass.ds(at, 1)]
                        seen = bass.AP(first.tensor, first.offset, [first.ap[0], [RUN, NG], [SW, 3], [1, 3]])
                        o = p2[:, :, q, :].rearrange("p g (a b) -> p g a b", a=3)
                        last = v.tensor_tensor(o, seen, o, ALU.mult)
                    if h == 0:
                        link(last)
                    else:
                        last.then_inc(win_used, 1)
                        dve.wait_ge(win_used, n + 1)
                    for w in range(2):
                        last = v.tensor_reduce(s5[:, w, :, 4 * h:4 * h + 4, :], p5[:, w], axis=AX.X, op=ALU.add)
                    link(last)
                ge(dve, x1_ready, a * 2 + (k - 1))
                link(v.transpose(warped[:, k, :].rearrange("p (w c j) -> p w j c", w=2, j=GP),
                                 warp_sum[:, :].rearrange("p (w j c) -> p w j c", w=2, j=GP)))

            def add_warp(a, k):
                dve.wait_ge(x_in[k], a * 16 + 16)
                v.tensor_tensor(x1[:, k, :], xin[:, k, :], warped[:, k, :], ALU.add).then_inc(x1_ready, 1)

            def body(i, warp_next, ffn, tail):
                c = i - 1
                count = [0]

                def link(ins):
                    count[0] += 1
                    ins.then_inc(tail_chain, 1)
                    dve.wait_ge(tail_chain, count[0])

                def mask_scores(k):
                    n = c * 2 + k
                    now = mask_now[:, k, :]
                    ge(dve, masked_ready, c * 2 + (k - 1))
                    link(v.scalar_tensor_tensor(now, prompt_mask[:, 1, :], col(is_postfix, n), prompt_mask[:, 2, :], ALU.mult, ALU.add))
                    dve.wait_ge(score_ps, n + 1)
                    link(v.scalar_tensor_tensor(now, prompt_mask[:, 0, :], col(is_prefix, n), now, ALU.mult, ALU.add))
                    v.tensor_tensor_reduce(out=masked[:, k, :], in0=mid_ps[:, 0:T], in1=now, scale=1.0, scalar=3e38,
                                           op0=ALU.add, op1=ALU.min, accum_out=neg_max[:, k:k + 1]).then_inc(masked_ready, 1)

                def add_pooled(k):
                    n = c * 2 + k
                    dve.wait_ge(probs_ready, n + 1)
                    ps = pool_scale[:, k:k + 1]
                    link(v.reciprocal(ps, row_sum[:, k:k + 1]))
                    link(v.tensor_tensor(ps, ps, col(inv_count, n), ALU.mult))
                    dve.wait_ge(pooled_ps, n + 1)
                    v.scalar_tensor_tensor(x2[:, k, :], wide_ps[:, :], ps, x2[:, k, :], ALU.mult, ALU.add).then_inc(x3_ready, 1)

                def adapted(k):
                    n = c * 2 + k
                    yk = y[:, k, :]
                    dve.wait_ge(adapt_ps, n + 1)
                    ge(dve, stored[k], c * 16)
                    v.tensor_tensor(yk, wide_ps[:, :], x2[:, k, :], ALU.add).then_inc(adapt_read, 1)
                    dve.wait_ge(adapt_read, n + 1)
                    link(v.bn_stats(stats[:, k, :], yk))
                    link(v.bn_aggr(mv[:, k, :], stats[:, k, :]))

                def inverse_deviations():
                    link(v.tensor_scalar(var_eps[:, :], mv[:, :, 1], EPS, None, ALU.add))
                    link(v.tensor_scalar(guess_i[:, :], var_eps[:, :].bitcast(i32), 1, None, ALU.arith_shift_right))
                    link(v.tensor_scalar(rstd[:, :].bitcast(i32), guess_i[:, :], -1.0, float(0x5F3759DF), ALU.mult, ALU.add))
                    for _ in range(3):
                        link(v.tensor_tensor(newton[:, :], rstd[:, :], rstd[:, :], ALU.mult))
                        link(v.scalar_tensor_tensor(newton[:, :], newton[:, :], -0.5, var_eps[:, :], ALU.mult, ALU.mult))
                        link(v.scalar_tensor_tensor(rstd[:, :], newton[:, :], 1.5, rstd[:, :], ALU.add, ALU.mult))

                def normalise(k):
                    yk = y[:, k, :]
                    link(v.tensor_scalar(yk, yk, mv[:, k, 0:1], rstd[:, k:k + 1], ALU.subtract, ALU.mult))
                    link(v.tensor_tensor(yk, yk, gamma_b[:, k, :], ALU.mult))
                    link(v.tensor_tensor(yk, yk, beta_b[:, k, :], ALU.add))
                    v.tensor_tensor(yk, yk, x2[:, k, :], ALU.add).then_inc(y_ready, 1)

                if warp_next:
                    warp(i + 1, 0)
                if tail:
                    dve.sem_clear(tail_chain)
                    for k in range(2):
                        mask_scores(k)
                if warp_next:
                    warp(i + 1, 1)
                if tail:
                    for k in range(2):
                        add_pooled(k)
                    for k in range(2):
                        adapted(k)
                    inverse_deviations()
                    for k in range(2):
                        dve.wait_ge(lang_in[k], c * 80 + 80)
                        normalise(k)
                for k in range(2):
                    if ffn:
                        ge(dve, y_ready, c * 2 + (k + 1))
                        dve.wait_ge(ffn_done, i * 2 + (k + 1))
                        v.tensor_tensor(x2[:, k, :], down_ps[k][:, :], x1[:, k, :], ALU.add).then_inc(x2_ready, 1)
                    if warp_next:
                        ge(dve, x2_ready, i * 2 + (k + 1))
                        add_warp(i + 1, k)

            body(-1, True, False, False)
            body(0, True, True, False)
            body(1, True, True, True)
            with dve.Fori(2, NP - 1) as i:
                body(i, True, True, True)
            body(NP - 1, False, True, True)
            body(NP, False, False, True)

        @block.scalar
        def _(act):
            s = nc.scalar
            act.wait_ge(set_ready, 2)
            s.activation(sincos[:, :, :], trig[:, :, :], ACT.Sin).then_inc(sin_ready, 1)
            for n in range(1, len(jobs), 2):
                dst, src, factor = job_ends(*jobs[n])
                act.wait_ge(pe_set, n + 1)
                s.activation(dst, src, ACT.Copy, scale=factor).then_inc(ev_act, 1)
            act.wait_ge(corr_in, 16 * CORR)
            act.wait_ge(ev_dve, halves[0])

            def body(i, ffn, tail):
                c = i - 1

                def copy_T(k, filled, count):
                    act.wait_ge(filled, c * 2 + (k + 1))
                    s.activation(xT[:, k, :, :].rearrange("p t c -> p (t c)"), tr_ps[:, :], ACT.Copy).then_inc(xT_ready, 1)

                def attend(k):
                    act.wait_ge(att_ps, c * 2 + (k + 1))
                    s.activation(att[:, k, :], mid_ps[:, 0:T], ACT.Tanh, bias=ab1c[:, 0:1]).then_inc(att_ready, 1)

                def exponentials(k):
                    act.wait_ge(masked_ready, c * 2 + (k + 1))
                    s.activation(probs[:, k, :], masked[:, k, :], ACT.Exp, bias=neg_max[:, k:k + 1], scale=-1.0,
                                 accum_out=row_sum[:, k:k + 1]).then_inc(probs_ready, 1)

                def copy_probs(k):
                    act.wait_ge(probsT_ps, c * 2 + (k + 1))
                    s.activation(probsT[:, k, :], mid_ps[:, 0:T], ACT.Copy).then_inc(probsT_ready, 1)

                def adapter_relu(k):
                    act.wait_ge(h_ps, c * 2 + (k + 1))
                    s.activation(hA[:, k, :], mid_ps[:, 0:T], ACT.Relu, bias=lb1_now[:, k:k + 1]).then_inc(h_ready, 1)

                steps = {0: (copy_T, 0, x2T_ps, 0), 1: (copy_T, 1, x2T_ps, 1), 2: (attend, 0), 3: (attend, 1),
                         5: (exponentials, 0), 6: (exponentials, 1), 7: (copy_probs, 0), 8: (copy_probs, 1),
                         10: (copy_T, 0, x3T_ps, 2), 11: (copy_T, 1, x3T_ps, 3), 12: (adapter_relu, 0), 13: (adapter_relu, 1)}

                act.sem_clear(act_chain)
                ge(act, low_o_ready, i * 2)
                ge(act, h_ready, c * 2)
                if ffn:
                    s.activation(gain_now[:, :], expert_gain[:, bass.ds(i * 2, 2)], ACT.Copy).then_inc(act_chain, 1)
                if tail:
                    s.activation(lb1_now[:, :], lb1_img[:, bass.ds(c * 2, 2)], ACT.Copy).then_inc(act_chain, 1)
                act.wait_ge(act_chain, ffn + tail)
                if ffn:
                    for k in range(2):
                        act.wait_ge(x1T_ps, i * 2 + (k + 1))
                        s.activation(x1T[:, :, k * T:(k + 1) * T], up_ps[k][:, :].rearrange("p (t c) -> p t c", t=KT),
                                     ACT.Copy).then_inc(x1T_ready, 1)
                    act.wait_ge(low_i_ps, i + 1)
                    for k in range(2):
                        s.activation(low_i[:, k * T:(k + 1) * T], low_ps[:, k * T:(k + 1) * T], ACT.Copy,
                                     scale=gain_now[:, k:k + 1]).then_inc(low_i_ready, 1)
                for f in range(FT):
                    if ffn:
                        act.wait_ge(up_done, i * FT + (f + 1))
                        ge(act, down_done, i * FT + (f - 3))
                        s.activation(hidden[:, f % 4, :], up_ps[f % 2][:, 0:2 * T], ACT.Relu).then_inc(hidden_ready, 1)
                    if tail and f in steps:
                        steps[f][0](*steps[f][1:])
                if ffn:
                    act.wait_ge(low_o_ps, i + 1)
                    for k in range(2):
                        s.activation(low_o[:, k * T:(k + 1) * T], low_ps[:, k * T:(k + 1) * T], ACT.Copy,
                                     scale=gain_now[:, k:k + 1]).then_inc(low_o_ready, 1)

            body(0, True, False)
            body(1, True, True)
            with act.Fori(2, NP) as i:
                body(i, True, True)
            body(NP, False, True)

        @block.tensor
        def _(pe):
            t = nc.tensor

            def transposes(dst, src, width=128):
                for n in range(4):
                    last = t.transpose(dst[:, n * 128:(n + 1) * 128], src(n), ident[:, :])
                return last

            def tile(n):
                return slice(n * 128, (n + 1) * 128)

            pe.wait_ge(consts_ready, 10)
            pe.wait_ge(common_in, 16 * 7)
            for n, (kind, j) in enumerate(jobs):
                b = banks[n % 8]
                if n >= 8:
                    pe.wait_ge((ev_dve, ev_act)[n % 2], (n - 8) // 2 + 1)
                if kind in ("cwib", "cwob"):
                    st = st_cwib if kind == "cwib" else st_cwob
                    last = transposes(b[0:R, :], lambda m: st[:, 4 * j + m, :])
                elif kind == "wi":
                    if j % 8 == 0:
                        pe.wait_ge(wi_in[j // 8], 16)
                    if j == 0:
                        pe.wait_ge(ev_dve, 3)
                        pe.wait_ge(ev_act, 2)
                    for m in range(KT):
                        at = (j % 8) * D
                        t.matmul(b[:, tile(m)], st_w[:, at + m * 128:at + (m + 1) * 128], ident[:, :], start=True, stop=False)
                        last = t.matmul(b[:, tile(m)], st_cwia[:, tile(m)], cwibT[j // 4][:, tile(j % 4)], start=False, stop=True)
                elif kind == "ewia":
                    pe.wait_ge(corr_in, 16 * CORR)
                    last = transposes(b, lambda m: st_ewia[:, tile(m)])
                elif kind == "lb1":
                    pe.wait_ge(set_ready, 3)
                    last = t.matmul(b[:, 0:B], st_lb1, lang_hot, start=True, stop=True)
                elif kind == "ewoa":
                    last = transposes(b, lambda m: st_ewoa[:, tile(4 * j + m)])
                elif kind == "ewob":
                    last = transposes(b, lambda m: st_ewob[:, m].rearrange("p e r -> p (e r)"))
                elif kind == "ewib":
                    if j == 0:
                        pe.wait_ge(ewib_in, 16 * FT)
                    last = transposes(b, lambda m: st_ewib[:, 4 * j + m].rearrange("p e r -> p (e r)"))
                else:
                    dt, j = j
                    if j == 0 and dt % 2 == 0:
                        pe.wait_ge(wo_in[dt // 2], 16)
                    for m in range(4):
                        at = (dt % 2) * F + (4 * j + m) * 128
                        t.matmul(b[:, tile(m)], st_w[:, at:at + 128], ident[:, :], start=True, stop=False)
                        last = t.matmul(b[:, tile(m)], st_cwoa[j][:, tile(m)], cwobT[:, tile(dt)], start=False, stop=True)
                last.then_inc(pe_set, 1)
            pe.wait_ge(ev_dve, halves[0])
            pe.wait_ge(ev_act, halves[1])

            def body(i, ffn, tail):
                c = i - 1

                def x2_T(k):
                    n = c * 2 + k
                    pe.wait_ge(x2_ready, n + 1)
                    ge(pe, xT_ready, c * 4 + k)
                    transposes(tr_ps, lambda m: x2[:, k, tile(m)]).then_inc(x2T_ps, 1)

                def att_in(k):
                    n = c * 2 + k
                    pe.wait_ge(xT_ready, c * 4 + (k + 1))
                    if k == 0:
                        ge(pe, h_ready, n)
                    else:
                        pe.wait_ge(att_ready, n)
                    for m in range(KT):
                        last = t.matmul(mid_ps[:, 0:T], aw1[:, m, :], xT[:, k, m, :], start=(m == 0), stop=(m == KT - 1))
                    last.then_inc(att_ps, 1)

                def scores(k):
                    n = c * 2 + k
                    pe.wait_ge(att_ready, n + 1 if k else n + 2)
                    if k:
                        pe.wait_ge(masked_ready, n)
                    t.matmul(mid_ps[:, 0:T], vneg[:, :], att[:, k, :], start=True, stop=True).then_inc(score_ps, 1)

                def probs_T(k):
                    n = c * 2 + k
                    pe.wait_ge(probs_ready, n + 1)
                    if k:
                        pe.wait_ge(probsT_ready, n)
                    else:
                        pe.wait_ge(masked_ready, n + 2)
                    t.transpose(mid_ps[:, 0:T], probs[:, k, :], ident[:, :]).then_inc(probsT_ps, 1)

                def pooled(k):
                    n = c * 2 + k
                    pe.wait_ge(probsT_ready, n + 1)
                    if k:
                        pe.wait_ge(x3_ready, n)
                    else:
                        ge(pe, adapt_read, n)
                    t.matmul(wide_ps[:, :], probsT[:, k, :], x2[:, k, :], start=True, stop=True).then_inc(pooled_ps, 1)

                def x3_T(k):
                    n = c * 2 + k
                    pe.wait_ge(x3_ready, n + 1)
                    pe.wait_ge(xT_ready, c * 4 + (k + 2))
                    transposes(tr_ps, lambda m: x2[:, k, tile(m)]).then_inc(x3T_ps, 1)

                def adapter_in(k):
                    n = c * 2 + k
                    pe.wait_ge(xT_ready, c * 4 + (k + 3))
                    pe.wait_ge(lang_in[k], c * 80 + 80)
                    if k:
                        pe.wait_ge(h_ready, n)
                    else:
                        pe.wait_ge(probsT_ready, n + 2)
                    for m in range(KT):
                        last = t.matmul(mid_ps[:, 0:T], lw1[:, k, m, :], xT[:, k, m, :], start=(m == 0), stop=(m == KT - 1))
                    last.then_inc(h_ps, 1)

                def adapter_out(k):
                    n = c * 2 + k
                    pe.wait_ge(h_ready, n + 1)
                    if k:
                        pe.wait_ge(adapt_read, n)
                    else:
                        pe.wait_ge(x3_ready, n + 2)
                    t.matmul(wide_ps[:, :], hA[:, k, :], lw2[:, k, :], start=True, stop=False)
                    t.matmul(wide_ps[:, :], ones_row[:, :], lb2_row[:, k, :], start=False, stop=True).then_inc(adapt_ps, 1)

                steps = [(x2_T, 0), (x2_T, 1), (att_in, 0), (att_in, 1), (scores, 0), (scores, 1), (probs_T, 0), (probs_T, 1),
                         (pooled, 0), (pooled, 1), (x3_T, 0), (x3_T, 1), (adapter_in, 0), (adapter_in, 1),
                         (adapter_out, 0), (adapter_out, 1)]

                def up(f):
                    b = up_ps[f % 2]
                    if f >= 2:
                        pe.wait_ge(hidden_ready, i * FT + (f - 1))
                    for m in range(KT):
                        t.matmul(b[:, 0:2 * T], wiT[:, m, tile(f)], x1T[:, m, :], start=(m == 0), stop=False)
                    if f == 0:
                        pe.wait_ge(low_i_ready, i * 2 + 2)
                    t.matmul(b[:, 0:2 * T], ewibT[:, tile(f)], low_i[:, :], start=False, stop=True).then_inc(up_done, 1)

                def down(f):
                    pe.wait_ge(hidden_ready, i * FT + (f + 1))
                    if f == 0:
                        ge(pe, x2_ready, i * 2)
                    h = hidden[:, f % 4, :]
                    low = t.matmul(low_ps[:, 0:2 * T], ewoaT[:, f, :], h, start=(f == 0), stop=(f == FT - 1))
                    if f == FT - 1:
                        low.then_inc(low_o_ps, 1)
                    for k in range(2):
                        last = t.matmul(down_ps[k][:, :], h[:, k * T:(k + 1) * T], woT[:, f, :], start=(f == 0), stop=False)
                    last.then_inc(down_done, 1)

                if ffn:
                    ge(pe, hidden_ready, i * FT)
                    for k in range(2):
                        pe.wait_ge(x1_ready, i * 2 + (k + 1))
                        transposes(up_ps[k], lambda m: x1[:, k, tile(m)]).then_inc(x1T_ps, 1)
                    pe.wait_ge(x1T_ready, i * 2 + 2)
                    ge(pe, low_o_ready, i * 2)
                    for m in range(KT):
                        last = t.matmul(low_ps[:, 0:2 * T], ewiaT[:, m, :], x1T[:, m, :], start=(m == 0), stop=(m == KT - 1))
                    last.then_inc(low_i_ps, 1)
                for f in range(FT):
                    if ffn:
                        up(f)
                        if f:
                            down(f - 1)
                    if tail:
                        steps[f][0](steps[f][1])
                if ffn:
                    down(FT - 1)
                    pe.wait_ge(low_o_ready, i * 2 + 2)
                    for k in range(2):
                        t.matmul(down_ps[k][:, :], low_o[:, k * T:(k + 1) * T], ewobT[:, :], start=False, stop=True).then_inc(ffn_done, 1)

            body(0, True, False)
            body(1, True, True)
            with pe.Fori(2, NP) as i:
                body(i, True, True)
            body(NP, False, True)


_INS = ['x', 'fside_Bx2_0', 'condB_angle', 'itok_B_0_7', 'itok_B_0_2', 'itok_B_0_8', 'L1_cond_wi', 'L1_cond_wo',
        'L1_cond_common_wi_a', 'L1_cond_common_wi_b', 'L1_cond_common_wo_a', 'L1_cond_common_wo_b',
        'L1_cond_experts_wi_a', 'L1_cond_experts_wi_b', 'L1_cond_experts_wo_a', 'L1_cond_experts_wo_b',
        'L2_cond_W1', 'L2_cond_b1', 'L2_cond_v', 'L3_cond_W1', 'L3_cond_b1', 'L3_cond_W2', 'L3_cond_b2',
        'L3_cond_gamma', 'L3_cond_beta']


def kernel(**inputs):
    import concourse.bacc as _bacc
    from concourse.bass_utils import run_bass_kernel_spmd as _run

    nc = _bacc.Bacc("TRN2", target_bir_lowering=False, num_devices=1)
    arrays, args = {}, []
    for name in _INS:
        a = np.ascontiguousarray(inputs[name])
        arrays[f"in_{name}_dram"] = a
        args.append(nc.dram_tensor(f"in_{name}_dram", a.shape, mybir.dt.from_np(a.dtype), kind="ExternalInput").ap())
    shape = inputs["x"].shape
    out = nc.dram_tensor("out_0_dram", tuple(shape), fp32, kind="ExternalOutput").ap()
    build(nc, *args, out)
    return _run(nc, [arrays], core_ids=[0]).results[0]["out_0_dram"]
```

```python
import numpy as np
import concourse.bass as bass
from concourse import mybir
from contextlib import ExitStack

T = 128
D = 512
F = 2048
KT = D // 128
FT = F // 128
E, R = 8, 16
NL = 10
A = 128
ALPHA = 2.0
EPS = 1e-5
BIG = 1e30

ACT_UP = 16.0
W_UP = 64.0
PS_DOWN = 1.0 / (ACT_UP * W_UP)
RING = 8
LAG = 4
PARTS = ((0, 0), (0, 1), (1, 0))

RY = (T - 1) / D
RX = (D - 1) / T
GP = 8
NG = 8
Q = GP * GP
HALF = Q // 2
TAPS = 3
SW, SS = 128, 64
NS = D // SS + 2
PADY = 5
ROWS = T + 2 * PADY
SLOT = NS * ROWS * SW
RUN = 4 * SW + 44
OFF_MAX = 2 * SW + 39
XLO, XHI = -float(SS), float(D)
YLO, YHI = -float(PADY), float(T)

ALU = mybir.AluOpType
ACT = mybir.ActivationFunctionType
AX = mybir.AxisListType
fp32, i32, f16, bf16 = mybir.dt.float32, mybir.dt.int32, mybir.dt.float16, mybir.dt.bfloat16


def build(nc, x, fside, angle, tok_expert, tok_prompt, tok_lang, wi, wo, cwi_a, cwi_b, cwo_a, cwo_b,
          ewi_a, ewi_b, ewo_a, ewo_b, aW1, ab1, av, lW1, lb1, lW2, lb2, lgamma, lbeta, out):
    B = x.shape[0]
    NP = B // 2
    ctx = ExitStack()
    with ctx:
        def sb(name, shape, dt=fp32):
            return ctx.enter_context(nc.sbuf_tensor(name, shape, dt))

        def sem(name):
            return ctx.enter_context(nc.semaphore(name))

        def ap(handle, offset, dims):
            return bass.AP(handle.tensor, offset, dims)

        strips = nc.dram_tensor("strips", (2, NS, ROWS, SW), fp32).ap()
        frac_dram = nc.dram_tensor("frac_dram", (B, 2 * Q), fp32).ap()
        offs_dram = nc.dram_tensor("offs_dram", (B, Q), i32).ap()

        wiT = sb("wiT", [128, 2, KT, F], f16)
        woT = sb("woT", [128, 2, FT, D], f16)
        ewiaT = sb("ewiaT", [128, 2, KT, E * R], f16)
        ewibT = sb("ewibT", [E * R, 2, F], f16)
        ewoaT = sb("ewoaT", [128, 2, FT, E * R], f16)
        ewobT = sb("ewobT", [E * R, 2, D], f16)
        aw1 = sb("aw1", [128, KT, A])
        ab1c = sb("ab1c", [A, 1])
        avc = sb("avc", [A, 1])
        vneg = sb("vneg", [A, T])
        lb2_parts = sb("lb2_parts", [96, D], bf16)
        ident = sb("ident", [128, 128])
        prompt_mask = sb("prompt_mask", [T, 3, T])
        is_prefix = sb("is_prefix", [128, B])
        is_postfix = sb("is_postfix", [128, B])
        inv_count = sb("inv_count", [128, B])
        expert_gain = sb("expert_gain", [128, B])
        lb1_img = sb("lb1_img", [A, B])
        lang_hot = sb("lang_hot", [128, B])
        lang_row = sb("lang_row", [1, B], i32)
        gather_at = sb("gather_at", [128, B, NG], i32)
        gather_now = sb("gather_now", [128, 2, NG], i32)
        frac_group = sb("frac_group", [128, B, 2, NG])
        N_WIN, N_PROD, N_TAPS = NG * RUN, TAPS * TAPS * D // 2, 2 * TAPS * D
        work = sb("work", [128, N_WIN + N_PROD + N_TAPS])
        win = work[:, 0:N_WIN].rearrange("p (g r) -> p g r", g=NG)
        prod = work[:, N_WIN:N_WIN + N_PROD]
        taps = work[:, N_WIN + N_PROD:]
        warp_sum = sb("warp_sum", [128, D])
        warped = sb("warped", [T, D])
        frac_now = sb("frac_now", [128, 2, NG])
        frac_pix = sb("frac_pix", [128, 2, 2 * Q])
        offs = sb("offs", [1, 2, Q], i32)
        offs_now = sb("offs_now", [1, Q], i32)
        xs = sb("xs", [T, 2, 2, D])
        x1T = sb("x1T", [128, 2, KT, 2 * T], f16)
        hidden = sb("hidden", [128, 4, 2 * T])
        hidden_parts = sb("hidden_parts", [128, 2, RING, 2 * T], f16)
        low_i = sb("low_i", [E * R, 2, 2 * T], f16)
        low_o = sb("low_o", [E * R, 2, 2 * T], f16)
        x2 = sb("x2", [T, 2, 2, D])
        xT = sb("xT", [128, 2, KT, T])
        att = sb("att", [A, 2, T])
        masked = sb("masked", [T, 2, T])
        probs = sb("probs", [T, 2, T])
        probsT = sb("probsT", [T, 2, T])
        hA = att
        neg_max = sb("neg_max", [T, 2])
        row_sum = sb("row_sum", [T, 2])
        pool_scale = sb("pool_scale", [T, 2])
        stats = sb("stats", [T, 2, 6])
        mv = sb("mv", [T, 2, 2])
        rstd = sb("rstd", [T, 2])
        gain_now = sb("gain_now", [128, 2])
        lb1_now = sb("lb1_now", [A, 2])
        lang_now = sb("lang_now", [96, 2, T], bf16)
        var_eps = sb("var_eps", [T, 2])
        newton = sb("newton", [T, 2])
        guess_i = sb("guess_i", [T, 2], i32)
        y = sb("y", [T, 2, D])
        lw1 = sb("lw1", [128, 2, KT, A])
        lw2 = sb("lw2", [A, 2, D])
        gamma_b = sb("gamma_b", [T, 2, D])
        beta_b = sb("beta_b", [T, 2, D])
        NA = B + 1
        ang = sb("ang", [128, NA])
        sincos = sb("sincos", [128, 2, NA])
        trig = sb("trig", [128, 2, NA])
        part_i = sb("part_i", [128, 3], i32)
        part = sb("part", [128, 5])
        group_i = sb("group_i", [128, 2, NG], i32)
        group = sb("group", [128, 2, NG])
        pixel_i = sb("pixel_i", [128, 2, Q], i32)
        shift = masked[:, 0, :].rearrange("p (b c) -> p b c", c=2)[:, 0:B, :]
        ids_i, ids = (t[:, :, :].rearrange("p k t -> p (k t)")[:, 0:3 * B].rearrange("p (n b) -> p n b", n=3)
                      for t in (probs, probsT))
        ids_i = ids_i.bitcast(i32)

        banks = [ctx.enter_context(nc.psum_tensor(f"bank{n}", [128, 512], fp32)) for n in range(8)]
        up_ps = [banks[0], banks[1]]
        down_ps = [banks[2], banks[3]]
        low_ps = banks[4]
        tr_ps = banks[5]
        mid_ps = banks[6]
        wide_ps = banks[7]

        in_loaded = sem("in_loaded")
        wi_in = [sem("wi_in0"), sem("wi_in1")]
        wo_in = [sem("wo_in0"), sem("wo_in1")]
        common_in = sem("common_in")
        corr_in = sem("corr_in")
        ewib_in = sem("ewib_in")
        zero_ready = sem("zero_ready")
        strips_zero = sem("strips_zero")
        consts_ready = sem("consts_ready")
        pool_chain = sem("pool_chain")
        set_chain = sem("set_chain")
        set_ready = sem("set_ready")
        sin_ready = sem("sin_ready")
        pe_set = sem("pe_set")
        ev_act = sem("ev_act")
        ev_dve = sem("ev_dve")
        lb2_zero = sem("lb2_zero")
        lb2_in = sem("lb2_in")
        pix_out = sem("pix_out")
        strips_in = [sem("strips_in0"), sem("strips_in1")]
        x_in = [sem("x_in0"), sem("x_in1")]
        pix_in = [sem("pix_in0"), sem("pix_in1")]
        lang_in = [sem("lang_in0"), sem("lang_in1")]
        stored = [sem("stored0"), sem("stored1")]
        gathered = [sem("gathered0"), sem("gathered1")]
        taps_ready = sem("taps_ready")
        taps_used = sem("taps_used")
        win_used = sem("win_used")
        x1_ready = sem("x1_ready")
        x1T_ps = sem("x1T_ps")
        x1T_hi = sem("x1T_hi")
        x1T_ready = sem("x1T_ready")
        low_i_ps = sem("low_i_ps")
        low_i_hi = sem("low_i_hi")
        low_i_ready = sem("low_i_ready")
        up_done = sem("up_done")
        hidden_hi = sem("hidden_hi")
        hidden_ready = sem("hidden_ready")
        down_done = sem("down_done")
        low_o_ps = sem("low_o_ps")
        low_o_hi = sem("low_o_hi")
        low_o_ready = sem("low_o_ready")
        ffn_done = sem("ffn_done")
        x2_ready = sem("x2_ready")
        x2T_ps = sem("x2T_ps")
        xT_ready = sem("xT_ready")
        att_ps = sem("att_ps")
        att_ready = sem("att_ready")
        score_ps = sem("score_ps")
        masked_ready = sem("masked_ready")
        probs_ready = sem("probs_ready")
        probsT_ps = sem("probsT_ps")
        probsT_ready = sem("probsT_ready")
        pooled_ps = sem("pooled_ps")
        x3_ready = sem("x3_ready")
        x3T_ps = sem("x3T_ps")
        h_ps = sem("h_ps")
        h_ready = sem("h_ready")
        adapt_ps = sem("adapt_ps")
        adapt_read = sem("adapt_read")
        y_ready = sem("y_ready")
        dve_chain = sem("dve_chain")
        act_chain = sem("act_chain")
        lang_ready = sem("lang_ready")

        def ge(eng, s, n):
            if not isinstance(n, int) or n > 0:
                eng.wait_ge(s, n)

        def there(i, first, end=None):
            return not isinstance(i, int) or first <= i < NP + first

        def col(table, n):
            return table[:, bass.ds(n, 1)]

        st_w = work[:, 0:4096]
        st_ewib = work[:, 4096:6144].rearrange("p (t e r) -> p t e r", e=E, r=R)
        st_ewoa = work[:, 6144:8192]
        st_ewia = work[:, 8192:8704]
        st_ewob = work[:, 8704:9216].rearrange("p (t e r) -> p t e r", e=E, r=R)
        st_cwib = work[:, 9216:9472].rearrange("p (t r) -> p t r", r=R)
        st_cwob = work[:, 9472:9536].rearrange("p (t r) -> p t r", r=R)
        st_lb1 = y[0:NL, 0, 0:A]
        st_cwia = xs[0:R, 0, 0, :]
        cwobT = xs[0:R, 0, 1, :]
        hidden_flat = hidden[:, :, :].rearrange("p s t -> p (s t)")
        cwibT = [hidden_flat[0:R, 0:512], hidden_flat[0:R, 512:1024], x2[0:R, 0, 0, :], x2[0:R, 0, 1, :]]
        st_cwoa = [gamma_b[0:R, 0, :], gamma_b[0:R, 1, :], beta_b[0:R, 0, :], beta_b[0:R, 1, :]]

        jobs = ([("cwib", t) for t in range(FT // 4)] + [("cwob", 0)] + [("wi", t) for t in range(FT)]
                + [("ewia", 0), ("lb1", 0)] + [("ewoa", t) for t in range(4)] + [("ewob", 0)]
                + [("ewib", t) for t in range(4)]
                + [("wo", (dt, t)) for dt in range(KT) for t in range(4)])
        at_job = {job: n for n, job in enumerate(jobs)}
        plain = ("cwib", "cwob", "lb1")
        splits = [sum(kind not in plain for kind, _ in jobs[:n]) for n in range(len(jobs) + 1)]

        def job_ends(kind, t):
            b = banks[at_job[(kind, t)] % 8]
            tiles = b[:, :].rearrange("p (a b) -> p a b", b=128)
            if kind == "cwib":
                return [cwibT[t]], b[0:R, :], ALPHA
            if kind == "cwob":
                return [cwobT], b[0:R, :], ALPHA
            if kind == "lb1":
                return [lb1_img[:, :]], b[:, 0:B], 1.0
            if kind == "wi":
                return [wiT[:, s, :, t * 128:(t + 1) * 128] for s in range(2)], tiles, W_UP
            if kind == "ewia":
                return [ewiaT[:, s, :, :] for s in range(2)], tiles, W_UP
            if kind == "ewib":
                return [ewibT[:, s, t * 512:(t + 1) * 512] for s in range(2)], b[:, :], W_UP
            if kind == "ewoa":
                return [ewoaT[:, s, 4 * t:4 * t + 4, :] for s in range(2)], tiles, W_UP
            if kind == "ewob":
                return [ewobT[:, s, :] for s in range(2)], b[:, :], W_UP
            dt, t = t
            return [woT[:, s, 4 * t:4 * t + 4, dt * 128:(dt + 1) * 128] for s in range(2)], tiles, W_UP

        lb2_stage, lb2_rest = (lw2[0:96, n, :] for n in range(2))
        ZEROS = 2048
        zeros = hidden_parts[:, :, :, :].rearrange("p s r t -> p (s r t)").bitcast(fp32)[:, 0:ZEROS]
        CORR = 2 + KT + 4
        pixel_f = xT[:, :, :, :].rearrange("p k t c -> p (k t c)")[0:B, :]
        pix_frac = pixel_f[:, 6 * Q:8 * Q]
        pix_offs = pixel_f[:, 8 * Q:9 * Q].bitcast(i32)

        block = ctx.enter_context(nc.Block())

        @block.sync
        def _(sp):
            small = 0
            sp.dma_start(ang[:, 0:B], angle.unsqueeze(0).broadcast_to([128, B])).then_inc(in_loaded, 16)
            sp.dma_start(masked[:, 0, 0:2 * B],
                         fside.rearrange("b c -> (b c)").unsqueeze(0).broadcast_to([128, 2 * B])).then_inc(in_loaded, 16)
            for n, tok in enumerate((tok_expert, tok_prompt, tok_lang)):
                sp.dma_start(ids_i[:, n, :], tok.unsqueeze(0).broadcast_to([128, B])).then_inc(in_loaded, 16)
            sp.dma_start(lang_row[:, :], tok_lang.unsqueeze(0)).then_inc(in_loaded, 16)
            sp.wait_ge(set_ready, 1)
            sp.dma_start(ang[0:B, B:B + 1], angle.unsqueeze(1)).then_inc(in_loaded, 16)
            sp.dma_start(st_cwib, cwi_b.rearrange("(t p) r -> p t r", p=128)).then_inc(common_in, 16)
            sp.dma_start(st_cwia, cwi_a).then_inc(common_in, 16)
            sp.dma_start(st_cwob, cwo_b.rearrange("(t p) r -> p t r", p=128)).then_inc(common_in, 16)
            for t in range(4):
                sp.dma_start(st_cwoa[t], cwo_a[:, t * 512:(t + 1) * 512]).then_inc(common_in, 16)
            sp.dma_start(st_w.rearrange("p (t d) -> p t d", t=8),
                         wi[0:1024, :].rearrange("(t p) d -> p t d", p=128)).then_inc(wi_in[0], 16)
            sp.dma_start(st_ewia, ewi_a.rearrange("e r d -> (e r) d")).then_inc(corr_in, 16)
            sp.dma_start(st_ewoa, ewo_a.rearrange("e r f -> (e r) f")).then_inc(corr_in, 16)
            for t in range(KT):
                sp.dma_start(st_ewob[:, t], ewo_b[:, t * 128:(t + 1) * 128, :].rearrange("e p r -> p e r")).then_inc(corr_in, 16)
            sp.dma_start(aw1[:, :, :], aW1.rearrange("(t p) a -> p t a", p=128)).then_inc(corr_in, 16)
            sp.dma_start(ab1c[:, :], ab1.unsqueeze(1)).then_inc(corr_in, 16)
            sp.dma_start(avc[:, :], av.unsqueeze(1)).then_inc(corr_in, 16)
            sp.dma_start(st_lb1, lb1).then_inc(corr_in, 16)
            sp.wait_ge(lb2_zero, 1)
            for n in range(3):
                sp.dma_start(lb2_stage[n * 32:n * 32 + NL, :], lb2).then_inc(lb2_in, 16)
            sp.wait_ge(zero_ready, 1)
            per = 2 * SLOT // 128
            flat = strips.rearrange("k s r c -> (k s r c)").rearrange("(p n) -> p n", p=128)
            cuts = list(range(0, per, ZEROS)) + [per]
            for a, b in zip(cuts[:-1], cuts[1:]):
                sp.dma_start(flat[:, a:b], zeros[:, 0:b - a]).then_inc(strips_zero, 16)
            sp.wait_ge(pe_set, at_job[("wi", 7)] + 1)
            sp.dma_start(st_w.rearrange("p (t d) -> p t d", t=8),
                         wi[1024:2048, :].rearrange("(t p) d -> p t d", p=128)).then_inc(wi_in[1], 16)
            sp.wait_ge(strips_zero, 16 * (len(cuts) - 1))

            def load_strips(a, k):
                ge(sp, gathered[k], 16 * NG * a)
                img = x[bass.ds(a * 2 + k, 1)].squeeze(0)
                src = bass.AP(img.tensor, img.offset, [[SS, NS - 3], [D, T], [1, SW]])
                sp.dma_start(strips[k, 1:NS - 2, PADY:PADY + T, :], src).then_inc(strips_in[k], 16)
                sp.dma_start(strips[k, 0, PADY:PADY + T, SS:SW], img[:, 0:SS]).then_inc(strips_in[k], 16)
                sp.dma_start(strips[k, NS - 2, PADY:PADY + T, 0:SS], img[:, D - SS:D]).then_inc(strips_in[k], 16)

            def load_pix(a, k):
                ge(sp, win_used, a * 2 + (k - 1))
                sp.dma_start(frac_pix[:, k, :], frac_dram[bass.ds(a * 2 + k, 1), :].broadcast_to([128, 2 * Q])).then_inc(pix_in[k], 16)
                sp.dma_start(offs[:, k, :], offs_dram[bass.ds(a * 2 + k, 1), :]).then_inc(pix_in[k], 16)

            def load_x(a, k, q):
                if isinstance(a, int) and a < 2:
                    ge(sp, x1_ready, a * 2 + (k - 1))
                else:
                    sp.wait_ge(x2_ready, a * 2 + (k - 3))
                sp.dma_start(xs[:, q, k, :], x[bass.ds(a * 2 + k, 1)].squeeze(0)).then_inc(x_in[k], 16)

            def load_lang(c, k):
                ge(sp, y_ready, c * 2 + (k - 1))
                lang = sp.value_load(lang_row[0:1, bass.ds(c * 2 + k, 1)], min_val=0, max_val=NL - 1)
                pick = bass.ds(lang, 1)
                sp.dma_start(lw1[:, k, :, :], lW1[pick].squeeze(0).rearrange("(t p) a -> p t a", p=128)).then_inc(lang_in[k], 16)
                sp.dma_start(lw2[:, k, :], lW2[pick].squeeze(0)).then_inc(lang_in[k], 16)
                sp.dma_start(gamma_b[:, k, :], lgamma[pick, :].broadcast_to([T, D])).then_inc(lang_in[k], 16)
                sp.dma_start(beta_b[:, k, :], lbeta[pick, :].broadcast_to([T, D])).then_inc(lang_in[k], 16)

            def store(c, k):
                sp.wait_ge(y_ready, c * 2 + (k + 1))
                sp.dma_start(out[bass.ds(c * 2 + k, 1)].squeeze(0), y[:, k, :]).then_inc(stored[k], 16)

            for k in range(2):
                load_strips(0, k)
            for r, last in enumerate((("wi", FT - 1), ("wo", (1, 3)))):
                sp.wait_ge(pe_set, at_job[last] + 1)
                sp.dma_start(st_w.rearrange("p (t f) -> p t f", t=2),
                             wo[r * 256:(r + 1) * 256, :].rearrange("(t p) f -> p t f", p=128)).then_inc(wo_in[r], 16)
            sp.wait_ge(set_ready, 3)
            sp.dma_start(frac_dram, pix_frac).then_inc(pix_out, 16)
            sp.dma_start(offs_dram, pix_offs).then_inc(pix_out, 16)
            sp.wait_ge(pix_out, 32)
            sp.wait_ge(pe_set, len(jobs))
            for k in range(2):
                load_pix(0, k)

            def body(i, q):
                for k in range(2):
                    if there(i, -1):
                        load_x(i + 1, k, 1 - q)
                for k in range(2):
                    if there(i, 2):
                        store(i - 2, k)
                for k in range(2):
                    if there(i, 1):
                        load_lang(i - 1, k)
                for k in range(2):
                    if there(i, -2):
                        load_strips(i + 2, k)
                        load_pix(i + 2, k)

            for i in range(-1, 4):
                body(i, i % 2)
            with sp.Fori(2, NP // 2 - 1) as i:
                for q in range(2):
                    body(i * 2 + q, q)
            for i in range(NP - 2, NP + 2):
                body(i, i % 2)
            for k in range(2):
                sp.wait_ge(stored[k], 16 * NP)

        @block.gpsimd
        def _(pool):
            g = nc.gpsimd
            g.memset(zeros, 0.0).then_inc(zero_ready, 1)
            g.memset(ident[:, :], 0.0).then_inc(pool_chain, 1)
            g.memset(prompt_mask[:, :, :], 0.0).then_inc(pool_chain, 1)
            g.memset(lb2_stage, 0.0).then_inc(lb2_zero, 1)
            g.iota(part_i[:, 0:1], pattern=[[0, 1]], base=0, channel_multiplier=1).then_inc(consts_ready, 1)
            g.iota(group_i[:, 0, :], pattern=[[32 * GP, 2], [0, 4]], base=-D // 2, channel_multiplier=0).then_inc(consts_ready, 1)
            g.iota(group_i[:, 1, :], pattern=[[0, 2], [GP, 4]], base=-T // 2, channel_multiplier=1).then_inc(consts_ready, 1)
            g.iota(pixel_i[:, 0, :], pattern=[[0, GP], [1, GP]], base=0, channel_multiplier=0).then_inc(consts_ready, 1)
            g.iota(pixel_i[:, 1, :], pattern=[[1, GP], [0, GP]], base=0, channel_multiplier=0).then_inc(consts_ready, 1)
            pool.wait_ge(pool_chain, 2)
            g.affine_select(out=ident[:, :], in_=ident[:, :], compare_op=ALU.not_equal, fill=1.0, base=0,
                            pattern=[[-1, 128]], channel_multiplier=1).then_inc(consts_ready, 1)
            for n, (op, sign) in enumerate(((ALU.is_ge, 1), (ALU.is_ge, -1), (ALU.not_equal, 1))):
                g.affine_select(out=prompt_mask[:, n, :], in_=prompt_mask[:, n, :], compare_op=op, fill=BIG, base=0,
                                pattern=[[-sign, T]], channel_multiplier=sign).then_inc(consts_ready, 1)
            for t in range(FT):
                pool.dma_start(st_ewib[:, t], ewi_b[:, t * 128:(t + 1) * 128, :].rearrange("e p r -> p e r")).then_inc(ewib_in, 16)
            pool.wait_ge(set_ready, 3)
            pool.wait_ge(pe_set, len(jobs))
            flat = bass.AP(strips.tensor, 0, [[1, 2 * SLOT], [1, 1]])
            tap = taps.rearrange("p (x t m) -> p x t m", x=2, t=TAPS)

            def weights(a, k, h, links):
                n = a * 2 + k
                m = slice(h * D // 2, (h + 1) * D // 2)
                ge(pool, taps_used, n * 2 + (h - 1))
                for ax in range(2):
                    fg = frac_now[:, ax, :]
                    fp = frac_pix[:, k, ax * Q + h * HALF:ax * Q + (h + 1) * HALF].rearrange("p (j i) -> p j i", i=GP)
                    g.tensor_tensor(tap[:, ax, 1, m].rearrange("p (j g i) -> p j g i", g=NG, i=GP),
                                    fg.unsqueeze(1).unsqueeze(3).broadcast_to([128, GP // 2, NG, GP]),
                                    fp.unsqueeze(2).broadcast_to([128, GP // 2, NG, GP]),
                                    ALU.add).then_inc(pool_chain, 1)
                pool.wait_ge(pool_chain, links + 2)
                before, mid, after = (tap[:, :, t, m] for t in range(TAPS))
                g.tensor_scalar(before, mid, 0.0, -1.0, ALU.min, ALU.mult).then_inc(pool_chain, 1)
                g.tensor_scalar(after, mid, 0.0, None, ALU.max).then_inc(pool_chain, 1)
                pool.wait_ge(pool_chain, links + 4)
                g.tensor_tensor(mid, before, after, ALU.add).then_inc(pool_chain, 1)
                pool.wait_ge(pool_chain, links + 5)
                g.tensor_scalar(mid, mid, -1.0, 1.0, ALU.mult, ALU.add).then_inc(taps_ready, 1)

            def warp(a, k):
                n = a * 2 + k
                pool.sem_clear(pool_chain)
                pool.wait_ge(pix_in[k], a * 32 + 32)
                g.tensor_copy(frac_now[:, :, :], frac_group[:, bass.ds(n, 1), :, :].squeeze(1)).then_inc(pool_chain, 1)
                pool.wait_ge(pool_chain, 1)
                weights(a, k, 0, 1)
                pool.wait_ge(strips_in[k], a * 48 + 48)
                ge(pool, win_used, n)
                ge(pool, gathered[k], a * (16 * NG))
                g.tensor_copy(gather_now[:, k, :], gather_at[:, bass.ds(n, 1), :].squeeze(1)).then_inc(pool_chain, 1)
                pool.wait_ge(pool_chain, 7)
                for gi in range(NG):
                    at = gather_now[:, k, gi:gi + 1]
                    g.indirect_dma_start(out=win[:, gi, :], out_offset=None, in_=flat,
                                         in_offset=bass.IndirectOffsetOnAxis(at, 0)).then_inc(gathered[k], 16)
                weights(a, k, 1, 7)

            for k in range(2):
                warp(0, k)
            with pool.Fori(0, NP - 1) as i:
                for k in range(2):
                    warp(i + 1, k)

        @block.vector
        def _(dve):
            v = nc.vector
            chain = [0]

            def link(ins):
                chain[0] += 1
                ins.then_inc(set_chain, 1)
                dve.wait_ge(set_chain, chain[0])

            v.memset(ang[:, B:B + 1], 0.0).then_inc(set_ready, 1)
            dve.wait_ge(in_loaded, 16 * 7)
            dve.wait_ge(consts_ready, 9)
            PI = 3.1415925
            two_pi_hi, two_pi_lo = 6.28125, 2 * np.pi - 6.28125
            turns, r = trig[:, 1, :], trig[:, 0, :]
            turns_i = gather_at[:, :, :].rearrange("p b g -> p (b g)")[:, 0:NA]
            step = sincos[:, 0, :]
            link(v.tensor_scalar(turns_i, ang[:, :], float(1 / (2 * np.pi)), None, ALU.mult))
            link(v.tensor_copy(turns, turns_i))
            link(v.scalar_tensor_tensor(r, turns, -two_pi_hi, ang[:, :], ALU.mult, ALU.add))
            link(v.scalar_tensor_tensor(r, turns, -two_pi_lo, r, ALU.mult, ALU.add))
            link(v.tensor_scalar(step, r, PI, float(-2 * np.pi), ALU.is_gt, ALU.mult))
            link(v.tensor_tensor(r, r, step, ALU.add))
            link(v.tensor_scalar(step, r, -PI, float(2 * np.pi), ALU.is_lt, ALU.mult))
            link(v.tensor_tensor(r, r, step, ALU.add))
            link(v.tensor_scalar(trig[:, 1, :], r, float(np.pi / 2), None, ALU.add))
            link(v.tensor_scalar(step, trig[:, 1, :], PI, float(-2 * np.pi), ALU.is_gt, ALU.mult))
            link(v.tensor_tensor(trig[:, 1, :], trig[:, 1, :], step, ALU.add))
            v.tensor_scalar(trig[:, :, :], trig[:, :, :], PI, -PI, ALU.min, ALU.max).then_inc(set_ready, 1)
            link(v.tensor_scalar(part_i[:, 1:2], part_i[:, 0:1], 31, None, ALU.bitwise_and))
            link(v.tensor_scalar(part_i[:, 2:3], part_i[:, 0:1], 4, None, ALU.arith_shift_right))
            link(v.tensor_copy(part[:, 0:3], part_i[:, :]))
            link(v.tensor_scalar(part[:, 3:4], part[:, 0:1], float(2 - T), None, ALU.add))
            link(v.tensor_scalar(part[:, 4:5], part[:, 0:1], -1.0, 1.0, ALU.mult, ALU.add))
            link(v.tensor_copy(group[:, :, :], group_i[:, :, :]))
            first_column = stats[:, 0, 0:1]
            link(v.tensor_scalar(first_column, part[:, 1:2], float(GP), None, ALU.mult))
            link(v.tensor_scalar(group[:, 0, :], group[:, 0, :], first_column, None, ALU.add))
            link(v.tensor_scalar(group[:, 1, :], group[:, 1, :], part[:, 1:2], None, ALU.subtract))
            link(v.tensor_copy(ids[:, :, :], ids_i[:, :, :]))
            link(v.tensor_scalar(expert_gain[:, :], ids[:, 0, :], part[:, 2:3], ALPHA / W_UP, ALU.is_equal, ALU.mult))
            link(v.tensor_scalar(is_prefix[:, :], ids[:, 1, :], 0.0, None, ALU.is_equal))
            link(v.tensor_scalar(is_postfix[:, :], ids[:, 1, :], 1.0, None, ALU.is_equal))
            link(v.tensor_scalar(lang_hot[:, :], ids[:, 2, :], part[:, 1:2], None, ALU.is_equal))
            link(v.tensor_scalar(inv_count[:, :], is_prefix[:, :], part[:, 3:4], float(T - 1), ALU.mult, ALU.add))
            link(v.scalar_tensor_tensor(inv_count[:, :], is_postfix[:, :], part[:, 4:5], inv_count[:, :], ALU.mult, ALU.add))
            link(v.reciprocal(inv_count[:, :], inv_count[:, :]))
            for n in range(2):
                link(v.tensor_tensor(prompt_mask[:, n, :], prompt_mask[:, n, :], prompt_mask[:, 2, :], ALU.subtract))
            dve.wait_ge(sin_ready, 1)
            sin, cos = sincos[:, 0, :], sincos[:, 1, :]
            low = trig
            link(v.tensor_scalar(low[:, 0, :], sin, 0.0, None, ALU.max))
            link(v.tensor_scalar(low[:, 1, :], cos, 0.0, None, ALU.min))
            link(v.tensor_tensor(low[:, 0, :], low[:, 1, :], low[:, 0, :], ALU.subtract))
            link(v.tensor_scalar(ang[:, :], sin, 0.0, None, ALU.min))
            link(v.tensor_tensor(low[:, 1, :], low[:, 1, :], ang[:, :], ALU.add))
            link(v.tensor_scalar(low[:, :, :], low[:, :, :], float(GP - 1), None, ALU.mult))

            def floor(value, whole_i, whole, over):
                link(v.tensor_copy(whole_i, value))
                link(v.tensor_copy(whole, whole_i))
                link(v.tensor_tensor(over, whole, value, ALU.is_gt))
                link(v.tensor_tensor(whole, whole, over, ALU.subtract))

            xs_flat = xs[:, 1, :, :].rearrange("p k d -> p (k d)")
            x1T_flat = x1T[:, :, :, :].rearrange("p s k t -> p (s k t)").bitcast(fp32)
            M = B * NG
            shape = lambda t: t.rearrange("p (b g) -> p b g", g=NG)
            pos, other = xs_flat[:, 0:M], xs_flat[:, M:2 * M]
            whole, whole_i = x1T_flat[:, 0:M], x1T_flat[:, M:2 * M].bitcast(i32)
            at_f = y[:, 1, 0:M]
            for ax in range(2):
                on_x, on_y = (cos, sin) if ax == 0 else (sin, cos)
                wide = lambda t: t.unsqueeze(2).broadcast_to([128, B, NG])
                grp = lambda t: t.unsqueeze(1).broadcast_to([128, B, NG])
                link(v.tensor_tensor(shape(pos), wide(on_x[:, 0:B]), grp(group[:, 0, :]), ALU.mult))
                link(v.tensor_tensor(shape(other), wide(on_y[:, 0:B]), grp(group[:, 1, :]), ALU.mult))
                link(v.tensor_tensor(pos, pos, other, ALU.subtract if ax == 0 else ALU.add))
                link(v.tensor_tensor(ang[:, 0:B], shift[:, :, ax], low[:, ax, 0:B], ALU.add))
                link(v.tensor_tensor(shape(pos), shape(pos), wide(ang[:, 0:B]), ALU.add))
                rate, mid, lo, hi = (RY, (T - 1) / 2, YLO, YHI) if ax == 0 else (RX, (D - 1) / 2, XLO, XHI)
                link(v.tensor_scalar(pos, pos, rate, mid, ALU.mult, ALU.add))
                link(v.tensor_scalar(pos, pos, hi, lo, ALU.min, ALU.max))
                floor(pos, whole_i, whole, other)
                link(v.scalar_tensor_tensor(frac_group[:, :, ax, :], shape(pos), -1.0, shape(whole), ALU.add, ALU.subtract))
                if ax == 0:
                    link(v.tensor_scalar(at_f, whole, float(PADY), float(SW), ALU.add, ALU.mult))
                else:
                    strip_i, in_strip_i = pos.bitcast(i32), other.bitcast(i32)
                    link(v.tensor_scalar(whole_i, whole, float(SS), None, ALU.add))
                    link(v.tensor_scalar(strip_i, whole_i, 6, None, ALU.arith_shift_right))
                    link(v.tensor_scalar(in_strip_i, whole_i, SS - 1, None, ALU.bitwise_and))
                    link(v.tensor_copy(whole, strip_i))
                    link(v.scalar_tensor_tensor(at_f, whole, float(ROWS * SW), at_f, ALU.mult, ALU.add))
                    link(v.tensor_copy(whole, in_strip_i))
                    link(v.tensor_tensor(at_f, at_f, whole, ALU.add))
            odd = at_f.rearrange("p (a k g) -> p a k g", k=2, g=NG)[:, :, 1, :]
            link(v.tensor_scalar(odd, odd, float(SLOT), None, ALU.add))
            link(v.tensor_copy(gather_at[:, :, :].rearrange("p b g -> p (b g)"), at_f))

            pix = pixel_f
            own_sin, own_cos = sincos[0:B, 0, B:NA], sincos[0:B, 1, B:NA]
            row, column = pix[:, 0:Q], pix[:, Q:2 * Q]
            a1, a2, a3, a4 = (pix[:, (2 + n) * Q:(3 + n) * Q] for n in range(4))
            link(v.tensor_copy(pix[:, 0:2 * Q], pixel_i[0:B, :, :].rearrange("p a q -> p (a q)")))
            for ax in range(2):
                on_x, on_y = (own_cos, own_sin) if ax == 0 else (own_sin, own_cos)
                link(v.tensor_scalar(a1, column, on_x, None, ALU.mult))
                link(v.tensor_scalar(a2, row, on_y, None, ALU.mult))
                link(v.tensor_tensor(a1, a1, a2, ALU.subtract if ax == 0 else ALU.add))
                link(v.tensor_scalar(a1, a1, low[0:B, ax, B:NA], RY if ax == 0 else RX, ALU.subtract, ALU.mult))
                link(v.tensor_scalar(a1, a1, 0.0, None, ALU.max))
                floor(a1, pix_offs, a2, a3)
                link(v.tensor_tensor(pix_frac[:, ax * Q:(ax + 1) * Q], a1, a2, ALU.subtract))
                if ax == 0:
                    link(v.tensor_scalar(a4, a2, float(SW), None, ALU.mult))
                else:
                    link(v.tensor_tensor(a4, a4, a2, ALU.add))
            v.tensor_copy(pix_offs, a4).then_inc(set_ready, 1)
            dve.wait_ge(corr_in, 16 * CORR)
            link(v.tensor_scalar(vneg[:, :], ident[:, :], 0.0, avc[:, 0:1], ALU.mult, ALU.subtract))

            dve.wait_ge(lb2_in, 48)
            for n in range(2):
                link(v.tensor_copy(lb2_parts[:, :], lb2_stage))
                for m in range(n + 1, 3):
                    rows = slice(32 * m, 32 * m + 32)
                    link(v.tensor_tensor(lb2_stage[rows, :], lb2_stage[rows, :], lb2_parts[rows, :], ALU.subtract))
            v.tensor_copy(lb2_parts[:, :], lb2_stage).then_inc(set_ready, 1)

            for n, (kind, t) in enumerate(jobs):
                if kind not in plain:
                    (high, low), src, factor = job_ends(kind, t)
                    dve.wait_ge(ev_act, n + 1)
                    v.scalar_tensor_tensor(low, src, factor, high, ALU.mult, ALU.subtract).then_inc(ev_dve, 1)

            regs = [ctx.enter_context(v.register(f"window_offset{n}")) for n in range(8)]
            tap = taps.rearrange("p (x t j g i) -> p x t j g i", x=2, t=TAPS, g=NG, i=GP)
            tap_rows = taps.rearrange("p (x t m) -> p x t m", x=2, t=TAPS)
            prods = prod.rearrange("p (a b j g i) -> p a b j g i", a=TAPS, b=TAPS, g=NG, i=GP)
            by_column_tap = prod.rearrange("p (a b m) -> p a b m", a=TAPS, b=TAPS)

            def body(i, q):
                c, w = i - 1, i + 1
                ffn, tail, warp, finish = there(i, 0), there(i, 1), there(i, -1), there(i, 2)
                count = [0]

                def link(ins):
                    count[0] += 1
                    ins.then_inc(dve_chain, 1)
                    dve.wait_ge(dve_chain, count[0])

                def warp_half(k, h):
                    n = w * 2 + k
                    if h == 0:
                        dve.wait_ge(pix_in[k], w * 32 + 32)
                        dve.wait_ge(gathered[k], w * (16 * NG) + 16 * NG)
                        link(v.tensor_copy(offs_now[:, :], offs[:, k, :]))
                    v.load(regs, offs_now[0:1, h * HALF:h * HALF + 8])
                    dve.wait_ge(taps_ready, n * 2 + (h + 1))
                    for m in range(HALF):
                        j, row = m // GP, m % GP
                        if m and m % 8 == 0:
                            v.load(regs, offs_now[0:1, h * HALF + m:h * HALF + m + 8])
                        at = v.snap(regs[m % 8], min_val=0, max_val=OFF_MAX)
                        first = win[:, :, bass.ds(at, 1)]
                        seen = bass.AP(first.tensor, first.offset, [first.ap[0], [RUN, NG], [SW, TAPS], [1, TAPS]])
                        wx = tap[:, 1, :, h * (GP // 2) + j, :, row].rearrange("p t g -> p g t")
                        last = v.tensor_tensor(prods[:, :, :, j, :, row].rearrange("p a b g -> p g b a"), seen,
                                               wx.unsqueeze(2).broadcast_to([128, NG, TAPS, TAPS]), ALU.mult)
                    if h == 0:
                        link(last)
                    else:
                        last.then_inc(win_used, 1)
                        dve.wait_ge(win_used, n + 1)
                    half = slice(h * D // 2, (h + 1) * D // 2)
                    total = by_column_tap[:, 0]
                    link(v.tensor_tensor(total, total, by_column_tap[:, 1], ALU.add))
                    link(v.tensor_tensor(total, total, by_column_tap[:, 2], ALU.add))
                    v.tensor_tensor(total, total, tap_rows[:, 0, :, half], ALU.mult).then_inc(taps_used, 1)
                    dve.wait_ge(taps_used, n * 2 + (h + 1))
                    link(v.tensor_tensor(warp_sum[:, half], total[:, 0], total[:, 1], ALU.add))
                    link(v.tensor_tensor(warp_sum[:, half], warp_sum[:, half], total[:, 2], ALU.add))

                def add_warp(k):
                    link(v.transpose(warped[:, :].rearrange("p (w c j) -> p j w c", w=2, j=GP),
                                     warp_sum[:, :].rearrange("p (j w c) -> p j w c", w=2, j=GP)))
                    dve.wait_ge(x_in[k], w * 16 + 16)
                    x1 = xs[:, 1 - q, k, :]
                    v.tensor_tensor(x1, x1, warped[:, :], ALU.add).then_inc(x1_ready, 1)
                    dve.wait_ge(x1_ready, w * 2 + (k + 1))

                def residual(k):
                    dve.wait_ge(ffn_done, c * 2 + (k + 1))
                    ge(dve, y_ready, c * 2 + (k - 3))
                    v.scalar_tensor_tensor(x2[:, 1 - q, k, :], down_ps[k][:, :], PS_DOWN, xs[:, 1 - q, k, :],
                                           ALU.mult, ALU.add).then_inc(x2_ready, 1)

                def low_part(out, ps, high_ready, ready):
                    dve.wait_ge(high_ready, i * 2 + 2)
                    for k in range(2):
                        cols = slice(k * T, (k + 1) * T)
                        v.scalar_tensor_tensor(out[:, 1, cols], ps[:, cols], gain_now[:, k:k + 1], out[:, 0, cols],
                                               ALU.mult, ALU.subtract).then_inc(ready, 1)

                def hidden_low(g):
                    if ffn:
                        f = 2 * g
                        dve.wait_ge(hidden_hi, i * FT + (f + 2))
                        v.tensor_tensor(hidden_parts[:, 1, f % RING:f % RING + 2, :], hidden[:, f % 4:f % 4 + 2, :],
                                        hidden_parts[:, 0, f % RING:f % RING + 2, :], ALU.subtract).then_inc(hidden_ready, 1)

                def x1T_low(k):
                    dve.wait_ge(x1T_hi, w * 2 + (k + 1))
                    cols = slice(k * T, (k + 1) * T)
                    v.scalar_tensor_tensor(x1T[:, 1, :, cols], up_ps[k][:, :].rearrange("p (t c) -> p t c", t=KT), ACT_UP,
                                           x1T[:, 0, :, cols], ALU.mult, ALU.subtract).then_inc(x1T_ready, 1)

                def mask_scores(k):
                    n = c * 2 + k
                    now = masked[:, k, :]
                    ge(dve, probs_ready, n - 1)
                    link(v.scalar_tensor_tensor(now, prompt_mask[:, 1, :], col(is_postfix, n), prompt_mask[:, 2, :], ALU.mult, ALU.add))
                    dve.wait_ge(score_ps, n + 1)
                    link(v.scalar_tensor_tensor(now, prompt_mask[:, 0, :], col(is_prefix, n), now, ALU.mult, ALU.add))
                    v.tensor_tensor_reduce(out=now, in0=mid_ps[:, 0:T], in1=now, scale=1.0, scalar=3e38,
                                           op0=ALU.add, op1=ALU.min, accum_out=neg_max[:, k:k + 1]).then_inc(masked_ready, 1)

                def add_pooled(k):
                    n = c * 2 + k
                    dve.wait_ge(probs_ready, n + 1)
                    ps, x3 = pool_scale[:, k:k + 1], x2[:, 1 - q, k, :]
                    link(v.reciprocal(ps, row_sum[:, k:k + 1]))
                    link(v.tensor_tensor(ps, ps, col(inv_count, n), ALU.mult))
                    dve.wait_ge(pooled_ps, n + 1)
                    v.scalar_tensor_tensor(x3, wide_ps[:, :], ps, x3, ALU.mult, ALU.add).then_inc(x3_ready, 1)

                def adapted(k):
                    n = c * 2 + k
                    yk = y[:, k, :]
                    dve.wait_ge(adapt_ps, n + 1)
                    ge(dve, stored[k], c * 16)
                    v.tensor_tensor(yk, wide_ps[:, :], x2[:, 1 - q, k, :], ALU.add).then_inc(adapt_read, 1)
                    dve.wait_ge(adapt_read, n + 1)
                    link(v.bn_stats(stats[:, k, :], yk))
                    link(v.bn_aggr(mv[:, k, :], stats[:, k, :]))

                def inverse_deviations():
                    link(v.tensor_scalar(var_eps[:, :], mv[:, :, 1], EPS, None, ALU.add))
                    link(v.tensor_scalar(guess_i[:, :], var_eps[:, :].bitcast(i32), 1, None, ALU.arith_shift_right))
                    link(v.tensor_scalar(rstd[:, :].bitcast(i32), guess_i[:, :], -1.0, float(0x5F3759DF), ALU.mult, ALU.add))
                    for _ in range(3):
                        link(v.tensor_tensor(newton[:, :], rstd[:, :], rstd[:, :], ALU.mult))
                        link(v.scalar_tensor_tensor(newton[:, :], newton[:, :], -0.5, var_eps[:, :], ALU.mult, ALU.mult))
                        link(v.scalar_tensor_tensor(rstd[:, :], newton[:, :], 1.5, rstd[:, :], ALU.add, ALU.mult))

                def normalise(k):
                    yk = y[:, k, :]
                    link(v.tensor_scalar(yk, yk, mv[:, k, 0:1], rstd[:, k:k + 1], ALU.subtract, ALU.mult))
                    dve.wait_ge(lang_in[k], c * 64)
                    link(v.tensor_tensor(yk, yk, gamma_b[:, k, :], ALU.mult))
                    link(v.tensor_tensor(yk, yk, beta_b[:, k, :], ALU.add))
                    v.tensor_tensor(yk, yk, x2[:, q, k, :], ALU.add).then_inc(y_ready, 1)

                dve.sem_clear(dve_chain)
                if tail:
                    for k in range(2):
                        residual(k)
                if ffn:
                    low_part(low_i, low_ps, low_i_hi, low_i_ready)
                if finish:
                    inverse_deviations()
                    for k in range(2):
                        normalise(k)
                if warp:
                    warp_half(0, 0)
                hidden_low(0)
                if warp:
                    warp_half(0, 1)
                hidden_low(1)
                if warp:
                    add_warp(0)
                if tail:
                    mask_scores(0)
                hidden_low(2)
                if tail:
                    mask_scores(1)
                hidden_low(3)
                if warp:
                    warp_half(1, 0)
                if tail:
                    add_pooled(0)
                hidden_low(4)
                if tail:
                    add_pooled(1)
                if warp:
                    warp_half(1, 1)
                hidden_low(5)
                if warp:
                    add_warp(1)
                hidden_low(6)
                if tail:
                    adapted(0)
                    adapted(1)
                hidden_low(7)
                if warp:
                    for k in range(2):
                        x1T_low(k)
                if ffn:
                    low_part(low_o, low_ps, low_o_hi, low_o_ready)

            for i in range(-1, 4):
                body(i, i % 2)
            with dve.Fori(2, NP // 2 - 1) as i:
                for q in range(2):
                    body(i * 2 + q, q)
            for i in range(NP - 2, NP + 2):
                body(i, i % 2)

        @block.scalar
        def _(act):
            s = nc.scalar
            act.wait_ge(set_ready, 2)
            s.activation(sincos[:, :, :], trig[:, :, :], ACT.Sin).then_inc(sin_ready, 1)
            for n, job in enumerate(jobs):
                dst, src, factor = job_ends(*job)
                act.wait_ge(pe_set, n + 1)
                s.activation(dst[0], src, ACT.Copy, scale=factor).then_inc(ev_act, 1)
            act.wait_ge(corr_in, 16 * CORR)

            def body(i, q):
                c, w = i - 1, i + 1
                ffn, tail, warp = there(i, 0), there(i, 1), there(i, -1)

                def copy_T(k, filled):
                    act.wait_ge(filled, c * 2 + (k + 1))
                    s.activation(xT[:, k, :, :].rearrange("p t c -> p (t c)"), tr_ps[:, :], ACT.Copy).then_inc(xT_ready, 1)

                def attend(k):
                    act.wait_ge(att_ps, c * 2 + (k + 1))
                    s.activation(att[:, k, :], mid_ps[:, 0:T], ACT.Tanh, bias=ab1c[:, 0:1]).then_inc(att_ready, 1)

                def exponentials(k):
                    act.wait_ge(masked_ready, c * 2 + (k + 1))
                    s.activation(probs[:, k, :], masked[:, k, :], ACT.Exp, bias=neg_max[:, k:k + 1], scale=-1.0,
                                 accum_out=row_sum[:, k:k + 1]).then_inc(probs_ready, 1)

                def copy_probs(k):
                    act.wait_ge(probsT_ps, c * 2 + (k + 1))
                    s.activation(probsT[:, k, :], mid_ps[:, 0:T], ACT.Copy).then_inc(probsT_ready, 1)

                def adapter_relu(k):
                    act.wait_ge(h_ps, c * 2 + (k + 1))
                    s.activation(hA[:, k, :], mid_ps[:, 0:T], ACT.Relu, bias=lb1_now[:, k:k + 1]).then_inc(h_ready, 1)

                steps = {2: [(copy_T, 0, x2T_ps)], 3: [(copy_T, 1, x2T_ps), (attend, 0)], 4: [(attend, 1)],
                         7: [(exponentials, 0)], 8: [(copy_probs, 0), (exponentials, 1)], 9: [(copy_probs, 1)],
                         11: [(copy_T, 0, x3T_ps)], 12: [(copy_T, 1, x3T_ps)],
                         13: [(adapter_relu, 0)], 14: [(adapter_relu, 1)]}

                act.sem_clear(act_chain)
                ge(act, low_o_ready, i * 2)
                ge(act, h_ready, c * 2)
                ge(act, adapt_ps, c * 2)
                if ffn:
                    s.activation(gain_now[:, :], expert_gain[:, bass.ds(i * 2, 2)], ACT.Copy).then_inc(act_chain, 1)
                if tail:
                    s.activation(lb1_now[:, :], lb1_img[:, bass.ds(c * 2, 2)], ACT.Copy).then_inc(act_chain, 1)
                    s.activation(lang_now[:, :, :], lang_hot[0:96, bass.ds(c * 2, 2)].unsqueeze(2).broadcast_to([96, 2, T]),
                                 ACT.Copy).then_inc(lang_ready, 1)
                if ffn or tail:
                    act.wait_ge(act_chain, ffn + tail)

                def project(out, filled, ready):
                    act.wait_ge(filled, i + 1)
                    for k in range(2):
                        s.activation(out[:, 0, k * T:(k + 1) * T], low_ps[:, k * T:(k + 1) * T], ACT.Copy,
                                     scale=gain_now[:, k:k + 1]).then_inc(ready, 1)

                if ffn:
                    project(low_i, low_i_ps, low_i_hi)
                for f in range(FT):
                    if ffn:
                        act.wait_ge(up_done, i * FT + (f + 1))
                        ge(act, hidden_ready, i * (FT // 2) + (f // 2 - 1))
                        s.activation(hidden[:, f % 4, :], up_ps[f % 2][:, 0:2 * T], ACT.Relu, scale=1.0 / W_UP)
                        ge(act, down_done, i * FT + (f - RING + 1))
                        s.activation(hidden_parts[:, 0, f % RING, :], up_ps[f % 2][:, 0:2 * T], ACT.Relu,
                                     scale=1.0 / W_UP).then_inc(hidden_hi, 1)
                    if tail:
                        for step in steps.get(f, []):
                            step[0](*step[1:])
                if warp:
                    for k in range(2):
                        act.wait_ge(x1T_ps, w * 2 + (k + 1))
                        s.activation(x1T[:, 0, :, k * T:(k + 1) * T], up_ps[k][:, :].rearrange("p (t c) -> p t c", t=KT),
                                     ACT.Copy, scale=ACT_UP).then_inc(x1T_hi, 1)
                if ffn:
                    project(low_o, low_o_ps, low_o_hi)

            for i in range(-1, 4):
                body(i, i % 2)
            with act.Fori(2, NP // 2 - 1) as i:
                for q in range(2):
                    body(i * 2 + q, q)
            for i in range(NP - 2, NP + 1):
                body(i, i % 2)

        @block.tensor
        def _(pe):
            t = nc.tensor

            def transposes(dst, src, width=128):
                for n in range(4):
                    last = t.transpose(dst[:, n * 128:(n + 1) * 128], src(n), ident[:, :])
                return last

            def tile(n):
                return slice(n * 128, (n + 1) * 128)

            pe.wait_ge(consts_ready, 9)
            pe.wait_ge(common_in, 16 * 7)
            for n, (kind, j) in enumerate(jobs):
                b = banks[n % 8]
                if n >= 8:
                    if jobs[n - 8][0] in plain:
                        pe.wait_ge(ev_act, n - 7)
                    else:
                        pe.wait_ge(ev_dve, splits[n - 7])
                if kind in ("cwib", "cwob"):
                    st = st_cwib if kind == "cwib" else st_cwob
                    last = transposes(b[0:R, :], lambda m: st[:, 4 * j + m, :])
                elif kind == "wi":
                    if j % 8 == 0:
                        pe.wait_ge(wi_in[j // 8], 16)
                    if j == 0:
                        pe.wait_ge(ev_act, 5)
                    for m in range(KT):
                        at = (j % 8) * D
                        t.matmul(b[:, tile(m)], st_w[:, at + m * 128:at + (m + 1) * 128], ident[:, :], start=True, stop=False)
                        last = t.matmul(b[:, tile(m)], st_cwia[:, tile(m)], cwibT[j // 4][:, tile(j % 4)], start=False, stop=True)
                elif kind == "ewia":
                    pe.wait_ge(corr_in, 16 * CORR)
                    last = transposes(b, lambda m: st_ewia[:, tile(m)])
                elif kind == "lb1":
                    pe.wait_ge(set_ready, 3)
                    last = t.matmul(b[:, 0:B], st_lb1, lang_hot[0:NL, :], start=True, stop=True)
                elif kind == "ewoa":
                    last = transposes(b, lambda m: st_ewoa[:, tile(4 * j + m)])
                elif kind == "ewob":
                    last = transposes(b, lambda m: st_ewob[:, m].rearrange("p e r -> p (e r)"))
                elif kind == "ewib":
                    if j == 0:
                        pe.wait_ge(ewib_in, 16 * FT)
                    last = transposes(b, lambda m: st_ewib[:, 4 * j + m].rearrange("p e r -> p (e r)"))
                else:
                    dt, j = j
                    if j == 0 and dt % 2 == 0:
                        pe.wait_ge(wo_in[dt // 2], 16)
                    for m in range(4):
                        at = (dt % 2) * F + (4 * j + m) * 128
                        t.matmul(b[:, tile(m)], st_w[:, at:at + 128], ident[:, :], start=True, stop=False)
                        last = t.matmul(b[:, tile(m)], st_cwoa[j][:, tile(m)], cwobT[:, tile(dt)], start=False, stop=True)
                last.then_inc(pe_set, 1)
            pe.wait_ge(ev_dve, splits[-1])
            pe.wait_ge(set_ready, 4)

            def body(i, q):
                c, w = i - 1, i + 1
                ffn, tail, warp = there(i, 0), there(i, 1), there(i, -1)

                def x2_T(k):
                    n = c * 2 + k
                    pe.wait_ge(x2_ready, n + 1)
                    ge(pe, xT_ready, c * 4 + k)
                    transposes(tr_ps, lambda m: x2[:, 1 - q, k, tile(m)]).then_inc(x2T_ps, 1)

                def att_in(k):
                    n = c * 2 + k
                    pe.wait_ge(xT_ready, c * 4 + (k + 1))
                    if k == 0:
                        ge(pe, h_ready, n)
                    else:
                        pe.wait_ge(att_ready, n)
                    for m in range(KT):
                        last = t.matmul(mid_ps[:, 0:T], aw1[:, m, :], xT[:, k, m, :], start=(m == 0), stop=(m == KT - 1))
                    last.then_inc(att_ps, 1)

                def scores(k):
                    n = c * 2 + k
                    pe.wait_ge(att_ready, n + 1 if k else n + 2)
                    if k:
                        pe.wait_ge(masked_ready, n)
                    t.matmul(mid_ps[:, 0:T], vneg[:, :], att[:, k, :], start=True, stop=True).then_inc(score_ps, 1)

                def probs_T(k):
                    n = c * 2 + k
                    pe.wait_ge(probs_ready, n + 1)
                    if k:
                        pe.wait_ge(probsT_ready, n)
                    else:
                        pe.wait_ge(masked_ready, n + 2)
                    t.transpose(mid_ps[:, 0:T], probs[:, k, :], ident[:, :]).then_inc(probsT_ps, 1)

                def pooled(k):
                    n = c * 2 + k
                    pe.wait_ge(probsT_ready, n + 1)
                    if k:
                        pe.wait_ge(x3_ready, n)
                    else:
                        ge(pe, adapt_read, n)
                    t.matmul(wide_ps[:, :], probsT[:, k, :], x2[:, 1 - q, k, :], start=True, stop=True).then_inc(pooled_ps, 1)

                def x3_T(k):
                    n = c * 2 + k
                    pe.wait_ge(x3_ready, n + 1)
                    pe.wait_ge(xT_ready, c * 4 + (k + 2))
                    transposes(tr_ps, lambda m: x2[:, 1 - q, k, tile(m)]).then_inc(x3T_ps, 1)

                def adapter_in(k):
                    n = c * 2 + k
                    pe.wait_ge(xT_ready, c * 4 + (k + 3))
                    pe.wait_ge(lang_in[k], c * 64 + 64)
                    if k:
                        pe.wait_ge(h_ready, n)
                    else:
                        pe.wait_ge(probsT_ready, n + 2)
                    for m in range(KT):
                        last = t.matmul(mid_ps[:, 0:T], lw1[:, k, m, :], xT[:, k, m, :], start=(m == 0), stop=(m == KT - 1))
                    last.then_inc(h_ps, 1)

                def adapter_out(k):
                    n = c * 2 + k
                    pe.wait_ge(h_ready, n + 1)
                    if k:
                        pe.wait_ge(adapt_read, n)
                    else:
                        pe.wait_ge(x3_ready, n + 2)
                    t.matmul(wide_ps[:, :], hA[:, k, :], lw2[:, k, :], start=True, stop=False)
                    pe.wait_ge(lang_ready, c + 1)
                    t.matmul(wide_ps[:, :], lang_now[:, k, :], lb2_parts[:, :], start=False, stop=True).then_inc(adapt_ps, 1)

                steps = {2: [(x2_T, 0)], 3: [(x2_T, 1), (att_in, 0)], 4: [(att_in, 1)], 5: [(scores, 0)], 6: [(scores, 1)],
                         8: [(probs_T, 0)], 9: [(probs_T, 1), (pooled, 0)], 10: [(pooled, 1)], 11: [(x3_T, 0)],
                         12: [(x3_T, 1)], 13: [(adapter_in, 0)], 14: [(adapter_in, 1), (adapter_out, 0)], 15: [(adapter_out, 1)]}

                def up(f):
                    b = up_ps[f % 2]
                    if f >= 2:
                        pe.wait_ge(hidden_hi, i * FT + (f - 1))
                    for m in range(KT):
                        for ws, xs_ in PARTS:
                            t.matmul(b[:, 0:2 * T], wiT[:, ws, m, tile(f)], x1T[:, xs_, m, :],
                                     start=(m == 0 and ws + xs_ == 0), stop=False)
                    if f == 0:
                        pe.wait_ge(low_i_ready, i * 2 + 2)
                    for n, (ws, xs_) in enumerate(PARTS):
                        last = t.matmul(b[:, 0:2 * T], ewibT[:, ws, tile(f)], low_i[:, xs_, :], start=False, stop=(n == 2))
                    last.then_inc(up_done, 1)

                def down(f):
                    pe.wait_ge(hidden_ready, i * (FT // 2) + (f // 2 + 1))
                    if f == 0:
                        ge(pe, x2_ready, i * 2)
                    first, end = (f == 0), (f == FT - 1)
                    for n, (ws, hs) in enumerate(PARTS):
                        low = t.matmul(low_ps[:, 0:2 * T], ewoaT[:, ws, f, :], hidden_parts[:, hs, f % RING, :],
                                       start=(first and n == 0), stop=(end and n == 2))
                    if end:
                        low.then_inc(low_o_ps, 1)
                    for k in range(2):
                        for n, (hs, ws) in enumerate(PARTS):
                            last = t.matmul(down_ps[k][:, :], hidden_parts[:, hs, f % RING, k * T:(k + 1) * T], woT[:, ws, f, :],
                                            start=(first and n == 0), stop=False)
                    last.then_inc(down_done, 1)

                if ffn:
                    pe.wait_ge(x1T_ready, i * 2 + 2)
                    ge(pe, low_o_ready, i * 2)
                    for m in range(KT):
                        for n, (ws, xs_) in enumerate(PARTS):
                            last = t.matmul(low_ps[:, 0:2 * T], ewiaT[:, ws, m, :], x1T[:, xs_, m, :],
                                            start=(m == 0 and n == 0), stop=(m == KT - 1 and n == 2))
                    last.then_inc(low_i_ps, 1)
                for f in range(FT):
                    if ffn:
                        up(f)
                        if f >= LAG:
                            down(f - LAG)
                    if tail:
                        for step in steps.get(f, []):
                            step[0](*step[1:])
                if warp:
                    ge(pe, hidden_hi, w * FT)
                    for k in range(2):
                        pe.wait_ge(x1_ready, w * 2 + (k + 1))
                        transposes(up_ps[k], lambda m: xs[:, 1 - q, k, tile(m)]).then_inc(x1T_ps, 1)
                if ffn:
                    for f in range(FT - LAG, FT):
                        down(f)
                    pe.wait_ge(low_o_ready, i * 2 + 2)
                    for k in range(2):
                        for n, (hs, ws) in enumerate(PARTS):
                            last = t.matmul(down_ps[k][:, :], low_o[:, hs, k * T:(k + 1) * T], ewobT[:, ws, :],
                                            start=False, stop=(n == 2))
                        last.then_inc(ffn_done, 1)

            for i in range(-1, 4):
                body(i, i % 2)
            with pe.Fori(2, NP // 2 - 1) as i:
                for q in range(2):
                    body(i * 2 + q, q)
            for i in range(NP - 2, NP + 1):
                body(i, i % 2)


_INS = ['x', 'fside_Bx2_0', 'condB_angle', 'itok_B_0_7', 'itok_B_0_2', 'itok_B_0_8', 'L1_cond_wi', 'L1_cond_wo',
        'L1_cond_common_wi_a', 'L1_cond_common_wi_b', 'L1_cond_common_wo_a', 'L1_cond_common_wo_b',
        'L1_cond_experts_wi_a', 'L1_cond_experts_wi_b', 'L1_cond_experts_wo_a', 'L1_cond_experts_wo_b',
        'L2_cond_W1', 'L2_cond_b1', 'L2_cond_v', 'L3_cond_W1', 'L3_cond_b1', 'L3_cond_W2', 'L3_cond_b2',
        'L3_cond_gamma', 'L3_cond_beta']


def kernel(**inputs):
    import concourse.bacc as _bacc
    from concourse.bass_utils import run_bass_kernel_spmd as _run

    nc = _bacc.Bacc("TRN2", target_bir_lowering=False, num_devices=1)
    arrays, args = {}, []
    for name in _INS:
        a = np.ascontiguousarray(inputs[name])
        arrays[f"in_{name}_dram"] = a
        args.append(nc.dram_tensor(f"in_{name}_dram", a.shape, mybir.dt.from_np(a.dtype), kind="ExternalInput").ap())
    shape = inputs["x"].shape
    out = nc.dram_tensor("out_0_dram", tuple(shape), fp32, kind="ExternalOutput").ap()
    build(nc, *args, out)
    return _run(nc, [arrays], core_ids=[0]).results[0]["out_0_dram"]
```

```python
import numpy as np
import concourse.bass as bass
from concourse import mybir
from contextlib import ExitStack

T = 128
D = 512
F = 2048
KT = D // 128
FT = F // 128
E, R = 8, 16
NL = 10
A = 128
ALPHA = 2.0
EPS = 1e-5
BIG = 1e30

ACT_UP = 16.0
W_UP = 64.0
PS_DOWN = 1.0 / (ACT_UP * W_UP)
RING = 8
LAG = 6
PARTS = ((0, 0), (0, 1), (1, 0))

RY = (T - 1) / D
RX = (D - 1) / T
GP = 8
NG = 8
Q = GP * GP
HALF = Q // 2
LOADED = 32
TAPS = 3
SW, SS = 128, 64
NS = D // SS + 2
PADY = 5
ROWS = T + 2 * PADY
SLOT = NS * ROWS * SW
RUN = 4 * SW + 44
OFF_MAX = 2 * SW + 39
XLO, XHI = -float(SS), float(D)
YLO, YHI = -float(PADY), float(T)

ALU = mybir.AluOpType
ACT = mybir.ActivationFunctionType
fp32, i32, f16, bf16 = mybir.dt.float32, mybir.dt.int32, mybir.dt.float16, mybir.dt.bfloat16



def build(nc, x, fside, angle, tok_expert, tok_prompt, tok_lang, wi, wo, cwi_a, cwi_b, cwo_a, cwo_b,
          ewi_a, ewi_b, ewo_a, ewo_b, aW1, ab1, av, lW1, lb1, lW2, lb2, lgamma, lbeta, out):
    B = x.shape[0]
    NP = B // 2
    ctx = ExitStack()
    with ctx:
        def sb(name, shape, dt=fp32):
            return ctx.enter_context(nc.sbuf_tensor(name, shape, dt))

        def sem(name):
            return ctx.enter_context(nc.semaphore(name))

        def ap(handle, offset, dims):
            return bass.AP(handle.tensor, offset, dims)

        strips = nc.dram_tensor("strips", (2, NS, ROWS, SW), fp32).ap()
        ia_dram = nc.dram_tensor("ia_dram", (E, 128, KT * 4 * R), f16).ap()
        ib_dram = nc.dram_tensor("ib_dram", (E, 2, R, F), f16).ap()
        oa_dram = nc.dram_tensor("oa_dram", (E, 128, FT * 2 * R), f16).ap()
        ob_dram = nc.dram_tensor("ob_dram", (E, R, 2 * D), f16).ap()
        frac_dram = nc.dram_tensor("frac_dram", (B, 2 * Q), fp32).ap()
        offs_dram = nc.dram_tensor("offs_dram", (B, Q), i32).ap()

        wiT = sb("wiT", [128, 2, KT, F], f16)
        woT = sb("woT", [128, 2, FT, D], f16)
        N_IA, N_OA = KT * 4 * R, FT * 2 * R
        experts = sb("experts", [128, E * (N_IA + N_OA) + 2 * F + 2 * D], f16)
        cuts_all = np.cumsum([0, E * N_IA, 2 * F, E * N_OA, 2 * D]).tolist()
        ia_all, ib_all, oa_all, ob_all = (experts[:, a:b] for a, b in zip(cuts_all[:-1], cuts_all[1:]))
        cuts_now = np.cumsum([0, 2 * N_IA, 2 * F, 2 * N_OA, 4 * D]).tolist()
        ia_now, ib_now, oa_now, ob_now = (experts[:, a:b] for a, b in zip(cuts_now[:-1], cuts_now[1:]))
        ewiaT = ia_now.rearrange("p (k t s c) -> p k t s c", k=2, t=KT, s=2)
        ewibT = ib_now[0:2 * R, :].rearrange("p (k f) -> p k f", k=2)
        ewoaT = oa_now.rearrange("p (k t c) -> p k t c", k=2, t=FT)
        ewobT = ob_now[0:2 * R, :].rearrange("p (k s d) -> p k s d", k=2, s=2)
        aw1 = sb("aw1", [128, KT, A])
        ab1c = sb("ab1c", [A, 1])
        avc = sb("avc", [A, 1])
        vneg = sb("vneg", [A, T])
        lb2_parts = sb("lb2_parts", [96, D], bf16)
        ident = sb("ident", [128, 128])
        prompt_mask = sb("prompt_mask", [T, 3, T])
        is_prefix = sb("is_prefix", [128, B])
        is_postfix = sb("is_postfix", [128, B])
        inv_count = sb("inv_count", [128, B])
        lb1_img = sb("lb1_img", [A, B])
        lang_hot = sb("lang_hot", [128, B])
        lang_row = sb("lang_row", [1, B], i32)
        expert_row = sb("expert_row", [1, B], i32)
        gather_at = sb("gather_at", [128, B, NG], i32)
        gather_now = sb("gather_now", [128, 2, NG], i32)
        frac_group = sb("frac_group", [128, B, 2, NG])
        N_WIN, N_PROD, N_TAPS = NG * RUN, TAPS * TAPS * D // 2, 2 * TAPS * D
        work = sb("work", [128, N_WIN + N_PROD + N_TAPS])
        win = work[:, 0:N_WIN].rearrange("p (g r) -> p g r", g=NG)
        prod = work[:, N_WIN:N_WIN + N_PROD]
        taps = work[:, N_WIN + N_PROD:]
        warp_sum = sb("warp_sum", [128, D])
        warped = sb("warped", [T, D])
        frac_now = sb("frac_now", [128, 2, NG])
        frac_pix = sb("frac_pix", [128, 2, 2 * Q])
        offs = sb("offs", [1, 2, Q], i32)
        offs_now = sb("offs_now", [1, Q], i32)
        xs = sb("xs", [T, 2, 2, D])
        x1T = sb("x1T", [128, 2, KT, 2 * T], f16)
        hidden = sb("hidden", [128, 4, 2 * T])
        hidden_parts = sb("hidden_parts", [128, 2, RING, 2 * T], f16)
        low_i = sb("low_i", [2 * R, 2, 2 * T], f16)
        low_o = sb("low_o", [2 * R, 2, 2 * T], f16)
        x2 = sb("x2", [T, 2, 2, D])
        xT = sb("xT", [128, 2, KT, T])
        att = sb("att", [A, 2, T])
        masked = sb("masked", [T, 2, T])
        probs = sb("probs", [T, 2, T])
        probsT = sb("probsT", [T, 2, T])
        hA = att
        neg_max = sb("neg_max", [T, 2])
        row_sum = sb("row_sum", [T, 2])
        pool_scale = sb("pool_scale", [T, 2])
        stats = sb("stats", [T, 2, 6])
        mv = sb("mv", [T, 2, 2])
        rstd = sb("rstd", [T, 2])
        lb1_now = sb("lb1_now", [A, 2])
        lang_now = sb("lang_now", [96, 2, T], bf16)
        var_eps = sb("var_eps", [T, 2])
        newton = sb("newton", [T, 2])
        neg_mean = sb("neg_mean", [T, 2])
        guess_i = sb("guess_i", [T, 2], i32)
        y = sb("y", [T, 2, D])
        lw1 = sb("lw1", [128, 2, KT, A])
        lw2 = sb("lw2", [A, 2, D])
        gamma_b = sb("gamma_b", [T, 2, D])
        beta_b = sb("beta_b", [T, 2, D])
        NA = B + 1
        ang = sb("ang", [128, NA])
        sincos = sb("sincos", [128, 2, NA])
        trig = sb("trig", [128, 2, NA])
        part_i = sb("part_i", [128, 2], i32)
        part = sb("part", [128, 4])
        pixel_i = warp_sum[:, 0:2 * Q].bitcast(i32).rearrange("p (a q) -> p a q", a=2)
        group_i = warp_sum[:, 2 * Q:2 * Q + 2 * NG].bitcast(i32).rearrange("p (a g) -> p a g", a=2)
        group = warp_sum[:, 2 * Q + 2 * NG:2 * Q + 4 * NG].rearrange("p (a g) -> p a g", a=2)
        shift = masked[:, 0, :].rearrange("p (b c) -> p b c", c=2)[:, 0:B, :]
        ids_i, ids = (t[:, :, :].rearrange("p k t -> p (k t)")[:, 0:2 * B].rearrange("p (n b) -> p n b", n=2)
                      for t in (probs, probsT))
        ids_i = ids_i.bitcast(i32)

        banks = [ctx.enter_context(nc.psum_tensor(f"bank{n}", [128, 512], fp32)) for n in range(8)]
        up_ps = [banks[0], banks[1]]
        down_ps = [banks[2], banks[3]]
        low_ps = banks[4]
        tr_ps = banks[5]
        mid_ps = banks[6]
        wide_ps = banks[7]

        in_loaded = sem("in_loaded")
        wi_in = [sem("wi_in0"), sem("wi_in1")]
        wo_in = [sem("wo_in0"), sem("wo_in1")]
        common_in = sem("common_in")
        corr_in = sem("corr_in")
        ewib_in = sem("ewib_in")
        zero_ready = sem("zero_ready")
        strips_zero = sem("strips_zero")
        consts_ready = sem("consts_ready")
        pool_chain = sem("pool_chain")
        set_chain = sem("set_chain")
        set_ready = sem("set_ready")
        sin_ready = sem("sin_ready")
        pe_set = sem("pe_set")
        ev_act = sem("ev_act")
        ev_dve = sem("ev_dve")
        lb2_zero = sem("lb2_zero")
        lb2_in = sem("lb2_in")
        pix_out = sem("pix_out")
        strips_in = [sem("strips_in0"), sem("strips_in1")]
        x_in = [sem("x_in0"), sem("x_in1")]
        pix_in = [sem("pix_in0"), sem("pix_in1")]
        lang_in = [sem("lang_in0"), sem("lang_in1")]
        stored = [sem("stored0"), sem("stored1")]
        gathered = [sem("gathered0"), sem("gathered1")]
        taps_ready = sem("taps_ready")
        taps_used = sem("taps_used")
        win_used = sem("win_used")
        x1_ready = sem("x1_ready")
        x1T_ps = sem("x1T_ps")
        x1T_hi = sem("x1T_hi")
        x1T_ready = sem("x1T_ready")
        low_i_ps = sem("low_i_ps")
        low_i_hi = sem("low_i_hi")
        low_i_ready = sem("low_i_ready")
        up_done = sem("up_done")
        hidden_hi = sem("hidden_hi")
        hidden_ready = sem("hidden_ready")
        down_done = sem("down_done")
        low_o_ps = sem("low_o_ps")
        low_o_hi = sem("low_o_hi")
        low_o_ready = sem("low_o_ready")
        ffn_done = sem("ffn_done")
        x2_ready = sem("x2_ready")
        x2T_ps = sem("x2T_ps")
        xT_ready = sem("xT_ready")
        att_ps = sem("att_ps")
        att_ready = sem("att_ready")
        score_ps = sem("score_ps")
        masked_ready = sem("masked_ready")
        probs_ready = sem("probs_ready")
        probsT_ps = sem("probsT_ps")
        probsT_ready = sem("probsT_ready")
        pooled_ps = sem("pooled_ps")
        x3_ready = sem("x3_ready")
        x3T_ps = sem("x3T_ps")
        h_ps = sem("h_ps")
        h_ready = sem("h_ready")
        adapt_ps = sem("adapt_ps")
        adapt_read = sem("adapt_read")
        guess_ready = sem("guess_ready")
        scale_ready = sem("scale_ready")
        centred = sem("centred")
        norm_ready = sem("norm_ready")
        y_ready = sem("y_ready")
        dve_chain = sem("dve_chain")
        act_chain = sem("act_chain")
        lang_ready = sem("lang_ready")
        experts_out = sem("experts_out")
        expert_i_in = sem("expert_i_in")
        expert_o_in = sem("expert_o_in")

        def ge(eng, s, n):
            if not isinstance(n, int) or n > 0:
                eng.wait_ge(s, n)

        def there(i, first):
            return not isinstance(i, int) or first <= i < NP + first

        def col(table, n):
            return table[:, bass.ds(n, 1)]

        room = woT[:, :, :, :].rearrange("p s t d -> p (s t d)").bitcast(fp32)
        st_ewib = room[:, 0:2048].rearrange("p (t e r) -> p t e r", e=E, r=R)
        st_ewoa = room[:, 2048:4096]
        st_ewia = room[:, 4096:4608]
        st_ewob = room[:, 4608:5120].rearrange("p (t e r) -> p t e r", e=E, r=R)
        st_cwib = room[:, 5120:5376].rearrange("p (t r) -> p t r", r=R)
        st_cwob = room[:, 5376:5440].rearrange("p (t r) -> p t r", r=R)
        x2_flat = x2[:, :, :, :].rearrange("p q k d -> p (q k d)")
        parts_flat = hidden_parts[:, :, :, :].rearrange("p s r t -> p (s r t)").bitcast(fp32)
        st_wi = [room[:, 6144:8192], x2_flat]
        st_wo = [parts_flat, x2_flat]
        zeros = parts_flat
        st_lb1 = masked[0:NL, 1, 0:A]
        st_cwia = lw2[0:R, 1, :]
        cwobT = y[0:R, 0, :]
        hidden_flat = hidden[:, :, :].rearrange("p s t -> p (s t)")
        lw1_flat = lw1[:, :, :, :].rearrange("p k t a -> p (k t a)")
        cwibT = [flat[0:R, n * 512:(n + 1) * 512] for flat in (hidden_flat, lw1_flat) for n in range(2)]
        st_cwoa = [gamma_b[0:R, 0, :], gamma_b[0:R, 1, :], beta_b[0:R, 0, :], beta_b[0:R, 1, :]]
        lb2_stage = lw2[0:96, 0, :]

        def load_wi(eng, r):
            eng.dma_start(st_wi[r % 2].rearrange("p (t d) -> p t d", t=4),
                          wi[r * 512:(r + 1) * 512, :].rearrange("(t p) d -> p t d", p=128)).then_inc(wi_in[r % 2], 16)

        def load_wo(eng, r):
            eng.dma_start(st_wo[r % 2], wo[r * 128:(r + 1) * 128, :]).then_inc(wo_in[r % 2], 16)

        jobs = ([("cwib", t) for t in range(FT // 4)] + [("cwob", 0)] + [("wi", t) for t in range(FT)]
                + [("ewia", 0), ("lb1", 0)] + [("ewoa", t) for t in range(4)] + [("ewob", 0)]
                + [("ewib", t) for t in range(4)]
                + [("wo", (dt, t)) for dt in range(KT) for t in range(4)])
        at_job = {job: n for n, job in enumerate(jobs)}
        plain = ("cwib", "cwob", "lb1")
        splits = [sum(kind not in plain for kind, _ in jobs[:n]) for n in range(len(jobs) + 1)]

        def job_ends(kind, t):
            b = banks[at_job[(kind, t)] % 8]
            tiles = b[:, :].rearrange("p (a b) -> p a b", b=128)
            if kind == "cwib":
                return [cwibT[t]], b[0:R, :], ALPHA
            if kind == "cwob":
                return [cwobT], b[0:R, :], ALPHA
            if kind == "lb1":
                return [lb1_img[:, :]], b[:, 0:B], 1.0
            if kind == "wi":
                return [wiT[:, s, :, t * 128:(t + 1) * 128] for s in range(2)], tiles, W_UP
            by_expert = tiles.rearrange("p t (e r) -> p t e r", r=R)
            if kind == "ewia":
                twice = ia_all.rearrange("p (e t s c r) -> p t s c e r", e=E, t=KT, s=2, c=2)
                return [[twice[:, :, s, c] for c in range(2)] for s in range(2)], by_expert, W_UP
            if kind == "ewib":
                return [ib_all[:, s * F + t * 512:s * F + (t + 1) * 512] for s in range(2)], b[:, :], W_UP
            if kind == "ewoa":
                return [oa_all.rearrange("p (e t s r) -> p t s e r", e=E, t=FT, s=2)[:, 4 * t:4 * t + 4, s]
                        for s in range(2)], by_expert, W_UP
            if kind == "ewob":
                return [ob_all[:, s * D:(s + 1) * D] for s in range(2)], b[:, :], W_UP
            dt, t = t
            return [woT[:, s, 4 * t:4 * t + 4, dt * 128:(dt + 1) * 128] for s in range(2)], tiles, W_UP

        per = 2 * SLOT // 128
        CORR = 2 + KT + 4
        pixel_f = xT[:, :, :, :].rearrange("p k t c -> p (k t c)")[0:B, :]
        pix_frac = pixel_f[:, 6 * Q:8 * Q]
        pix_offs = pixel_f[:, 8 * Q:9 * Q].bitcast(i32)

        block = ctx.enter_context(nc.Block())

        @block.sync
        def _(sp):
            sp.dma_start(ang[:, 0:B], angle.unsqueeze(0).broadcast_to([128, B])).then_inc(in_loaded, 16)
            sp.dma_start(masked[:, 0, 0:2 * B],
                         fside.rearrange("b c -> (b c)").unsqueeze(0).broadcast_to([128, 2 * B])).then_inc(in_loaded, 16)
            for n, tok in enumerate((tok_prompt, tok_lang)):
                sp.dma_start(ids_i[:, n, :], tok.unsqueeze(0).broadcast_to([128, B])).then_inc(in_loaded, 16)
            sp.dma_start(lang_row[:, :], tok_lang.unsqueeze(0)).then_inc(in_loaded, 16)
            sp.dma_start(expert_row[:, :], tok_expert.unsqueeze(0)).then_inc(in_loaded, 16)
            sp.wait_ge(set_ready, 1)
            sp.dma_start(ang[0:B, B:B + 1], angle.unsqueeze(1)).then_inc(in_loaded, 16)
            sp.dma_start(st_cwib, cwi_b.rearrange("(t p) r -> p t r", p=128)).then_inc(common_in, 16)
            sp.dma_start(st_cwia, cwi_a).then_inc(common_in, 16)
            sp.dma_start(st_cwob, cwo_b.rearrange("(t p) r -> p t r", p=128)).then_inc(common_in, 16)
            for t in range(4):
                sp.dma_start(st_cwoa[t], cwo_a[:, t * 512:(t + 1) * 512]).then_inc(common_in, 16)
            for r in range(2):
                load_wi(sp, r)
            sp.dma_start(st_ewia, ewi_a.rearrange("e r d -> (e r) d")).then_inc(corr_in, 16)
            sp.dma_start(st_ewoa, ewo_a.rearrange("e r f -> (e r) f")).then_inc(corr_in, 16)
            for t in range(KT):
                sp.dma_start(st_ewob[:, t], ewo_b[:, t * 128:(t + 1) * 128, :].rearrange("e p r -> p e r")).then_inc(corr_in, 16)
            sp.dma_start(aw1[:, :, :], aW1.rearrange("(t p) a -> p t a", p=128)).then_inc(corr_in, 16)
            sp.dma_start(ab1c[:, :], ab1.unsqueeze(1)).then_inc(corr_in, 16)
            sp.dma_start(avc[:, :], av.unsqueeze(1)).then_inc(corr_in, 16)
            sp.dma_start(st_lb1, lb1).then_inc(corr_in, 16)
            sp.wait_ge(lb2_zero, 1)
            for n in range(3):
                sp.dma_start(lb2_stage[n * 32:n * 32 + NL, :], lb2).then_inc(lb2_in, 16)
            sp.wait_ge(zero_ready, 1)
            flat = strips.rearrange("k s r c -> (k s r c)").rearrange("(p n) -> p n", p=128)
            cuts = list(range(0, per, 2048)) + [per]
            for a, b in zip(cuts[:-1], cuts[1:]):
                sp.dma_start(flat[:, a:b], zeros[:, 0:b - a]).then_inc(strips_zero, 16)
            sp.wait_ge(strips_zero, 16 * (len(cuts) - 1))

            def load_strips(a, k):
                ge(sp, gathered[k], 16 * NG * a)
                img = x[bass.ds(a * 2 + k, 1)].squeeze(0)
                src = bass.AP(img.tensor, img.offset, [[SS, NS - 3], [D, T], [1, SW]])
                sp.dma_start(strips[k, 1:NS - 2, PADY:PADY + T, :], src).then_inc(strips_in[k], 16)
                sp.dma_start(strips[k, 0, PADY:PADY + T, SS:SW], img[:, 0:SS]).then_inc(strips_in[k], 16)
                sp.dma_start(strips[k, NS - 2, PADY:PADY + T, 0:SS], img[:, D - SS:D]).then_inc(strips_in[k], 16)

            def load_pix(a, k):
                ge(sp, win_used, a * 2 + (k - 1))
                sp.dma_start(frac_pix[:, k, :], frac_dram[bass.ds(a * 2 + k, 1), :].broadcast_to([128, 2 * Q])).then_inc(pix_in[k], 16)
                sp.dma_start(offs[:, k, :], offs_dram[bass.ds(a * 2 + k, 1), :]).then_inc(pix_in[k], 16)

            def load_x(a, k, q):
                if isinstance(a, int) and a < 2:
                    ge(sp, x1_ready, a * 2 + (k - 1))
                else:
                    sp.wait_ge(x2_ready, a * 2 + (k - 3))
                sp.dma_start(xs[:, q, k, :], x[bass.ds(a * 2 + k, 1)].squeeze(0)).then_inc(x_in[k], 16)

            def publish_experts():
                sp.wait_ge(ev_dve, splits[at_job[("ewib", 3)] + 1])
                sp.dma_start(ia_dram.rearrange("e p n -> p e n"), ia_all.rearrange("p (e n) -> p e n", e=E)).then_inc(experts_out, 16)
                sp.dma_start(oa_dram.rearrange("e p n -> p e n"), oa_all.rearrange("p (e n) -> p e n", e=E)).then_inc(experts_out, 16)
                sp.dma_start(ob_dram.rearrange("e r n -> (e r) n"), ob_all).then_inc(experts_out, 16)
                for e in range(E):
                    sp.dma_start(ib_dram[e].rearrange("s r f -> r s f"),
                                 ib_all[e * R:(e + 1) * R, :].rearrange("p (s f) -> p s f", s=2)).then_inc(experts_out, 16)
                sp.wait_ge(experts_out, 16 * (3 + E))

            def pick_expert(n):
                return bass.ds(sp.value_load(expert_row[0:1, bass.ds(n, 1)], min_val=0, max_val=E - 1), 1)

            def load_expert_in(a):
                ge(sp, up_done, a * FT)
                for k in range(2):
                    pick = pick_expert(a * 2 + k)
                    sp.dma_start(ewiaT[:, k].rearrange("p t s c -> p (t s c)"), ia_dram[pick].squeeze(0)).then_inc(expert_i_in, 16)
                    sp.dma_start(ewibT[:, k, :], ib_dram[pick].squeeze(0).rearrange("s r f -> (s r) f")).then_inc(expert_i_in, 16)

            def load_expert_out(a, k):
                pick = pick_expert(a * 2 + k)
                sp.dma_start(ewoaT[:, k].rearrange("p t c -> p (t c)"), oa_dram[pick].squeeze(0)).then_inc(expert_o_in, 16)
                for c in range(2):
                    sp.dma_start(ewobT[c * R:(c + 1) * R, k].rearrange("p s d -> p (s d)"), ob_dram[pick].squeeze(0)).then_inc(expert_o_in, 16)

            def load_lang(c, k):
                lang = sp.value_load(lang_row[0:1, bass.ds(c * 2 + k, 1)], min_val=0, max_val=NL - 1)
                pick = bass.ds(lang, 1)
                sp.dma_start(lw1[:, k, :, :], lW1[pick].squeeze(0).rearrange("(t p) a -> p t a", p=128)).then_inc(lang_in[k], 16)
                sp.dma_start(lw2[:, k, :], lW2[pick].squeeze(0)).then_inc(lang_in[k], 16)
                sp.dma_start(gamma_b[:, k, :], lgamma[pick, :].broadcast_to([T, D])).then_inc(lang_in[k], 16)
                sp.dma_start(beta_b[:, k, :], lbeta[pick, :].broadcast_to([T, D])).then_inc(lang_in[k], 16)

            def store(c, k):
                sp.wait_ge(y_ready, c * 2 + (k + 1))
                sp.dma_start(out[bass.ds(c * 2 + k, 1)].squeeze(0), y[:, k, :]).then_inc(stored[k], 16)

            for k in range(2):
                load_strips(0, k)
            sp.wait_ge(set_ready, 3)
            sp.dma_start(frac_dram, pix_frac).then_inc(pix_out, 16)
            sp.dma_start(offs_dram, pix_offs).then_inc(pix_out, 16)
            sp.wait_ge(pix_out, 32)
            for k in range(2):
                load_pix(0, k)

            def body(i, q):
                for k in range(2):
                    if there(i, -1):
                        load_x(i + 1, k, 1 - q)
                for k in range(2):
                    if there(i, 0):
                        if isinstance(i, int) and i == NP - 1:
                            sp.wait_ge(x2_ready, i * 2)
                        load_expert_out(i, k)
                for k in range(2):
                    if there(i, 2):
                        store(i - 2, k)
                for k in range(2):
                    if there(i, 1):
                        load_lang(i - 1, k)
                for k in range(2):
                    if there(i, -2):
                        load_strips(i + 2, k)
                        if isinstance(i, int) and i == -1 and k == 1:
                            publish_experts()
                            load_expert_in(0)
                        load_pix(i + 2, k)
                if there(i, -1) and not (isinstance(i, int) and i == -1):
                    load_expert_in(i + 1)

            for i in range(-1, 4):
                if i == 1:
                    sp.wait_ge(pe_set, len(jobs))
                body(i, i % 2)
            with sp.Fori(2, NP // 2 - 1) as i:
                for q in range(2):
                    body(i * 2 + q, q)
            for i in range(NP - 2, NP + 2):
                body(i, i % 2)
            for k in range(2):
                sp.wait_ge(stored[k], 16 * NP)

        @block.gpsimd
        def _(pool):
            g = nc.gpsimd
            g.memset(zeros, 0.0).then_inc(zero_ready, 1)
            g.memset(ident[:, :], 0.0).then_inc(pool_chain, 1)
            g.memset(prompt_mask[:, :, :], 0.0).then_inc(pool_chain, 1)
            g.memset(lb2_stage, 0.0).then_inc(lb2_zero, 1)
            g.iota(part_i[:, 0:1], pattern=[[0, 1]], base=0, channel_multiplier=1).then_inc(consts_ready, 1)
            g.iota(group_i[:, 0, :], pattern=[[32 * GP, 2], [0, 4]], base=-D // 2, channel_multiplier=0).then_inc(consts_ready, 1)
            g.iota(group_i[:, 1, :], pattern=[[0, 2], [GP, 4]], base=-T // 2, channel_multiplier=1).then_inc(consts_ready, 1)
            g.iota(pixel_i[:, 0, :], pattern=[[0, GP], [1, GP]], base=0, channel_multiplier=0).then_inc(consts_ready, 1)
            g.iota(pixel_i[:, 1, :], pattern=[[1, GP], [0, GP]], base=0, channel_multiplier=0).then_inc(consts_ready, 1)
            pool.wait_ge(pool_chain, 2)
            g.affine_select(out=ident[:, :], in_=ident[:, :], compare_op=ALU.not_equal, fill=1.0, base=0,
                            pattern=[[-1, 128]], channel_multiplier=1).then_inc(consts_ready, 1)
            for n, (op, sign) in enumerate(((ALU.is_ge, 1), (ALU.is_ge, -1), (ALU.not_equal, 1))):
                g.affine_select(out=prompt_mask[:, n, :], in_=prompt_mask[:, n, :], compare_op=op, fill=BIG, base=0,
                                pattern=[[-sign, T]], channel_multiplier=sign).then_inc(consts_ready, 1)
            for t in range(FT):
                pool.dma_start(st_ewib[:, t], ewi_b[:, t * 128:(t + 1) * 128, :].rearrange("e p r -> p e r")).then_inc(ewib_in, 16)
            pool.wait_ge(set_ready, 3)
            flat = bass.AP(strips.tensor, 0, [[1, 2 * SLOT], [1, 1]])
            tap = taps.rearrange("p (x t m) -> p x t m", x=2, t=TAPS)

            def weights(a, k, h, links):
                n = a * 2 + k
                m = slice(h * D // 2, (h + 1) * D // 2)
                ge(pool, taps_used, n * 2 + (h - 1))
                for ax in range(2):
                    fg = frac_now[:, ax, :]
                    fp = frac_pix[:, k, ax * Q + h * HALF:ax * Q + (h + 1) * HALF].rearrange("p (j i) -> p j i", i=GP)
                    g.tensor_tensor(tap[:, ax, 1, m].rearrange("p (j g i) -> p j g i", g=NG, i=GP),
                                    fg.unsqueeze(1).unsqueeze(3).broadcast_to([128, GP // 2, NG, GP]),
                                    fp.unsqueeze(2).broadcast_to([128, GP // 2, NG, GP]),
                                    ALU.add).then_inc(pool_chain, 1)
                pool.wait_ge(pool_chain, links + 2)
                before, mid, after = (tap[:, :, t, m] for t in range(TAPS))
                g.tensor_scalar(before, mid, 0.0, -1.0, ALU.min, ALU.mult).then_inc(pool_chain, 1)
                g.tensor_scalar(after, mid, 0.0, None, ALU.max).then_inc(pool_chain, 1)
                pool.wait_ge(pool_chain, links + 4)
                g.tensor_tensor(mid, before, after, ALU.add).then_inc(pool_chain, 1)
                pool.wait_ge(pool_chain, links + 5)
                g.tensor_scalar(mid, mid, -1.0, 1.0, ALU.mult, ALU.add).then_inc(taps_ready, 1)

            def warp(a, k):
                n = a * 2 + k
                pool.sem_clear(pool_chain)
                pool.wait_ge(pix_in[k], a * 32 + 32)
                g.tensor_copy(frac_now[:, :, :], frac_group[:, bass.ds(n, 1), :, :].squeeze(1)).then_inc(pool_chain, 1)
                pool.wait_ge(pool_chain, 1)
                weights(a, k, 0, 1)
                pool.wait_ge(strips_in[k], a * 48 + 48)
                ge(pool, win_used, n)
                ge(pool, gathered[k], a * (16 * NG))
                g.tensor_copy(gather_now[:, k, :], gather_at[:, bass.ds(n, 1), :].squeeze(1)).then_inc(pool_chain, 1)
                pool.wait_ge(pool_chain, 7)
                for gi in range(NG):
                    at = gather_now[:, k, gi:gi + 1]
                    g.indirect_dma_start(out=win[:, gi, :], out_offset=None, in_=flat,
                                         in_offset=bass.IndirectOffsetOnAxis(at, 0)).then_inc(gathered[k], 16)
                weights(a, k, 1, 7)

            def deviations(c):
                count = [0]

                def link(ins):
                    count[0] += 1
                    ins.then_inc(pool_chain, 1)
                    pool.wait_ge(pool_chain, count[0])

                pool.sem_clear(pool_chain)
                pool.wait_ge(guess_ready, c + 1)
                for step in range(3):
                    link(g.tensor_tensor(newton[:, :], rstd[:, :], rstd[:, :], ALU.mult))
                    if step == 0:
                        g.tensor_scalar(neg_mean[:, :], mv[:, :, 0], -1.0, None, ALU.mult).then_inc(scale_ready, 1)
                    link(g.tensor_tensor(newton[:, :], newton[:, :], var_eps[:, :], ALU.mult))
                    link(g.tensor_scalar(newton[:, :], newton[:, :], -0.5, 1.5, ALU.mult, ALU.add))
                    if step < 2:
                        link(g.tensor_tensor(rstd[:, :], rstd[:, :], newton[:, :], ALU.mult))
                g.tensor_tensor(rstd[:, :], rstd[:, :], newton[:, :], ALU.mult).then_inc(scale_ready, 1)

            def outputs(c, q):
                pool.sem_clear(pool_chain)
                for k in range(2):
                    pool.wait_ge(norm_ready, c * 2 + (k + 1))
                    pool.wait_ge(lang_in[k], c * 64 + 64)
                    g.tensor_tensor(y[:, k, :], y[:, k, :], gamma_b[:, k, :], ALU.mult).then_inc(pool_chain, 1)
                for k in range(2):
                    pool.wait_ge(pool_chain, 1 + k)
                    g.tensor_tensor(y[:, k, :], y[:, k, :], beta_b[:, k, :], ALU.add).then_inc(pool_chain, 1)
                for k in range(2):
                    pool.wait_ge(pool_chain, 3 + k)
                    g.tensor_tensor(y[:, k, :], y[:, k, :], x2[:, q, k, :], ALU.add).then_inc(y_ready, 1)

            def body(i, q):
                if there(i, 2):
                    deviations(i - 2)
                    outputs(i - 2, q)
                if there(i, -1):
                    warp(i + 1, 1)
                if there(i, -2):
                    warp(i + 2, 0)

            warp(0, 0)
            for i in range(-1, 4):
                body(i, i % 2)
            with pool.Fori(2, NP // 2 - 1) as i:
                for q in range(2):
                    body(i * 2 + q, q)
            for i in range(NP - 2, NP + 2):
                body(i, i % 2)

        @block.vector
        def _(dve):
            v = nc.vector
            chain = [0]

            def link(ins):
                chain[0] += 1
                ins.then_inc(set_chain, 1)
                dve.wait_ge(set_chain, chain[0])

            low_jobs = [(n, *job) for n, job in enumerate(jobs) if job[0] not in plain]

            def evacuate_low(count):
                for n, kind, t in low_jobs[:count]:
                    (high, low), src, factor = job_ends(kind, t)
                    dve.wait_ge(ev_act, n + 1)
                    if kind == "ewia":
                        pieces = [(low[c][:, m], src[:, m], high[c][:, m]) for c in range(2) for m in range(KT)]
                    elif kind == "ewoa":
                        pieces = [(low[:, m], src[:, m], high[:, m]) for m in range(4)]
                    else:
                        pieces = [(low, src, high)]
                    for low, src, high in pieces:
                        last = v.scalar_tensor_tensor(low, src, factor, high, ALU.mult, ALU.subtract)
                    last.then_inc(ev_dve, 1)
                del low_jobs[:count]

            v.memset(ang[:, B:B + 1], 0.0).then_inc(set_ready, 1)
            dve.wait_ge(in_loaded, 16 * 7)
            dve.wait_ge(consts_ready, 9)
            PI = 3.1415925
            two_pi_hi, two_pi_lo = 6.28125, 2 * np.pi - 6.28125
            turns, r = trig[:, 1, :], trig[:, 0, :]
            turns_i = gather_at[:, :, :].rearrange("p b g -> p (b g)")[:, 0:NA]
            step = sincos[:, 0, :]
            link(v.tensor_scalar(turns_i, ang[:, :], float(1 / (2 * np.pi)), None, ALU.mult))
            link(v.tensor_copy(turns, turns_i))
            link(v.scalar_tensor_tensor(r, turns, -two_pi_hi, ang[:, :], ALU.mult, ALU.add))
            link(v.scalar_tensor_tensor(r, turns, -two_pi_lo, r, ALU.mult, ALU.add))
            link(v.tensor_scalar(step, r, PI, float(-2 * np.pi), ALU.is_gt, ALU.mult))
            link(v.tensor_tensor(r, r, step, ALU.add))
            link(v.tensor_scalar(step, r, -PI, float(2 * np.pi), ALU.is_lt, ALU.mult))
            link(v.tensor_tensor(r, r, step, ALU.add))
            link(v.tensor_scalar(trig[:, 1, :], r, float(np.pi / 2), None, ALU.add))
            link(v.tensor_scalar(step, trig[:, 1, :], PI, float(-2 * np.pi), ALU.is_gt, ALU.mult))
            link(v.tensor_tensor(trig[:, 1, :], trig[:, 1, :], step, ALU.add))
            v.tensor_scalar(trig[:, :, :], trig[:, :, :], PI, -PI, ALU.min, ALU.max).then_inc(set_ready, 1)
            link(v.tensor_scalar(part_i[:, 1:2], part_i[:, 0:1], 31, None, ALU.bitwise_and))
            link(v.tensor_copy(part[:, 0:2], part_i[:, :]))
            link(v.tensor_scalar(part[:, 2:3], part[:, 0:1], float(2 - T), None, ALU.add))
            link(v.tensor_scalar(part[:, 3:4], part[:, 0:1], -1.0, 1.0, ALU.mult, ALU.add))
            link(v.tensor_copy(group[:, :, :], group_i[:, :, :]))
            first_column = stats[:, 0, 0:1]
            link(v.tensor_scalar(first_column, part[:, 1:2], float(GP), None, ALU.mult))
            link(v.tensor_scalar(group[:, 0, :], group[:, 0, :], first_column, None, ALU.add))
            link(v.tensor_scalar(group[:, 1, :], group[:, 1, :], part[:, 1:2], None, ALU.subtract))
            link(v.tensor_copy(ids[:, :, :], ids_i[:, :, :]))
            link(v.tensor_scalar(is_prefix[:, :], ids[:, 0, :], 0.0, None, ALU.is_equal))
            link(v.tensor_scalar(is_postfix[:, :], ids[:, 0, :], 1.0, None, ALU.is_equal))
            link(v.tensor_scalar(lang_hot[:, :], ids[:, 1, :], part[:, 1:2], None, ALU.is_equal))
            link(v.tensor_scalar(inv_count[:, :], is_prefix[:, :], part[:, 2:3], float(T - 1), ALU.mult, ALU.add))
            link(v.scalar_tensor_tensor(inv_count[:, :], is_postfix[:, :], part[:, 3:4], inv_count[:, :], ALU.mult, ALU.add))
            link(v.reciprocal(inv_count[:, :], inv_count[:, :]))
            for n in range(2):
                link(v.tensor_tensor(prompt_mask[:, n, :], prompt_mask[:, n, :], prompt_mask[:, 2, :], ALU.subtract))
            dve.wait_ge(sin_ready, 1)
            sin, cos = sincos[:, 0, :], sincos[:, 1, :]
            low = trig
            link(v.tensor_scalar(low[:, 0, :], sin, 0.0, None, ALU.max))
            link(v.tensor_scalar(low[:, 1, :], cos, 0.0, None, ALU.min))
            link(v.tensor_tensor(low[:, 0, :], low[:, 1, :], low[:, 0, :], ALU.subtract))
            link(v.tensor_scalar(ang[:, :], sin, 0.0, None, ALU.min))
            link(v.tensor_tensor(low[:, 1, :], low[:, 1, :], ang[:, :], ALU.add))
            link(v.tensor_scalar(low[:, :, :], low[:, :, :], float(GP - 1), None, ALU.mult))

            def floor(value, whole_i, whole, over):
                evacuate_low(1)
                link(v.tensor_copy(whole_i, value))
                link(v.tensor_copy(whole, whole_i))
                link(v.tensor_tensor(over, whole, value, ALU.is_gt))
                link(v.tensor_tensor(whole, whole, over, ALU.subtract))

            xs_flat = xs[:, 1, :, :].rearrange("p k d -> p (k d)")
            x1T_flat = x1T[:, :, :, :].rearrange("p s k t -> p (s k t)").bitcast(fp32)
            M = B * NG
            shape = lambda t: t.rearrange("p (b g) -> p b g", g=NG)
            pos, other = xs_flat[:, 0:M], xs_flat[:, M:2 * M]
            whole, whole_i = x1T_flat[:, 0:M], x1T_flat[:, M:2 * M].bitcast(i32)
            at_f = y[:, 1, 0:M]
            for ax in range(2):
                on_x, on_y = (cos, sin) if ax == 0 else (sin, cos)
                wide = lambda t: t.unsqueeze(2).broadcast_to([128, B, NG])
                grp = lambda t: t.unsqueeze(1).broadcast_to([128, B, NG])
                link(v.tensor_tensor(shape(pos), wide(on_x[:, 0:B]), grp(group[:, 0, :]), ALU.mult))
                link(v.tensor_tensor(shape(other), wide(on_y[:, 0:B]), grp(group[:, 1, :]), ALU.mult))
                link(v.tensor_tensor(pos, pos, other, ALU.subtract if ax == 0 else ALU.add))
                link(v.tensor_tensor(ang[:, 0:B], shift[:, :, ax], low[:, ax, 0:B], ALU.add))
                link(v.tensor_tensor(shape(pos), shape(pos), wide(ang[:, 0:B]), ALU.add))
                rate, mid, lo, hi = (RY, (T - 1) / 2, YLO, YHI) if ax == 0 else (RX, (D - 1) / 2, XLO, XHI)
                link(v.tensor_scalar(pos, pos, rate, mid, ALU.mult, ALU.add))
                link(v.tensor_scalar(pos, pos, hi, lo, ALU.min, ALU.max))
                floor(pos, whole_i, whole, other)
                link(v.scalar_tensor_tensor(frac_group[:, :, ax, :], shape(pos), -1.0, shape(whole), ALU.add, ALU.subtract))
                if ax == 0:
                    link(v.tensor_scalar(at_f, whole, float(PADY), float(SW), ALU.add, ALU.mult))
                else:
                    strip_i, in_strip_i = pos.bitcast(i32), other.bitcast(i32)
                    link(v.tensor_scalar(whole_i, whole, float(SS), None, ALU.add))
                    link(v.tensor_scalar(strip_i, whole_i, 6, None, ALU.arith_shift_right))
                    link(v.tensor_scalar(in_strip_i, whole_i, SS - 1, None, ALU.bitwise_and))
                    link(v.tensor_copy(whole, strip_i))
                    link(v.scalar_tensor_tensor(at_f, whole, float(ROWS * SW), at_f, ALU.mult, ALU.add))
                    link(v.tensor_copy(whole, in_strip_i))
                    link(v.tensor_tensor(at_f, at_f, whole, ALU.add))
            odd = at_f.rearrange("p (a k g) -> p a k g", k=2, g=NG)[:, :, 1, :]
            link(v.tensor_scalar(odd, odd, float(SLOT), None, ALU.add))
            link(v.tensor_copy(gather_at[:, :, :].rearrange("p b g -> p (b g)"), at_f))

            pix = pixel_f
            own_sin, own_cos = sincos[0:B, 0, B:NA], sincos[0:B, 1, B:NA]
            row, column = pix[:, 0:Q], pix[:, Q:2 * Q]
            a1, a2, a3, a4 = (pix[:, (2 + n) * Q:(3 + n) * Q] for n in range(4))
            link(v.tensor_copy(pix[:, 0:2 * Q], pixel_i[0:B, :, :].rearrange("p a q -> p (a q)")))
            for ax in range(2):
                on_x, on_y = (own_cos, own_sin) if ax == 0 else (own_sin, own_cos)
                link(v.tensor_scalar(a1, column, on_x, None, ALU.mult))
                link(v.tensor_scalar(a2, row, on_y, None, ALU.mult))
                link(v.tensor_tensor(a1, a1, a2, ALU.subtract if ax == 0 else ALU.add))
                link(v.tensor_scalar(a1, a1, low[0:B, ax, B:NA], RY if ax == 0 else RX, ALU.subtract, ALU.mult))
                link(v.tensor_scalar(a1, a1, 0.0, None, ALU.max))
                floor(a1, pix_offs, a2, a3)
                link(v.tensor_tensor(pix_frac[:, ax * Q:(ax + 1) * Q], a1, a2, ALU.subtract))
                if ax == 0:
                    link(v.tensor_scalar(a4, a2, float(SW), None, ALU.mult))
                else:
                    link(v.tensor_tensor(a4, a4, a2, ALU.add))
            v.tensor_copy(pix_offs, a4).then_inc(set_ready, 1)
            dve.wait_ge(corr_in, 16 * CORR)
            link(v.tensor_scalar(vneg[:, :], ident[:, :], 0.0, avc[:, 0:1], ALU.mult, ALU.subtract))

            dve.wait_ge(lb2_in, 48)
            for n in range(2):
                link(v.tensor_copy(lb2_parts[:, :], lb2_stage))
                for m in range(n + 1, 3):
                    rows = slice(32 * m, 32 * m + 32)
                    link(v.tensor_tensor(lb2_stage[rows, :], lb2_stage[rows, :], lb2_parts[rows, :], ALU.subtract))
            v.tensor_copy(lb2_parts[:, :], lb2_stage).then_inc(set_ready, 1)

            evacuate_low(11)
            regs = [ctx.enter_context(v.register(f"window_offset{n}")) for n in range(LOADED)]
            tap = taps.rearrange("p (x t j g i) -> p x t j g i", x=2, t=TAPS, g=NG, i=GP)
            tap_rows = taps.rearrange("p (x t m) -> p x t m", x=2, t=TAPS)
            prods = prod.rearrange("p (a b j g i) -> p a b j g i", a=TAPS, b=TAPS, g=NG, i=GP)
            by_column_tap = prod.rearrange("p (a b m) -> p a b m", a=TAPS, b=TAPS)

            def body(i, q):
                c, w = i - 1, i + 1
                ffn, tail, warp = there(i, 0), there(i, 1), there(i, -1)
                count = [0]

                def link(ins):
                    count[0] += 1
                    ins.then_inc(dve_chain, 1)
                    dve.wait_ge(dve_chain, count[0])

                def products(k, h, start, end, w=w):
                    n = w * 2 + k
                    if h == 0 and start == 0:
                        dve.wait_ge(pix_in[k], w * 32 + 32)
                        dve.wait_ge(gathered[k], w * (16 * NG) + 16 * NG)
                        link(v.tensor_copy(offs_now[:, :], offs[:, k, :]))
                    for m in range(start, end):
                        j, row = m // GP, m % GP
                        if m % LOADED == 0:
                            v.load(regs, offs_now[0:1, h * HALF + m:h * HALF + m + LOADED])
                        if m == 0:
                            dve.wait_ge(taps_ready, n * 2 + (h + 1))
                        at = v.snap(regs[m % LOADED], min_val=0, max_val=OFF_MAX)
                        first = win[:, :, bass.ds(at, 1)]
                        seen = bass.AP(first.tensor, first.offset, [first.ap[0], [RUN, NG], [SW, TAPS], [1, TAPS]])
                        wx = tap[:, 1, :, h * (GP // 2) + j, :, row].rearrange("p t g -> p g t")
                        last = v.tensor_tensor(prods[:, :, :, j, :, row].rearrange("p a b g -> p g b a"), seen,
                                               wx.unsqueeze(2).broadcast_to([128, NG, TAPS, TAPS]), ALU.mult)
                    if end == HALF and h == 1:
                        last.then_inc(win_used, 1)
                        dve.wait_ge(win_used, n + 1)
                    elif end == HALF:
                        link(last)

                def sums(k, h):
                    half = slice(h * D // 2, (h + 1) * D // 2)
                    total = by_column_tap[:, 0]
                    link(v.tensor_tensor(total, total, by_column_tap[:, 1], ALU.add))
                    link(v.tensor_tensor(total, total, by_column_tap[:, 2], ALU.add))
                    v.tensor_tensor(total, total, tap_rows[:, 0, :, half], ALU.mult).then_inc(taps_used, 1)
                    dve.wait_ge(taps_used, w * 4 + (k * 2 + h + 1))
                    link(v.tensor_tensor(warp_sum[:, half], total[:, 0], total[:, 1], ALU.add))
                    link(v.tensor_tensor(warp_sum[:, half], warp_sum[:, half], total[:, 2], ALU.add))

                def add_warp(k):
                    link(v.transpose(warped[:, :].rearrange("p (w c j) -> p j w c", w=2, j=GP),
                                     warp_sum[:, :].rearrange("p (j w c) -> p j w c", w=2, j=GP)))
                    dve.wait_ge(x_in[k], w * 16 + 16)
                    x1 = xs[:, 1 - q, k, :]
                    v.tensor_tensor(x1, x1, warped[:, :], ALU.add).then_inc(x1_ready, 1)
                    dve.wait_ge(x1_ready, w * 2 + (k + 1))

                def residual(k):
                    dve.wait_ge(ffn_done, c * 2 + (k + 1))
                    ge(dve, y_ready, c * 2 + (k - 3))
                    v.scalar_tensor_tensor(x2[:, 1 - q, k, :], down_ps[k][:, :], PS_DOWN, xs[:, 1 - q, k, :],
                                           ALU.mult, ALU.add).then_inc(x2_ready, 1)

                def low_part(out, ps, high_ready, ready):
                    dve.wait_ge(high_ready, i + 1)
                    v.scalar_tensor_tensor(out[:, 1, :], ps[0:2 * R, 0:2 * T], ALPHA / W_UP, out[:, 0, :],
                                           ALU.mult, ALU.subtract).then_inc(ready, 1)

                def hidden_low(g):
                    if not ffn:
                        evacuate_low(4 if g < 7 else len(jobs))
                    else:
                        f = 2 * g
                        dve.wait_ge(hidden_hi, i * FT + (f + 2))
                        v.tensor_tensor(hidden_parts[:, 1, f % RING:f % RING + 2, :], hidden[:, f % 4:f % 4 + 2, :],
                                        hidden_parts[:, 0, f % RING:f % RING + 2, :], ALU.subtract).then_inc(hidden_ready, 1)

                def x1T_low(k):
                    dve.wait_ge(x1T_hi, w * 2 + (k + 1))
                    cols = slice(k * T, (k + 1) * T)
                    v.scalar_tensor_tensor(x1T[:, 1, :, cols], up_ps[k][:, :].rearrange("p (t c) -> p t c", t=KT), ACT_UP,
                                           x1T[:, 0, :, cols], ALU.mult, ALU.subtract).then_inc(x1T_ready, 1)

                def begin_masks():
                    ge(dve, probs_ready, c * 2)
                    for k in range(2):
                        last = v.scalar_tensor_tensor(masked[:, k, :], prompt_mask[:, 1, :], col(is_postfix, c * 2 + k),
                                                      prompt_mask[:, 2, :], ALU.mult, ALU.add)
                    link(last)

                def mask_scores(k):
                    n = c * 2 + k
                    now = masked[:, k, :]
                    dve.wait_ge(score_ps, n + 1)
                    link(v.scalar_tensor_tensor(now, prompt_mask[:, 0, :], col(is_prefix, n), now, ALU.mult, ALU.add))
                    v.tensor_tensor_reduce(out=now, in0=mid_ps[:, 0:T], in1=now, scale=1.0, scalar=3e38,
                                           op0=ALU.add, op1=ALU.min, accum_out=neg_max[:, k:k + 1]).then_inc(masked_ready, 1)

                def add_pooled(k):
                    n = c * 2 + k
                    ps, x3 = pool_scale[:, k:k + 1], x2[:, 1 - q, k, :]
                    if k == 0:
                        dve.wait_ge(probs_ready, n + 2)
                        link(v.reciprocal(pool_scale[:, :], row_sum[:, :]))
                        link(v.tensor_tensor(pool_scale[:, :], pool_scale[:, :], inv_count[:, bass.ds(n, 2)], ALU.mult))
                    dve.wait_ge(pooled_ps, n + 1)
                    v.scalar_tensor_tensor(x3, wide_ps[:, :], ps, x3, ALU.mult, ALU.add).then_inc(x3_ready, 1)

                def adapted(k):
                    n = c * 2 + k
                    yk = y[:, k, :]
                    dve.wait_ge(adapt_ps, n + 1)
                    ge(dve, stored[k], c * 16)
                    v.tensor_tensor(yk, wide_ps[:, :], x2[:, 1 - q, k, :], ALU.add).then_inc(adapt_read, 1)
                    dve.wait_ge(adapt_read, n + 1)
                    link(v.bn_stats(stats[:, k, :], yk))
                    link(v.bn_aggr(mv[:, k, :], stats[:, k, :]))

                def guess_deviations():
                    link(v.tensor_scalar(var_eps[:, :], mv[:, :, 1], EPS, None, ALU.add))
                    link(v.tensor_scalar(guess_i[:, :], var_eps[:, :].bitcast(i32), 1, None, ALU.arith_shift_right))
                    v.tensor_scalar(rstd[:, :].bitcast(i32), guess_i[:, :], -1.0, float(0x5F3759DF), ALU.mult, ALU.add).then_inc(guess_ready, 1)

                def products_ahead(start, end):
                    if there(i, -2):
                        products(0, 0, start, end, w + 1)

                dve.sem_clear(dve_chain)
                if isinstance(i, int) and i == -1:
                    products(0, 0, 0, 16)
                if tail:
                    for k in range(2):
                        residual(k)
                if warp:
                    products(0, 0, 16, 22)
                if ffn:
                    low_part(low_i, low_ps, low_i_hi, low_i_ready)
                if tail:
                    begin_masks()

                def products_between(k, h, g):
                    if warp:
                        products(k, h, 0, HALF // 2)
                    hidden_low(g)
                    if warp:
                        products(k, h, HALF // 2, HALF)

                if warp:
                    products(0, 0, 22, HALF)
                hidden_low(0)
                if warp:
                    sums(0, 0)
                hidden_low(1)
                if tail:
                    mask_scores(0)
                if warp:
                    products(0, 1, 0, HALF // 2)
                if tail:
                    mask_scores(1)
                hidden_low(2)
                if warp:
                    products(0, 1, HALF // 2, HALF)
                    sums(0, 1)
                    add_warp(0)
                hidden_low(3)
                if tail:
                    add_pooled(0)
                    add_pooled(1)
                products_between(1, 0, 4)
                if warp:
                    sums(1, 0)
                hidden_low(5)
                products_between(1, 1, 6)
                if tail:
                    adapted(0)
                if warp:
                    sums(1, 1)
                    add_warp(1)
                hidden_low(7)
                if tail:
                    adapted(1)
                if warp:
                    for k in range(2):
                        x1T_low(k)
                if tail:
                    guess_deviations()
                products_ahead(0, 8)
                if ffn:
                    low_part(low_o, low_ps, low_o_hi, low_o_ready)
                products_ahead(8, 16)

            for i in range(-1, 4):
                body(i, i % 2)
            with dve.Fori(2, NP // 2 - 1) as i:
                for q in range(2):
                    body(i * 2 + q, q)
            for i in range(NP - 2, NP + 1):
                body(i, i % 2)

        @block.scalar
        def _(act):
            s = nc.scalar
            act.wait_ge(set_ready, 2)
            s.activation(sincos[:, :, :], trig[:, :, :], ACT.Sin).then_inc(sin_ready, 1)
            for n, job in enumerate(jobs):
                dst, src, factor = job_ends(*job)
                act.wait_ge(pe_set, n + 1)
                for high in dst[0] if job[0] == "ewia" else [dst[0]]:
                    last = s.activation(high, src, ACT.Copy, scale=factor)
                last.then_inc(ev_act, 1)
                if job in (("wi", 3), ("wi", 7)):
                    load_wi(act, 2 + job[1] // 4)
                elif job == ("wi", 8):
                    act.wait_ge(strips_zero, 16 * -(-per // 2048))
                    load_wo(act, 0)
                elif job == ("wi", 15):
                    load_wo(act, 1)
                elif job in (("wo", (0, 3)), ("wo", (1, 3))):
                    load_wo(act, 2 + job[1][0])
            act.wait_ge(corr_in, 16 * CORR)

            def body(i, q):
                c, w = i - 1, i + 1
                ffn, tail, warp = there(i, 0), there(i, 1), there(i, -1)

                def copy_T(k, filled):
                    act.wait_ge(filled, c * 2 + (k + 1))
                    s.activation(xT[:, k, :, :].rearrange("p t c -> p (t c)"), tr_ps[:, :], ACT.Copy).then_inc(xT_ready, 1)

                def attend(k):
                    act.wait_ge(att_ps, c * 2 + (k + 1))
                    s.activation(att[:, k, :], mid_ps[:, 0:T], ACT.Tanh, bias=ab1c[:, 0:1]).then_inc(att_ready, 1)

                def exponentials(k):
                    act.wait_ge(masked_ready, c * 2 + (k + 1))
                    s.activation(probs[:, k, :], masked[:, k, :], ACT.Exp, bias=neg_max[:, k:k + 1], scale=-1.0,
                                 accum_out=row_sum[:, k:k + 1]).then_inc(probs_ready, 1)

                def copy_probs(k):
                    act.wait_ge(probsT_ps, c * 2 + (k + 1))
                    s.activation(probsT[:, k, :], mid_ps[:, 0:T], ACT.Copy).then_inc(probsT_ready, 1)

                def adapter_relu(k):
                    act.wait_ge(h_ps, c * 2 + (k + 1))
                    s.activation(hA[:, k, :], mid_ps[:, 0:T], ACT.Relu, bias=lb1_now[:, k:k + 1]).then_inc(h_ready, 1)

                steps = {1: [(copy_T, 0, x2T_ps)], 2: [(copy_T, 1, x2T_ps), (attend, 0)], 3: [(attend, 1)],
                         6: [(exponentials, 0)], 7: [(copy_probs, 0), (exponentials, 1)], 8: [(copy_probs, 1)],
                         10: [(copy_T, 0, x3T_ps)], 11: [(copy_T, 1, x3T_ps)],
                         13: [(adapter_relu, 0)], 14: [(adapter_relu, 1)]}

                act.sem_clear(act_chain)
                ge(act, h_ready, c * 2)
                ge(act, adapt_ps, c * 2)
                if tail:
                    s.activation(lb1_now[:, :], lb1_img[:, bass.ds(c * 2, 2)], ACT.Copy).then_inc(act_chain, 1)
                    s.activation(lang_now[:, :, :], lang_hot[0:96, bass.ds(c * 2, 2)].unsqueeze(2).broadcast_to([96, 2, T]),
                                 ACT.Copy).then_inc(lang_ready, 1)
                    act.wait_ge(act_chain, 1)

                def project(out, filled, ready):
                    act.wait_ge(filled, i + 1)
                    s.activation(out[:, 0, :], low_ps[0:2 * R, 0:2 * T], ACT.Copy, scale=ALPHA / W_UP).then_inc(ready, 1)

                if ffn:
                    project(low_i, low_i_ps, low_i_hi)
                def centre():
                    act.wait_ge(scale_ready, i * 2 - 3)
                    for k in range(2):
                        s.activation(y[:, k, :], y[:, k, :], ACT.Identity, bias=neg_mean[:, k:k + 1]).then_inc(centred, 1)

                def scale():
                    act.wait_ge(scale_ready, i * 2 - 2)
                    act.wait_ge(centred, i * 2 - 2)
                    for k in range(2):
                        s.activation(y[:, k, :], y[:, k, :], ACT.Copy, scale=rstd[:, k:k + 1]).then_inc(norm_ready, 1)

                for f in range(FT):
                    if f == 0 and there(i, 2):
                        centre()
                    if f == 1 and there(i, 2):
                        scale()
                    if ffn:
                        act.wait_ge(up_done, i * FT + (f + 1))
                        ge(act, hidden_ready, i * (FT // 2) + (f // 2 - 1))
                        s.activation(hidden[:, f % 4, :], up_ps[f % 2][:, 0:2 * T], ACT.Relu, scale=1.0 / W_UP)
                        ge(act, down_done, i * FT + (f - RING + 1))
                        s.activation(hidden_parts[:, 0, f % RING, :], up_ps[f % 2][:, 0:2 * T], ACT.Relu,
                                     scale=1.0 / W_UP).then_inc(hidden_hi, 1)
                    if tail:
                        for step in steps.get(f, []):
                            step[0](*step[1:])
                if warp:
                    for k in range(2):
                        act.wait_ge(x1T_ps, w * 2 + (k + 1))
                        s.activation(x1T[:, 0, :, k * T:(k + 1) * T], up_ps[k][:, :].rearrange("p (t c) -> p t c", t=KT),
                                     ACT.Copy, scale=ACT_UP).then_inc(x1T_hi, 1)
                if ffn:
                    project(low_o, low_o_ps, low_o_hi)

            for i in range(-1, 4):
                body(i, i % 2)
            with act.Fori(2, NP // 2 - 1) as i:
                for q in range(2):
                    body(i * 2 + q, q)
            for i in range(NP - 2, NP + 2):
                body(i, i % 2)

        @block.tensor
        def _(pe):
            t = nc.tensor

            def transposes(dst, src, width=128):
                for n in range(4):
                    last = t.transpose(dst[:, n * 128:(n + 1) * 128], src(n), ident[:, :])
                return last

            def tile(n):
                return slice(n * 128, (n + 1) * 128)

            def images(k):
                return slice(k * T, (k + 1) * T)

            pe.wait_ge(consts_ready, 9)
            pe.wait_ge(common_in, 16 * 7)
            for n, (kind, j) in enumerate(jobs):
                b = banks[n % 8]
                if n >= 8:
                    if jobs[n - 8][0] in plain:
                        pe.wait_ge(ev_act, n - 7)
                    else:
                        pe.wait_ge(ev_dve, splits[n - 7])
                if kind in ("cwib", "cwob"):
                    st = st_cwib if kind == "cwib" else st_cwob
                    last = transposes(b[0:R, :], lambda m: st[:, 4 * j + m, :])
                elif kind == "wi":
                    if j % 4 == 0:
                        pe.wait_ge(wi_in[j // 4 % 2], 16 * (j // 8 + 1))
                    if j == 0:
                        pe.wait_ge(ev_act, 5)
                    for m in range(KT):
                        at = (j % 4) * D + m * 128
                        t.matmul(b[:, tile(m)], st_wi[j // 4 % 2][:, at:at + 128], ident[:, :], start=True, stop=False)
                        last = t.matmul(b[:, tile(m)], st_cwia[:, tile(m)], cwibT[j // 4][:, tile(j % 4)], start=False, stop=True)
                elif kind == "ewia":
                    pe.wait_ge(corr_in, 16 * CORR)
                    last = transposes(b, lambda m: st_ewia[:, tile(m)])
                elif kind == "lb1":
                    pe.wait_ge(set_ready, 3)
                    last = t.matmul(b[:, 0:B], st_lb1, lang_hot[0:NL, :], start=True, stop=True)
                elif kind == "ewoa":
                    last = transposes(b, lambda m: st_ewoa[:, tile(4 * j + m)])
                elif kind == "ewob":
                    last = transposes(b, lambda m: st_ewob[:, m].rearrange("p e r -> p (e r)"))
                elif kind == "ewib":
                    if j == 0:
                        pe.wait_ge(ewib_in, 16 * FT)
                    last = transposes(b, lambda m: st_ewib[:, 4 * j + m].rearrange("p e r -> p (e r)"))
                else:
                    dt, j = j
                    if j == 0:
                        pe.wait_ge(wo_in[dt % 2], 16 * (dt // 2 + 1))
                    for m in range(4):
                        at = (4 * j + m) * 128
                        t.matmul(b[:, tile(m)], st_wo[dt % 2][:, at:at + 128], ident[:, :], start=True, stop=False)
                        last = t.matmul(b[:, tile(m)], st_cwoa[j][:, tile(m)], cwobT[:, tile(dt)], start=False, stop=True)
                last.then_inc(pe_set, 1)
            pe.wait_ge(ev_dve, splits[-1])
            pe.wait_ge(set_ready, 4)

            def body(i, q):
                c, w = i - 1, i + 1
                ffn, tail, warp = there(i, 0), there(i, 1), there(i, -1)

                def x2_T(k):
                    n = c * 2 + k
                    pe.wait_ge(x2_ready, n + 1)
                    ge(pe, xT_ready, c * 4 + k)
                    transposes(tr_ps, lambda m: x2[:, 1 - q, k, tile(m)]).then_inc(x2T_ps, 1)

                def att_in(k):
                    n = c * 2 + k
                    pe.wait_ge(xT_ready, c * 4 + (k + 1))
                    if k == 0:
                        ge(pe, h_ready, n)
                    else:
                        pe.wait_ge(att_ready, n)
                    for m in range(KT):
                        last = t.matmul(mid_ps[:, 0:T], aw1[:, m, :], xT[:, k, m, :], start=(m == 0), stop=(m == KT - 1))
                    last.then_inc(att_ps, 1)

                def scores(k):
                    n = c * 2 + k
                    pe.wait_ge(att_ready, n + 1 if k else n + 2)
                    if k:
                        pe.wait_ge(masked_ready, n)
                    t.matmul(mid_ps[:, 0:T], vneg[:, :], att[:, k, :], start=True, stop=True).then_inc(score_ps, 1)

                def probs_T(k):
                    n = c * 2 + k
                    pe.wait_ge(probs_ready, n + 1)
                    if k:
                        pe.wait_ge(probsT_ready, n)
                    else:
                        pe.wait_ge(masked_ready, n + 2)
                    t.transpose(mid_ps[:, 0:T], probs[:, k, :], ident[:, :]).then_inc(probsT_ps, 1)

                def pooled(k):
                    n = c * 2 + k
                    pe.wait_ge(probsT_ready, n + 1)
                    if k:
                        pe.wait_ge(x3_ready, n)
                    else:
                        ge(pe, adapt_read, n)
                    t.matmul(wide_ps[:, :], probsT[:, k, :], x2[:, 1 - q, k, :], start=True, stop=True).then_inc(pooled_ps, 1)

                def x3_T(k):
                    n = c * 2 + k
                    pe.wait_ge(x3_ready, n + 1)
                    pe.wait_ge(xT_ready, c * 4 + (k + 2))
                    transposes(tr_ps, lambda m: x2[:, 1 - q, k, tile(m)]).then_inc(x3T_ps, 1)

                def adapter_in(k):
                    n = c * 2 + k
                    pe.wait_ge(xT_ready, c * 4 + (k + 3))
                    pe.wait_ge(lang_in[k], c * 64 + 64)
                    if k:
                        pe.wait_ge(h_ready, n)
                    else:
                        pe.wait_ge(probsT_ready, n + 2)
                    for m in range(KT):
                        last = t.matmul(mid_ps[:, 0:T], lw1[:, k, m, :], xT[:, k, m, :], start=(m == 0), stop=(m == KT - 1))
                    last.then_inc(h_ps, 1)

                def adapter_out(k):
                    n = c * 2 + k
                    pe.wait_ge(h_ready, n + 1)
                    if k:
                        pe.wait_ge(adapt_read, n)
                    else:
                        pe.wait_ge(x3_ready, n + 2)
                    t.matmul(wide_ps[:, :], hA[:, k, :], lw2[:, k, :], start=True, stop=False)
                    pe.wait_ge(lang_ready, c + 1)
                    t.matmul(wide_ps[:, :], lang_now[:, k, :], lb2_parts[:, :], start=False, stop=True).then_inc(adapt_ps, 1)

                steps = {1: [(x2_T, 0)], 2: [(x2_T, 1), (att_in, 0)], 3: [(att_in, 1)], 4: [(scores, 0)], 5: [(scores, 1)],
                         7: [(probs_T, 0)], 8: [(probs_T, 1), (pooled, 0)], 9: [(pooled, 1)], 10: [(x3_T, 0)],
                         11: [(x3_T, 1)], 13: [(adapter_in, 0)], 14: [(adapter_in, 1), (adapter_out, 0)]}

                def up(f):
                    b = up_ps[f % 2]
                    if f >= 2:
                        pe.wait_ge(hidden_hi, i * FT + (f - 1))
                    for m in range(KT):
                        for ws, xs_ in PARTS:
                            t.matmul(b[:, 0:2 * T], wiT[:, ws, m, tile(f)], x1T[:, xs_, m, :],
                                     start=(m == 0 and ws + xs_ == 0), stop=False)
                    if f == 0:
                        pe.wait_ge(low_i_ready, i + 1)
                    for k in range(2):
                        for xs_ in range(2):
                            last = t.matmul(b[:, k * T:(k + 1) * T], ewibT[:, k, tile(f)], low_i[:, xs_, images(k)],
                                            start=False, stop=(k == 1 and xs_ == 1))
                    last.then_inc(up_done, 1)

                def down(f):
                    pe.wait_ge(hidden_ready, i * (FT // 2) + (f // 2 + 1))
                    if f == 0:
                        ge(pe, x2_ready, i * 2)
                        pe.wait_ge(expert_o_in, i * 96 + 96)
                    first, end = (f == 0), (f == FT - 1)
                    for k in range(2):
                        for hs in range(2):
                            low = t.matmul(low_ps[0:2 * R, images(k)], ewoaT[:, k, f, :], hidden_parts[:, hs, f % RING, k * T:(k + 1) * T],
                                           start=(first and k + hs == 0), stop=(end and k + hs == 2))
                    if end:
                        low.then_inc(low_o_ps, 1)
                    for k in range(2):
                        for n, (hs, ws) in enumerate(PARTS):
                            last = t.matmul(down_ps[k][:, :], hidden_parts[:, hs, f % RING, k * T:(k + 1) * T], woT[:, ws, f, :],
                                            start=(first and n == 0), stop=False)
                    last.then_inc(down_done, 1)

                if ffn:
                    pe.wait_ge(x1T_ready, i * 2 + 2)
                    pe.wait_ge(expert_i_in, i * 64 + 64)
                    ge(pe, low_o_ready, i)
                    for k in range(2):
                        for m in range(KT):
                            for n, (ws, xs_) in enumerate(PARTS):
                                last = t.matmul(low_ps[0:2 * R, images(k)], ewiaT[:, k, m, ws, :], x1T[:, xs_, m, k * T:(k + 1) * T],
                                                start=(k + m + n == 0), stop=(k == 1 and m == KT - 1 and n == 2))
                    last.then_inc(low_i_ps, 1)
                for f in range(FT):
                    if ffn:
                        up(f)
                        if f >= LAG:
                            down(f - LAG)
                    if tail:
                        for step in steps.get(f, []):
                            step[0](*step[1:])
                if ffn:
                    for f in range(FT - LAG, FT - LAG + 2):
                        down(f)
                for k in range(2):
                    if warp:
                        ge(pe, hidden_hi, w * FT)
                        pe.wait_ge(x1_ready, w * 2 + (k + 1))
                        transposes(up_ps[k], lambda m: xs[:, 1 - q, k, tile(m)]).then_inc(x1T_ps, 1)
                    if tail and k == 0:
                        adapter_out(1)
                if ffn:
                    for f in range(FT - LAG + 2, FT):
                        down(f)
                    pe.wait_ge(low_o_ready, i + 1)
                    for k in range(2):
                        for n, (hs, ws) in enumerate(PARTS):
                            last = t.matmul(down_ps[k][:, :], low_o[:, hs, images(k)], ewobT[:, k, ws, :],
                                            start=False, stop=(n == 2))
                        last.then_inc(ffn_done, 1)

            for i in range(-1, 4):
                body(i, i % 2)
            with pe.Fori(2, NP // 2 - 1) as i:
                for q in range(2):
                    body(i * 2 + q, q)
            for i in range(NP - 2, NP + 1):
                body(i, i % 2)


_INS = ['x', 'fside_Bx2_0', 'condB_angle', 'itok_B_0_7', 'itok_B_0_2', 'itok_B_0_8', 'L1_cond_wi', 'L1_cond_wo',
        'L1_cond_common_wi_a', 'L1_cond_common_wi_b', 'L1_cond_common_wo_a', 'L1_cond_common_wo_b',
        'L1_cond_experts_wi_a', 'L1_cond_experts_wi_b', 'L1_cond_experts_wo_a', 'L1_cond_experts_wo_b',
        'L2_cond_W1', 'L2_cond_b1', 'L2_cond_v', 'L3_cond_W1', 'L3_cond_b1', 'L3_cond_W2', 'L3_cond_b2',
        'L3_cond_gamma', 'L3_cond_beta']


def kernel(**inputs):
    import concourse.bacc as _bacc
    from concourse.bass_utils import run_bass_kernel_spmd as _run

    nc = _bacc.Bacc("TRN2", target_bir_lowering=False, num_devices=1)
    arrays, args = {}, []
    for name in _INS:
        a = np.ascontiguousarray(inputs[name])
        arrays[f"in_{name}_dram"] = a
        args.append(nc.dram_tensor(f"in_{name}_dram", a.shape, mybir.dt.from_np(a.dtype), kind="ExternalInput").ap())
    shape = inputs["x"].shape
    out = nc.dram_tensor("out_0_dram", tuple(shape), fp32, kind="ExternalOutput").ap()
    build(nc, *args, out)
    return _run(nc, [arrays], core_ids=[0]).results[0]["out_0_dram"]
```
